# Optimizing a Trainium2 kernel written in Bass

```python
import numpy as np
import jax
import jax.numpy as jnp

def _softmax(x, axis=-1):
    return jax.nn.softmax(x, axis=axis)

def _gelu(x):
    return jax.nn.gelu(x, approximate=True)

def _silu(x):
    return jax.nn.silu(x)

def _sigmoid(x):
    return jax.nn.sigmoid(x)

def _layernorm(x, axis=-1, eps=1e-05):
    m = jnp.mean(x, axis=axis, keepdims=True)
    v = jnp.var(x, axis=axis, keepdims=True)
    return (x - m) / jnp.sqrt(v + eps)

def _scatter_add(tgt, idx, src, axis=0):
    return tgt.at[idx].add(src)

def _segment_sum(src, seg, n):
    return jax.ops.segment_sum(src, seg, n)
kernel_name = 'mk_adaln_d2_jaxref_r8_2b6df9'

def setup_inputs(seed: int=0):
    np.random.seed(seed)
    _w = jnp.asarray

    def _L0_attn_setup():
        import jax, jax.numpy as jnp
        import numpy as np
        HIDDEN = 512
        HEAD_DIM = 128
        N_Q_HEADS = 32
        N_KV_HEADS = 8
        SLIDING_WINDOW = 128
        ROPE_THETA = 10000.0
        BATCH, SEQ = (1, 256)

        def _rope(t, pos):
            d = t.shape[-1]
            half = d // 2
            inv_freq = ROPE_THETA ** (-jnp.arange(half, dtype=jnp.float32) / half)
            ang = pos[:, None].astype(jnp.float32) * inv_freq[None, :]
            cos = jnp.cos(ang)[None, :, None, :]
            sin = jnp.sin(ang)[None, :, None, :]
            t1, t2 = (t[..., :half], t[..., half:])
            return jnp.concatenate([t1 * cos - t2 * sin, t1 * sin + t2 * cos], axis=-1)
        key = jax.random.key(seed)
        ks = jax.random.split(key, 5)
        w_scale = HIDDEN ** (-0.5)
        return {'x': jax.random.normal(ks[0], (BATCH, SEQ, HIDDEN), jnp.float32), 'wq': jax.random.normal(ks[1], (HIDDEN, N_Q_HEADS * HEAD_DIM), jnp.float32) * w_scale, 'wk': jax.random.normal(ks[2], (HIDDEN, N_KV_HEADS * HEAD_DIM), jnp.float32) * w_scale, 'wv': jax.random.normal(ks[3], (HIDDEN, N_KV_HEADS * HEAD_DIM), jnp.float32) * w_scale, 'wo': jax.random.normal(ks[4], (N_Q_HEADS * HEAD_DIM, HIDDEN), jnp.float32) * w_scale}
    _L0_attn_in = _L0_attn_setup()

    def _L0_ffn_setup():
        import jax, jax.numpy as jnp
        import numpy as np
        key = jax.random.key(seed)
        k = jax.random.split(key, 6)
        x = jax.random.normal(k[0], (4, 256, 512), jnp.float32)
        W = jax.random.normal(k[1], (512, 512), jnp.float32) * 0.02
        bias = jax.random.normal(k[2], (512,), jnp.float32) * 0.02
        A = jax.random.normal(k[3], (16, 16, 512), jnp.float32) * 0.02
        Bf = jax.random.normal(k[4], (16, 512, 16), jnp.float32) * 0.02
        coeffs = jax.random.uniform(k[5], (16,), jnp.float32)
        scales = jnp.full((16,), 0.5, jnp.float32)
        return {'x': x, 'W': W, 'bias': bias, 'A': A, 'Bf': Bf, 'coeffs': coeffs, 'scales': scales}
    _L0_ffn_in = _L0_ffn_setup()
    _L0_c = _w((lambda *s: np.random.randn(*s).astype(np.float32) * 0.05)(2, 512))
    _L0_wmod = _w((lambda *s: np.random.randn(*s).astype(np.float32) * 0.05)(512, 6 * 512) * 512 ** (-0.5))

    def _L1_attn_setup():
        import jax, jax.numpy as jnp
        import numpy as np
        D_MODEL, N_HEADS, LATENT, ROPE = (512, 128, 64, 64)
        HEAD_DIM = D_MODEL // N_HEADS
        B, S = (2, 128)
        key = jax.random.key(seed)
        ks = jax.random.split(key, 9)

        def w(k, i, o):
            return jax.random.normal(k, (i, o), dtype=jnp.float32) * (1.0 / np.sqrt(i))
        return {'x': jax.random.normal(ks[0], (B, S, D_MODEL), dtype=jnp.float32), 'Wq_down': w(ks[1], D_MODEL, LATENT), 'Wq_up': w(ks[2], LATENT, N_HEADS * HEAD_DIM), 'Wq_rope': w(ks[3], D_MODEL, N_HEADS * ROPE), 'Wkv_down': w(ks[4], D_MODEL, LATENT), 'Wk_up': w(ks[5], LATENT, N_HEADS * HEAD_DIM), 'Wv_up': w(ks[6], LATENT, N_HEADS * HEAD_DIM), 'Wk_rope': w(ks[7], D_MODEL, ROPE), 'Wo': w(ks[8], N_HEADS * HEAD_DIM, D_MODEL)}
    _L1_attn_in = _L1_attn_setup()

    def _L1_ffn_setup():
        import jax, jax.numpy as jnp
        import numpy as np
        SCALING = 32.0 / 16.0
        key = jax.random.key(seed)
        ks = jax.random.split(key, 7)
        B, T, D, O, R, E = (4, 256, 512, 512, 16, 8)
        x = jax.random.normal(ks[0], (B, T, D), dtype=jnp.float32)
        base_W = jax.random.normal(ks[1], (O, D), dtype=jnp.float32) * D ** (-0.5)
        base_b = jax.random.normal(ks[2], (O,), dtype=jnp.float32) * 0.01
        router_W = jax.random.normal(ks[3], (2 * E - 1, D), dtype=jnp.float32) * D ** (-0.5)
        router_b = jax.random.normal(ks[4], (2 * E - 1,), dtype=jnp.float32) * 0.01
        A = jax.random.normal(ks[5], (E, R, D), dtype=jnp.float32) * D ** (-0.5)
        Bm = jax.random.normal(ks[6], (E, O, R), dtype=jnp.float32) * R ** (-0.5)
        assigned_idx = 0
        others = [i for i in range(E) if i != assigned_idx]
        expert_map = jnp.array([assigned_idx] * E + others, dtype=jnp.int32)
        return {'x': x, 'base_W': base_W, 'base_b': base_b, 'router_W': router_W, 'router_b': router_b, 'A': A, 'B': Bm, 'expert_map': expert_map}
    _L1_ffn_in = _L1_ffn_setup()
    _L1_c = _w((lambda *s: np.random.randn(*s).astype(np.float32) * 0.05)(2, 512))
    _L1_wmod = _w((lambda *s: np.random.randn(*s).astype(np.float32) * 0.05)(512, 6 * 512) * 512 ** (-0.5))
    _d = {'L0_attn_x': _L0_attn_in['x'], 'L0_attn_wq': _L0_attn_in['wq'], 'L0_attn_wk': _L0_attn_in['wk'], 'L0_attn_wv': _L0_attn_in['wv'], 'L0_attn_wo': _L0_attn_in['wo'], 'L0_ffn_W': _L0_ffn_in['W'], 'L0_ffn_bias': _L0_ffn_in['bias'], 'L0_ffn_A': _L0_ffn_in['A'], 'L0_ffn_Bf': _L0_ffn_in['Bf'], 'L0_ffn_coeffs': _L0_ffn_in['coeffs'], 'L0_ffn_scales': _L0_ffn_in['scales'], 'L0_c': _L0_c, 'L0_wmod': _L0_wmod, 'L1_attn_Wq_down': _L1_attn_in['Wq_down'], 'L1_attn_Wq_up': _L1_attn_in['Wq_up'], 'L1_attn_Wq_rope': _L1_attn_in['Wq_rope'], 'L1_attn_Wkv_down': _L1_attn_in['Wkv_down'], 'L1_attn_Wk_up': _L1_attn_in['Wk_up'], 'L1_attn_Wv_up': _L1_attn_in['Wv_up'], 'L1_attn_Wk_rope': _L1_attn_in['Wk_rope'], 'L1_attn_Wo': _L1_attn_in['Wo'], 'L1_ffn_base_W': _L1_ffn_in['base_W'], 'L1_ffn_base_b': _L1_ffn_in['base_b'], 'L1_ffn_router_W': _L1_ffn_in['router_W'], 'L1_ffn_router_b': _L1_ffn_in['router_b'], 'L1_ffn_A': _L1_ffn_in['A'], 'L1_ffn_B': _L1_ffn_in['B'], 'L1_ffn_expert_map': _L1_ffn_in['expert_map'], 'L1_c': _L1_c, 'L1_wmod': _L1_wmod}
    _x0 = _d['L0_attn_x']
    _d['L0_attn_x'] = jax.random.normal(jax.random.fold_in(jax.random.key(seed), 1), (2, 512, 512), dtype=_x0.dtype)
    del _x0
    return _d

def reference(L0_attn_x, L0_attn_wq, L0_attn_wk, L0_attn_wv, L0_attn_wo, L0_ffn_W, L0_ffn_bias, L0_ffn_A, L0_ffn_Bf, L0_ffn_coeffs, L0_ffn_scales, L0_c, L0_wmod, L1_attn_Wq_down, L1_attn_Wq_up, L1_attn_Wq_rope, L1_attn_Wkv_down, L1_attn_Wk_up, L1_attn_Wv_up, L1_attn_Wk_rope, L1_attn_Wo, L1_ffn_base_W, L1_ffn_base_b, L1_ffn_router_W, L1_ffn_router_b, L1_ffn_A, L1_ffn_B, L1_ffn_expert_map, L1_c, L1_wmod):

    def _L0_attn_ref(x, wq, wk, wv, wo):
        import jax, jax.numpy as jnp
        import numpy as np
        HIDDEN = 512
        HEAD_DIM = 128
        N_Q_HEADS = 32
        N_KV_HEADS = 8
        SLIDING_WINDOW = 128
        ROPE_THETA = 10000.0
        BATCH, SEQ = (1, 256)

        def _rope(t, pos):
            d = t.shape[-1]
            half = d // 2
            inv_freq = ROPE_THETA ** (-jnp.arange(half, dtype=jnp.float32) / half)
            ang = pos[:, None].astype(jnp.float32) * inv_freq[None, :]
            cos = jnp.cos(ang)[None, :, None, :]
            sin = jnp.sin(ang)[None, :, None, :]
            t1, t2 = (t[..., :half], t[..., half:])
            return jnp.concatenate([t1 * cos - t2 * sin, t1 * sin + t2 * cos], axis=-1)
        B, S, _ = x.shape
        G = N_Q_HEADS // N_KV_HEADS
        sm_scale = HEAD_DIM ** (-0.5)
        q = (x @ wq).reshape(B, S, N_Q_HEADS, HEAD_DIM)
        k = (x @ wk).reshape(B, S, N_KV_HEADS, HEAD_DIM)
        v = (x @ wv).reshape(B, S, N_KV_HEADS, HEAD_DIM)
        pos = jnp.arange(S)
        q = _rope(q, pos)
        k = _rope(k, pos)
        qg = q.reshape(B, S, N_KV_HEADS, G, HEAD_DIM)
        scores = jnp.einsum('bqhgd,bshd->bhgqs', qg, k) * sm_scale
        i = pos[:, None]
        j = pos[None, :]
        allowed = (j <= i) & (j > i - SLIDING_WINDOW)
        neg = jnp.finfo(scores.dtype).min
        scores = jnp.where(allowed[None, None, None], scores, neg)
        attn = jax.nn.softmax(scores, axis=-1)
        out = jnp.einsum('bhgqs,bshd->bqhgd', attn, v).reshape(B, S, N_Q_HEADS * HEAD_DIM)
        return out @ wo

    def _L0_ffn_ref(x, W, bias, A, Bf, coeffs, scales):
        import jax, jax.numpy as jnp
        import numpy as np
        out = jnp.einsum('bsd,od->bso', x, W) + bias
        xa = jnp.einsum('bsd,erd->ebsr', x, A)
        w = coeffs * scales
        upd = jnp.einsum('ebsr,eor,e->bso', xa, Bf, w)
        return out + upd

    def _L1_attn_ref(x, Wq_down, Wq_up, Wq_rope, Wkv_down, Wk_up, Wv_up, Wk_rope, Wo):
        import jax, jax.numpy as jnp
        import numpy as np
        D_MODEL, N_HEADS, LATENT, ROPE = (512, 128, 64, 64)
        HEAD_DIM = D_MODEL // N_HEADS
        B, S = (2, 128)
        b, s, _ = x.shape
        c_q = x @ Wq_down
        c_kv = x @ Wkv_down
        q_c = (c_q @ Wq_up).reshape(b, s, N_HEADS, HEAD_DIM)
        q_r = (x @ Wq_rope).reshape(b, s, N_HEADS, ROPE)
        k_c = (c_kv @ Wk_up).reshape(b, s, N_HEADS, HEAD_DIM)
        v_c = (c_kv @ Wv_up).reshape(b, s, N_HEADS, HEAD_DIM)
        k_r = x @ Wk_rope
        scale = jnp.asarray((HEAD_DIM + ROPE) ** 0.5, x.dtype)
        scores = (jnp.einsum('bqhd,bkhd->bhqk', q_c, k_c) + jnp.einsum('bqhd,bkd->bhqk', q_r, k_r)) / scale
        attn = jax.nn.softmax(scores, axis=-1)
        out = jnp.einsum('bhqk,bkhd->bqhd', attn, v_c)
        out = out.reshape(b, s, N_HEADS * HEAD_DIM)
        return out @ Wo

    def _L1_ffn_ref(x, base_W, base_b, router_W, router_b, A, B, expert_map):
        import jax, jax.numpy as jnp
        import numpy as np
        SCALING = 32.0 / 16.0
        E = A.shape[0]
        base_out = jnp.einsum('btd,od->bto', x, base_W) + base_b
        logits = jnp.einsum('btd,nd->btn', x, router_W) + router_b
        probs = jax.nn.softmax(logits, axis=-1)
        topk_p, topk_i = jax.lax.top_k(probs, E)
        mapped = expert_map[topk_i]
        onehot = (mapped[..., None] == jnp.arange(E)).astype(x.dtype)
        w = jnp.einsum('btk,btke->bte', topk_p, onehot)
        h = jnp.einsum('btd,erd->bter', x, A)
        lora = jnp.einsum('bter,eor->bto', h * w[..., None], B) * SCALING
        return base_out + lora
    x = L0_attn_x
    mod = (_silu(L0_c) @ L0_wmod).reshape(L0_c.shape[0], 6, 1, -1)
    sa, ca, ga, sb, cb, gb = (mod[:, 0], mod[:, 1], mod[:, 2], mod[:, 3], mod[:, 4], mod[:, 5])
    ga = (2 * (ga >= 0) - 1) * jnp.maximum(jnp.abs(ga), 0.25)
    gb = (2 * (gb >= 0) - 1) * jnp.maximum(jnp.abs(gb), 0.25)
    h = _layernorm(x, axis=-1) * (1 + ca) + sa
    x = x + ga * _L0_attn_ref(h, L0_attn_wq, L0_attn_wk, L0_attn_wv, L0_attn_wo)
    h = _layernorm(x, axis=-1) * (1 + cb) + sb
    x = x + gb * _L0_ffn_ref(h, L0_ffn_W, L0_ffn_bias, L0_ffn_A, L0_ffn_Bf, L0_ffn_coeffs, L0_ffn_scales)
    mod = (_silu(L1_c) @ L1_wmod).reshape(L1_c.shape[0], 6, 1, -1)
    sa, ca, ga, sb, cb, gb = (mod[:, 0], mod[:, 1], mod[:, 2], mod[:, 3], mod[:, 4], mod[:, 5])
    ga = (2 * (ga >= 0) - 1) * jnp.maximum(jnp.abs(ga), 0.25)
    gb = (2 * (gb >= 0) - 1) * jnp.maximum(jnp.abs(gb), 0.25)
    h = _layernorm(x, axis=-1) * (1 + ca) + sa
    x = x + ga * _L1_attn_ref(h, L1_attn_Wq_down, L1_attn_Wq_up, L1_attn_Wq_rope, L1_attn_Wkv_down, L1_attn_Wk_up, L1_attn_Wv_up, L1_attn_Wk_rope, L1_attn_Wo)
    h = _layernorm(x, axis=-1) * (1 + cb) + sb
    x = x + gb * _L1_ffn_ref(h, L1_ffn_base_W, L1_ffn_base_b, L1_ffn_router_W, L1_ffn_router_b, L1_ffn_A, L1_ffn_B, L1_ffn_expert_map)
    return x

_drawn_inputs = setup_inputs


def setup_inputs(seed=0):
    import zlib

    import numpy as np

    out = dict(_drawn_inputs(seed))
    spreads = {'L0_ffn_scales': (0.5, 0.6)}
    factors = {'L0_ffn_bias': 28.811,
     'L0_ffn_A': 4.079,
     'L0_ffn_Bf': 4.064,
     'L0_ffn_coeffs': 8.0,
     'L1_attn_Wq_down': 5.869,
     'L1_attn_Wq_up': 5.882,
     'L1_attn_Wq_rope': 3.191,
     'L1_attn_Wk_up': 5.857,
     'L1_attn_Wk_rope': 3.163,
     'L1_ffn_base_b': 64.0,
     'L1_ffn_router_b': 64.0}
    for name, (base, spread) in spreads.items():
        noise = np.random.default_rng([zlib.crc32(name.encode()), seed]).standard_normal(out[name].shape)
        drawn = base * np.exp(spread * noise) if base else spread * noise
        out[name] = jnp.asarray(drawn.astype(out[name].dtype))
    for name, factor in factors.items():
        out[name] = (out[name] * factor).astype(out[name].dtype)
    return out
```

```python
from contextlib import ExitStack

import concourse.bass as bass
from concourse import mybir

F32 = mybir.dt.float32
F32R = mybir.dt.float32r
I32 = mybir.dt.int32
ALU = mybir.AluOpType
ACT = mybir.ActivationFunctionType
AX = mybir.AxisListType

P = 128
B, S, D = 2, 512, 512
KT = D // P
TB = S // P
NT = B * TB
EPS = 1e-5

HQ, HKV, HD = 32, 8, 128
GQ = HQ // HKV
NPROJ = GQ + 2
TURNS = NPROJ + 1
TURN = {"K": 0, "V": 1, "Q0": 2, "Vt": 3, "Q1": 4, "Q2": 5, "Q3": 6}
MASKED = -1e30
ER0 = 256

H1, HD1, LAT, ROPE = 128, 4, 64, 64
PAIRS = H1 // 2
UNITS = PAIRS * B
CR = 3 * HD1
SLOTS = [(0, 0), (0, 1), (1, 0), (1, 1), (0, 2), (0, 3), (1, 2), (1, 3)]
E1, R1 = 8, 16
NR = 2 * E1 - 1
SCALING = 2.0


def exists(v, n):
    return not isinstance(v, int) or 0 <= v < n


def wait(eng, sem, v):
    if not isinstance(v, int) or v > 0:
        eng.wait_ge(sem, v)


def adaln_two_layers(nc, a, out, upto=9):
    x_in, out_t = (v.rearrange("b (t p) d -> p (b t) d", p=P) for v in (a["L0_attn_x"], out))
    scratch = lambda name, shape: nc.dram_tensor(name, shape, F32, kind="Internal").ap()
    gate_d = scratch("gate_d", (4, B, D))
    qc_d = scratch("qc_d", (B, H1, CR, S))
    kc_d = scratch("kc_d", (B, H1, CR, S))
    o_d = scratch("o_d", (B, H1, 2, 8, S))

    ctx = ExitStack()
    with ctx:
        def sbuf_in(stack):
            return lambda name, shape, dt=F32: stack.enter_context(nc.sbuf_tensor(name, shape, dt))

        sb = sbuf_in(ctx)
        sem = lambda name: ctx.enter_context(nc.semaphore(name))
        bank = [ctx.enter_context(nc.psum_tensor(f"bank{i}", [P, 512], F32)) for i in range(8)]

        x = sb("x", [P, NT, D])
        hT_hi = sb("hT_hi", [P, KT, B * S], F32R)
        hT_lo = sb("hT_lo", [P, KT, B * S], F32R)
        ident = sb("ident", [P, P])
        gate = sb("gate", [P, 2, B, D])
        cT = sb("cT", [P, 2, B, KT])
        silu_e = sb("silu_e", [P, 2, B, KT])
        silu_d = sb("silu_d", [P, 2, B, KT])
        silu = sb("silu", [P, 2, B, KT])
        modc = sb("modc", [P, 2, 4, KT, B])
        stats = sb("stats", [P, NT, 6])
        mean_var = sb("mean_var", [P, NT, 2])
        var_eps = sb("var_eps", [P, NT])
        std = sb("std", [P, NT])
        rstd = sb("rstd", [P, NT])

        l0 = ctx.enter_context(ExitStack())
        sb0 = sbuf_in(l0)
        st_kv = sb0("st_kv", [P, 2, KT, HD])
        st_q = sb0("st_q", [P, KT, GQ * HD])
        st_wo = sb0("st_wo", [P, GQ, D])
        w_hi = sb0("w_hi", [P, NPROJ, KT, HD], F32R)
        w_lo = sb0("w_lo", [P, NPROJ, KT, HD], F32R)
        wo_hi = sb0("wo_hi", [P, GQ, D], F32R)
        wo_lo = sb0("wo_lo", [P, GQ, D], F32R)
        rope_cos = sb0("rope_cos", [P, S])
        rope_sin = sb0("rope_sin", [P, S])
        window = sb0("window", [P, 2 * P])
        gabs0 = sb0("gabs0", [B, 2, D])
        with ExitStack() as pro:
            sbp = sbuf_in(pro)
            wm0 = sbp("wm0", [P, 3, KT, D])
            modrow0 = sbp("modrow0", [B, 6, D])
            gsgn0 = sbp("gsgn0", [B, D])
            xn0 = sbp("xn0", [P, NT, D])
            full0 = sbp("full0", [P, 2, 512])
        kT_hi = sb0("kT_hi", [P, B, S], F32R)
        kT_lo = sb0("kT_lo", [P, B, S], F32R)
        qT_hi = sb0("qT_hi", [P, B, GQ, S], F32R)
        qT_lo = sb0("qT_lo", [P, B, GQ, S], F32R)
        v_hi = sb0("v_hi", [P, B, TB, HD], F32R)
        v_lo = sb0("v_lo", [P, B, TB, HD], F32R)
        vT = sb0("vT", [P, S])
        rope_a = sb0("rope_a", [P, 2, S])
        rope_b = sb0("rope_b", [P, 2, S])
        probs = sb0("probs", [P, 2, GQ, 2 * P])
        rmax = sb0("rmax", [P, 2, GQ])
        nmax = sb0("nmax", [P, 2, GQ])
        den = sb0("den", [P, 2, GQ])
        rden = sb0("rden", [P, 2, GQ])
        pT_hi = sb0("pT_hi", [P, 2, GQ * P], F32R)
        pT_lo = sb0("pT_lo", [P, 2, GQ * P], F32R)
        oT_hi = sb0("oT_hi", [P, GQ, P], F32R)
        oT_lo = sb0("oT_lo", [P, GQ, P], F32R)
        gated = sb0("gated", [P, D])
        l0.close()

        f0 = ctx.enter_context(ExitStack())
        sbf = sbuf_in(f0)
        wm1 = sbf("wm1", [P, 3, KT, D])
        modrow1 = sbf("modrow1", [B, 6, D])
        gsgn1 = sbf("gsgn1", [B, D])
        gabs1 = sbf("gabs1", [B, 2, D])
        xn1 = sbf("xn1", [P, NT, D])
        full1 = sbf("full1", [P, 2, 512])
        fw = sbf("fw", [P, KT, D])
        fbf = sbf("fbf", [P, KT, ER0])
        fa = sbf("fa", [P, 2, D])
        fa_s = sbf("fa_s", [P, 2, D])
        fbias = sbf("fbias", [P, D])
        fco = sbf("fco", [16, 2])
        fcw = sbf("fcw", [16, 1])
        expand = sbf("expand", [16, ER0])
        fer = sbf("fer", [P, 2])
        fbfT = sbf("fbfT", [P, 2, D])
        fwT = sbf("fwT", [P, KT, D])
        fw_hi = sbf("fw_hi", [P, KT, D], F32R)
        fw_lo = sbf("fw_lo", [P, KT, D], F32R)
        fu = sbf("fu", [P, 2, D])
        fg = sbf("fg", [P, 2, D])
        f0.close()

        l1 = ctx.enter_context(ExitStack())
        sb1 = sbuf_in(l1)
        k1 = sb1("k1", [P, B, S], F32R)
        k2 = sb1("k2", [P, B, 2, S], F32R)
        km = sb1("km", [P, B, 2, S], F32R)
        vc = sb1("vc", [P, NT, H1 * HD1])
        q1 = sb1("q1", [P, 4, 2, S], F32R)
        q2 = sb1("q2", [P, 4, 2, S], F32R)
        pT = sb1("pT", [P, 8, S])
        vp = sb1("vp", [P, 2, TB, 2, 32])
        wst = sb1("wst", [P, 2, KT, P])
        wr_hi = sb1("wr_hi", [P, 2, KT, P], F32R)
        wr_lo = sb1("wr_lo", [P, 2, KT, P], F32R)
        mcol = sb1("mcol", [P, 2, 4, 32], F32R)
        mrow = sb1("mrow", [P, 2, 4 * 32])
        ost = sb1("ost", [P, 2, S])
        ones = sb1("ones", [1, S])
        with ExitStack() as pre:
            sbq = sbuf_in(pre)
            dn = sbq("dn", [P, KT, P])
            kr = sbq("kr", [P, KT, P])
            dn_hi = sbq("dn_hi", [P, KT, P], F32R)
            dn_lo = sbq("dn_lo", [P, KT, P], F32R)
            kr_hi = sbq("kr_hi", [P, KT, P], F32R)
            kr_lo = sbq("kr_lo", [P, KT, P], F32R)
            up = sbq("up", [P, D])
            vup = sbq("vup", [P, D])
            lat = sbq("lat", [P, B * S])
            c_hi = sbq("c_hi", [P, 2, S], F32R)
            c_lo = sbq("c_lo", [P, 2, S], F32R)
        l1.close()

        f1 = ctx.enter_context(ExitStack())
        sbg = sbuf_in(f1)
        num = sbg("num", [P, 2, 2, S])
        dnm = sbg("dnm", [P, 2, 2, S])
        osum = sbg("osum", [P, 2, S])
        dsum = sbg("dsum", [P, 2, S])
        wo1 = sbg("wo1", [P, KT, D])
        wo1_hi = sbg("wo1_hi", [P, KT, D], F32R)
        wo1_lo = sbg("wo1_lo", [P, KT, D], F32R)
        oo_hi = sbg("oo_hi", [P, KT, B * S], F32R)
        oo_lo = sbg("oo_lo", [P, KT, B * S], F32R)
        og = sbg("og", [P, 2, D])
        f1.close()
        g1 = ctx.enter_context(ExitStack())
        sbh = sbuf_in(g1)
        xn2 = sbh("xn2", [P, NT, D])
        full2 = sbh("full2", [P, 2, 512])
        bw = sbh("bw", [P, KT, D])
        bwT_hi = sbh("bwT_hi", [P, KT, D], F32R)
        bwT_lo = sbh("bwT_lo", [P, KT, D], F32R)
        la = sbh("la", [P, D])
        laT_hi = sbh("laT_hi", [P, KT, P], F32R)
        laT_lo = sbh("laT_lo", [P, KT, P], F32R)
        rw = sbh("rw", [16, D])
        rwT_hi = sbh("rwT_hi", [P, KT, P], F32R)
        rwT_lo = sbh("rwT_lo", [P, KT, P], F32R)
        lb = sbh("lb", [P, KT, E1, R1])
        lbT_hi = sbh("lbT_hi", [P, D], F32R)
        lbT_lo = sbh("lbT_lo", [P, D], F32R)
        bbias = sbh("bbias", [P, D])
        rbias = sbh("rbias", [P, NR])
        emap_i = sbh("emap_i", [16, 1], I32)
        emap = sbh("emap", [16, 1])
        ecol = sbh("ecol", [16, P])
        ehot = sbh("ehot", [16, P])
        before = sbh("before", [P, NR, NR])
        lgT = sbh("lgT", [16, B * S])
        lg = sbh("lg", [P, NT, NR])
        lmax = sbh("lmax", [P, NT])
        lsum = sbh("lsum", [P, NT])
        lrec = sbh("lrec", [P, NT])
        prob = sbh("prob", [P, NT, NR])
        cmpg = sbh("cmpg", [P, NT, NR, NR])
        cmpe = sbh("cmpe", [P, NT, NR, NR])
        rank = sbh("rank", [P, NT, NR])
        kept = sbh("kept", [P, NT, 16])
        keptT = sbh("keptT", [16, B * S])
        wexp = sbh("wexp", [P, B * S])
        lh = sbh("lh", [P, B * S])
        lh_hi = sbh("lh_hi", [P, B * S], F32R)
        lh_lo = sbh("lh_lo", [P, B * S], F32R)
        gu = sbh("gu", [P, 2, D])
        gg = sbh("gg", [P, 2, D])
        g1.close()

        NORM = [(xn0, full0, 0, 0), (xn1, full1, 0, 2), (xn1, full1, 1, 0), (xn2, full2, 1, 2)]
        WM, MODROW, GSGN, GABS = (wm0, wm1), (modrow0, modrow1), (gsgn0, gsgn1), (gabs0, gabs1)

        x_loaded, consts_loaded, cond_loaded = sem("x_loaded"), sem("consts_loaded"), sem("cond_loaded")
        silu_exp, silu_step = sem("silu_exp"), sem("silu_step")
        wm_loaded = [sem(f"wm_loaded{i}") for i in range(3)]
        mod_mm, mod_row, col_mm, col_ready = (sem(n) for n in ("mod_mm", "mod_row", "col_mm", "col_ready"))
        gate_step, gate_row, gate_stored, gate_loaded = (sem(n) for n in ("gate_step", "gate_row", "gate_stored", "gate_loaded"))
        ln_stats, ln_aggr, ln_eps, ln_std, ln_rstd, ln_norm, ln_trans, ln_full, ln_hi, ln_lo = (
            sem(f"ln_{n}") for n in ("stats", "aggr", "eps", "std", "rstd", "norm", "trans", "full", "hi", "lo"))
        kv_loaded, q_loaded, wo_loaded = sem("kv_loaded"), sem("q_loaded"), sem("wo_loaded")
        w_hi_done, w_split, wo_hi_done, wo_split = sem("w_hi_done"), sem("w_split"), sem("wo_hi_done"), sem("wo_split")
        proj_done, proj_free = sem("proj_done"), sem("proj_free")
        rope_sum, rope_hi, rope_split, v_hi_done = sem("rope_sum"), sem("rope_hi"), sem("rope_split"), sem("v_hi_done")
        scores0, rowmax0, masked0, exp0, rden0, probs0 = (sem(n) for n in ("scores0", "rowmax0", "masked0", "exp0", "rden0", "probs0"))
        trans0, pT_hi_done, pT_split, pv0 = sem("trans0"), sem("pT_hi_done"), sem("pT_split"), sem("pv0")
        oT_hi_done, oT_split, wo_mm, wo_gated, attn0_added = (sem(n) for n in ("oT_hi_done", "oT_split", "wo_mm", "wo_gated", "attn0_added"))
        f_loaded, f_cw, f_er_mm, f_er, f_as = (sem(n) for n in ("f_loaded", "f_cw", "f_er_mm", "f_er", "f_as"))
        f_tr, f_trs, f_mg, f_sum, f_hi, f_split = (sem(n) for n in ("f_tr", "f_trs", "f_mg", "f_sum", "f_hi", "f_split"))
        f_mm, f_bias, f_gated, f_added = (sem(n) for n in ("f_mm", "f_bias", "f_gated", "f_added"))
        pre_loaded, pre_hi, pre_split, lat_mm, lat_ready = (sem(n) for n in ("pre_loaded", "pre_hi", "pre_split", "lat_mm", "lat_ready"))
        kr_mm, kr_hi_done, kr_split, zeroed = sem("kr_mm"), sem("kr_hi_done"), sem("kr_split"), sem("zeroed")
        c_mm, c_hi_done, c_split, vc_mm, vc_ready = (sem(n) for n in ("c_mm", "c_hi_done", "c_split", "vc_mm", "vc_ready"))
        c_stored = [sem(f"c_stored{i}") for i in range(2)]
        wr_loaded = [sem(f"wr_loaded{i}") for i in range(2)]
        wr_hi_done, wr_split = sem("wr_hi_done"), sem("wr_split")
        qr_mm, q2_hi, q1_hi, q1_split = sem("qr_mm"), sem("q2_hi"), sem("q1_hi"), sem("q1_split")
        mc_loaded, k2c_loaded, m_loaded = ([sem(f"{n}{i}") for i in range(2)] for n in ("mc_loaded", "k2c_loaded", "m_loaded"))
        ones_set = sem("ones_set")
        max_mm, max_done, m_turned = sem("max_mm"), sem("max_done"), sem("m_turned")
        scores1, exp1, pv1, vp_ready, o_copied = (sem(n) for n in ("scores1", "exp1", "pv1", "vp_ready", "o_copied"))
        o_stored = [sem(f"o_stored{i}") for i in range(2)]
        num_loaded = [sem(f"num_loaded{i}") for i in range(2)]
        o_step, oo_hi_done, oo_split = sem("o_step"), sem("oo_hi_done"), sem("oo_split")
        wo1_loaded, wo1_hi_done, wo1_split, wo1_mm, wo1_gated, attn1_added = (
            sem(n) for n in ("wo1_loaded", "wo1_hi_done", "wo1_split", "wo1_mm", "wo1_gated", "attn1_added"))
        g_loaded, g_tr, g_hi, g_lo, g_const = (sem(n) for n in ("g_loaded", "g_tr", "g_hi", "g_lo", "g_const"))
        r_mm, r_copied, r_tr, r_step, r_exp, r_kept, r_ktr, r_ktc = (
            sem(n) for n in ("r_mm", "r_copied", "r_tr", "r_step", "r_exp", "r_kept", "r_ktr", "r_ktc"))
        r_wmm, r_wexp, r_hmm, r_hfull, r_hhi, r_hlo = (sem(n) for n in ("r_wmm", "r_wexp", "r_hmm", "r_hfull", "r_hhi", "r_hlo"))
        g_mm, g_bias, g_gated, g_added, stored = (sem(n) for n in ("g_mm", "g_bias", "g_gated", "g_added", "stored"))
        spare = sem("spare")

        X_READY = [(x_loaded, 16 * NT), (attn0_added, NT * HKV), (f_added, NT), (attn1_added, NT)]

        wq, wk, wv, wo = a["L0_attn_wq"], a["L0_attn_wk"], a["L0_attn_wv"], a["L0_attn_wo"]
        wq_v, wk_v, wv_v = (w.rearrange("(k p) n -> p k n", p=P) for w in (wq, wk, wv))
        wo_v = wo.rearrange("(h p) n -> p h n", p=P)
        wr_v = a["L1_attn_Wq_rope"].rearrange("(k p) n -> p k n", p=P)
        wmod_v = [a[f"L{l}_wmod"].rearrange("(p k) n -> p k n", k=KT) for l in range(2)]

        SLOT_PROJ = [["K", "V"], ["Q0", "Vt", "Q1"], ["Q2", "Q3"], []]
        W_TILE = {"K": 0, "V": 1, "Q0": 2, "Q1": 3, "Q2": 4, "Q3": 5}
        ROPE_NO = {"K": 0, "Q0": 1, "Q1": 2, "Q2": 3, "Q3": 4}

        block = ctx.enter_context(nc.Block())

        @block.sync
        def _(sp):
            sp.dma_start(cT[:, 0], a["L0_c"].rearrange("b (p k) -> p b k", k=KT)).then_inc(cond_loaded, 16)
            sp.dma_start(cT[:, 1], a["L1_c"].rearrange("b (p k) -> p b k", k=KT)).then_inc(cond_loaded, 16)
            sp.dma_start(ident[:], a["identity"]).then_inc(consts_loaded, 16)
            for t in range(NT):
                sp.dma_start(x[:, t], x_in[:, t]).then_inc(x_loaded, 16)

            def load_wmod(l, c):
                i = 6 * l + c
                wait(sp, mod_mm, i - 2)
                sp.dma_start(WM[l][:, i % 3], wmod_v[l][:, :, c * D:(c + 1) * D]).then_inc(wm_loaded[i % 3], 16)

            def store_gates(l):
                for w in range(2):
                    sp.wait_ge(gate_row, 2 * l + w + 1)
                    sp.dma_start(gate_d[2 * l + w], GABS[l][:, w]).then_inc(gate_stored, 16)
                    sp.wait_ge(gate_stored, 16 * (2 * l + w + 1))
                    sp.dma_start(gate[:, w], gate_d[2 * l + w:2 * l + w + 1].rearrange("o b d -> o (b d)").partition_broadcast(P)
                                 .rearrange("p o n -> p (o n)")).then_inc(gate_loaded, 16)

            def hold(semaphore, v):
                if not isinstance(v, int) or v > 0:
                    sp.wait_ge(semaphore, v)
                    sp.sem_inc(spare, 1)

            def load_kv(n):
                if exists(n, HKV):
                    hold(w_split, 6 * n)
                    sp.dma_start(st_kv[:, 0], wk_v[:, :, bass.ts(n, HD)]).then_inc(kv_loaded, 16)
                    sp.dma_start(st_kv[:, 1], wv_v[:, :, bass.ts(n, HD)]).then_inc(kv_loaded, 16)
                    sp.dma_start(st_q[:], wq_v[:, :, bass.ts(n, GQ * HD)]).then_inc(q_loaded, 16)

            def load_wo(n):
                if exists(n, HKV):
                    hold(wo_split, n)
                    sp.dma_start(st_wo[:], wo_v[:, bass.ts(n, GQ)]).then_inc(wo_loaded, 16)

            load_wmod(0, 0)
            load_wmod(0, 1)
            load_kv(0)
            sp.dma_start(rope_cos[:], a["rope_cos"]).then_inc(consts_loaded, 16)
            sp.dma_start(rope_sin[:], a["rope_sin"]).then_inc(consts_loaded, 16)
            sp.dma_start(window[:], a["window_mask"]).then_inc(consts_loaded, 16)
            load_wo(0)
            for c in range(2, 6):
                load_wmod(0, c)
            store_gates(0)
            if upto >= 2:
              with sp.Fori(1, HKV) as n:
                load_kv(n)
                load_wo(n)

            if upto >= 3:
              sp.wait_ge(attn0_added, NT * HKV)
              sp.dma_start(fw[:], a["L0_ffn_W"].rearrange("(k p) d -> p k d", p=P)).then_inc(f_loaded, 16)
              for k in range(KT):
                  sp.dma_start(fbf[:, k].rearrange("p (e r) -> p e r", r=16),
                               a["L0_ffn_Bf"].rearrange("e (k p) r -> k p e r", p=P)[k]).then_inc(f_loaded, 16)
              sp.dma_start(fa[:], a["L0_ffn_A"].rearrange("(t e) r d -> (e r) t d", t=2)).then_inc(f_loaded, 16)
              sp.dma_start(fbias[:], a["L0_ffn_bias"].rearrange("(o n) -> o n", o=1).partition_broadcast(P)
                           .rearrange("p o n -> p (o n)")).then_inc(f_loaded, 16)
              sp.dma_start(fco[:, 0:1], a["L0_ffn_coeffs"].rearrange("(e o) -> e o", o=1)).then_inc(f_loaded, 16)
              sp.dma_start(fco[:, 1:2], a["L0_ffn_scales"].rearrange("(e o) -> e o", o=1)).then_inc(f_loaded, 16)
              sp.dma_start(expand[:], a["lora_expand"]).then_inc(f_loaded, 16)
              for c in range(6):
                  load_wmod(1, c)
              sp.wait_ge(f_gated, NT)
              store_gates(1)

            if upto >= 4:
              sp.wait_ge(ln_lo, 3 * NT)
              for w, name in enumerate(("L1_attn_Wq_down", "L1_attn_Wkv_down")):
                  sp.dma_start(dn[:, :, w * LAT:(w + 1) * LAT], a[name].rearrange("(k p) n -> p k n", p=P)).then_inc(pre_loaded, 16)
              for w in range(2):
                  sp.dma_start(kr[:, :, w * ROPE:(w + 1) * ROPE],
                               a["L1_attn_Wk_rope"].rearrange("(k p) n -> p k n", p=P)).then_inc(pre_loaded, 16)
              sp.dma_start(up[0:LAT], a["L1_attn_Wq_up"]).then_inc(pre_loaded, 16)
              sp.dma_start(up[LAT:P], a["L1_attn_Wk_up"]).then_inc(pre_loaded, 16)
              sp.dma_start(vup[LAT:P], a["L1_attn_Wv_up"]).then_inc(pre_loaded, 16)

              def load_rope_weights(p, par):
                  if exists(p, PAIRS):
                      hold(wr_split, p - 1)
                      sp.dma_start(wst[:, par], wr_v[:, :, bass.ts(p, P)]).then_inc(wr_loaded[par], 16)

              load_rope_weights(0, 0)
              load_rope_weights(1, 1)
              n = 0
              for b in range(B):
                  for m in range(KT):
                      for dst, order in ((qc_d, (0, 1, 0)), (kc_d, (0, 0, 1))):
                          n += 1
                          sp.wait_ge(c_split, n)
                          for g, half in enumerate(order):
                              src = (c_hi, c_lo)[half][:, (n - 1) % 2].bitcast(F32)
                              sp.dma_start(dst[b, 32 * m:32 * m + 32, HD1 * g:HD1 * g + HD1], src).then_inc(c_stored[(n - 1) % 2], 16)

            def rows(h):
                return slice(ROPE, ROPE + CR) if h == 0 else slice(0, CR)

            def maxrow(h):
                return ROPE + CR if h == 0 else CR

            def period(u, k):
                v, vb = u + 1, (k + 1) % 2
                if exists(v, UNITS):
                    hold(scores1, 8 * (v - 1))
                    for h in range(2):
                        sp.dma_start(k2[rows(h), vb, h].bitcast(F32), kc_d[vb, hd(u, k, 1, h)].rearrange("o c s -> (o c) s"))\
                          .then_inc(k2c_loaded[vb], 16)
                v, vb = u + 3, (k + 3) % 2
                if exists(v, UNITS):
                    hold(max_mm, 8 * (v - 1))
                    for h in range(2):
                        sp.dma_start(km[rows(h), vb, h].bitcast(F32), kc_d[vb, hd(u, k, 3, h)].rearrange("o c s -> (o c) s"))\
                          .then_inc(mc_loaded[vb], 16)
                    hold(scores1, 8 * (v - 3))
                    for h in range(2):
                        sp.dma_start(q2[rows(h), (k + 3) % 4, h].bitcast(F32), qc_d[vb, hd(u, k, 3, h)].rearrange("o c s -> (o c) s"))\
                          .then_inc(mc_loaded[vb], 16)
                if k % 2 == 0:
                    load_rope_weights(pairs(u, k, 6), (k // 2 + 3) % 2)
                v = u - 1
                if exists(v, UNITS):
                    vb = (k + 1) % 2
                    hold(o_copied, v + 1)
                    for h in range(2):
                        for par in range(2):
                            j = 2 * h + par
                            sp.dma_start(o_d[vb, hd(u, k, -1, h), par].rearrange("o c s -> (o c) s"), ost[32 * j:32 * j + 8, (k + 1) % 2])\
                              .then_inc(o_stored[(k + 1) % 2], 16)
                v = u + 2
                if exists(v, UNITS):
                    hold(m_turned, v + 1)
                    for h in range(2):
                        r = maxrow(h)
                        sp.dma_start(q2[r:r + 1, (k + 2) % 4, h].bitcast(F32).rearrange("p (q n) -> p q n", q=4),
                                     mrow[h:P:32, k % 2]).then_inc(m_loaded[k % 2], 16)

            def pairs(u, k, ahead):
                if isinstance(u, int):
                    return (u + ahead) // 2
                return 2 * G[0] + (k + ahead) // 2

            def hd(u, k, ahead, h):
                return bass.ds(2 * pairs(u, k, ahead) + h, 1)

            G = [None]
            if upto >= 4:
                for i in range(2):
                    sp.wait_ge(c_stored[i], 48 * KT * B)
                sp.wait_ge(zeroed, 6)
                for b in range(B):
                    for h in range(2):
                        sp.dma_start(k2[maxrow(h):maxrow(h) + 1, b, h].bitcast(F32), ones[:]).then_inc(ones_set, 16)
                for u in range(-3, 6):
                    period(u, u % 4)
                with sp.Fori(1, UNITS // 4 - 2) as g:
                    G[0] = g
                    for k in range(2, 6):
                        period(4 * g + k, k)
                for u in range(UNITS - 6, UNITS + 1):
                    period(u, u % 4)

                for i in range(2):
                    sp.wait_ge(o_stored[i], 64 * PAIRS)
                sp.dma_start(wo1[:], a["L1_attn_Wo"].rearrange("(k p) n -> p k n", p=P)).then_inc(wo1_loaded, 16)
                n = 0
                for b in range(B):
                    for m in range(KT):
                        wait(sp, o_step, 4 * (n - 1))
                        for par in range(2):
                            for dst, r in ((num, 0), (dnm, HD1)):
                                sp.dma_start(dst[:, n % 2, par], o_d[b, 32 * m:32 * m + 32, par, r:r + HD1])\
                                  .then_inc(num_loaded[n % 2], 16)
                        n += 1
            if upto >= 6:
                sp.wait_ge(attn1_added, NT)
                sp.dma_start(bw[:], a["L1_ffn_base_W"].rearrange("(k p) d -> p k d", p=P)).then_inc(g_loaded, 16)
                sp.dma_start(la[:], a["L1_ffn_A"].rearrange("e r d -> (e r) d")).then_inc(g_loaded, 16)
                sp.dma_start(rw[0:NR], a["L1_ffn_router_W"]).then_inc(g_loaded, 16)
                for k in range(KT):
                    sp.dma_start(lb[:, k], a["L1_ffn_B"].rearrange("e (k p) r -> k p e r", p=P)[k]).then_inc(g_loaded, 16)
                for dst, name in ((bbias, "L1_ffn_base_b"), (rbias, "L1_ffn_router_b")):
                    sp.dma_start(dst[:], a[name].rearrange("(o n) -> o n", o=1).partition_broadcast(P)
                                 .rearrange("p o n -> p (o n)")).then_inc(g_loaded, 16)
                sp.dma_start(emap_i[0:NR], a["L1_ffn_expert_map"].rearrange("(e o) -> e o", o=1)).then_inc(g_loaded, 16)
                sp.dma_start(ecol[:], a["expert_of_column"]).then_inc(g_loaded, 16)
                sp.dma_start(before[:].rearrange("p n m -> p (n m)"),
                             a["entry_before"].rearrange("n m -> (n m)").rearrange("(o k) -> o k", o=1).partition_broadcast(P)
                             .rearrange("p o n -> p (o n)")).then_inc(g_loaded, 16)
            last_sem, last = {1: X_READY[0], 2: X_READY[1], 3: X_READY[2], 4: X_READY[3], 5: X_READY[3]}.get(upto, (g_added, None))
            for t in range(NT):
                sp.wait_ge(last_sem, last or t + 1)
                sp.dma_start(out_t[:, t], x[:, t]).then_inc(stored, 16)
            sp.wait_ge(stored, 16 * NT)

        @block.gpsimd
        def _(pool):
            def split_weights(n, tiles):
                for m in tiles:
                    pool.wait_ge(w_hi_done, 6 * n + m + 1)
                    src = st_kv[:, m] if m < 2 else st_q[:, :, (m - 2) * HD:(m - 1) * HD]
                    pool.tensor_tensor(w_lo[:, m], src, w_hi[:, m].bitcast(F32), ALU.subtract).then_inc(w_split, 1)

            def split_wo(n):
                pool.wait_ge(wo_hi_done, n + 1)
                pool.tensor_tensor(wo_lo[:], st_wo[:], wo_hi[:].bitcast(F32), ALU.subtract).then_inc(wo_split, 1)

            def rope(half, name, b):
                r = 5 * half + ROPE_NO[name]
                i = (b + ROPE_NO[name]) % 2
                pool.wait_ge(proj_free, TURNS * half + TURN[name] + 1)
                pool.tensor_tensor(rope_a[:, i], rope_a[:, i], rope_b[:, i], ALU.add).then_inc(rope_sum, 1)
                pool.wait_ge(rope_hi, r + 1)
                hi, lo = (kT_hi[:, b], kT_lo[:, b]) if name == "K" else (qT_hi[:, b, ROPE_NO[name] - 1], qT_lo[:, b, ROPE_NO[name] - 1])
                pool.tensor_tensor(lo, rope_a[:, i], hi.bitcast(F32), ALU.subtract).then_inc(rope_split, 1)

            def add_attention(slot, tile):
                pool.wait_ge(wo_gated, slot + 1)
                pool.tensor_tensor(x[:, tile], x[:, tile], gated[:], ALU.add).then_inc(attn0_added, 1)

            split_weights(0, range(6))
            pool.wait_ge(ln_lo, NT)
            for name in ROPE_NO:
                rope(0, name, 0)

            def kv_head(n, last):
                for b in range(B):
                    half = 2 * n + b
                    more = not (last and b == 1)
                    for qb in range(TB):
                        slot = 4 * half + qb
                        if b == 0 and qb == 0:
                            split_wo(n)
                        for name in SLOT_PROJ[qb]:
                            if name in ROPE_NO and more:
                                rope(half + 1, name, 1 - b)
                        if b == 0 and qb in (1, 2, 3) and not last:
                            split_weights(n + 1, ((0, 1), (2, 3), (4, 5))[qb - 1])
                        if not (b == 0 and qb == 0):
                            add_attention(slot - 1, 4 * b + qb - 1)
                add_attention(8 * n + 7, NT - 1)

            if upto >= 2:
                kv_head(0, False)
                with pool.Fori(1, HKV - 1) as n:
                    kv_head(n, False)
                kv_head(HKV - 1, True)
            if upto >= 3:
                for t in range(NT):
                    pool.wait_ge(f_gated, t + 1)
                    pool.tensor_tensor(x[:, t], x[:, t], fg[:, t % 2], ALU.add).then_inc(f_added, 1)
            if upto >= 4:
                pool.wait_ge(ln_lo, 3 * NT)
                pool.memset(k2[:].bitcast(F32), 0.0).then_inc(zeroed, 1)
                pool.memset(km[:].bitcast(F32), 0.0).then_inc(zeroed, 1)
                pool.memset(q2[:].bitcast(F32), 0.0).then_inc(zeroed, 1)
                pool.memset(vp[:], 0.0).then_inc(zeroed, 1)
                pool.memset(mcol[:].bitcast(F32), 0.0).then_inc(zeroed, 1)
                pool.memset(ones[:], 1.0).then_inc(zeroed, 1)
                pool.wait_ge(zeroed, 6)
                pool.memset(vp[:, :, :, :, HD1:2 * HD1], 1.0).then_inc(zeroed, 1)

                def split_rope_weights(p, par):
                    if exists(p, PAIRS):
                        pool.wait_ge(wr_hi_done, p + 1)
                        pool.tensor_tensor(wr_lo[:, par], wst[:, par], wr_hi[:, par].bitcast(F32), ALU.subtract).then_inc(wr_split, 1)

                split_rope_weights(0, 0)
                split_rope_weights(1, 1)
                with pool.Fori(0, PAIRS // 2 - 1) as g:
                    split_rope_weights(2 * g + 2, 0)
                    split_rope_weights(2 * g + 3, 1)
            if upto >= 5:
                for t in range(NT):
                    pool.wait_ge(wo1_gated, t + 1)
                    pool.tensor_tensor(x[:, t], x[:, t], og[:, t % 2], ALU.add).then_inc(attn1_added, 1)
            if upto >= 6:
                for t in range(NT):
                    pool.wait_ge(g_gated, t + 1)
                    pool.tensor_tensor(x[:, t], x[:, t], gg[:, t % 2], ALU.add).then_inc(g_added, 1)

        @block.scalar
        def _(act):
            act.wait_ge(cond_loaded, 32)
            act.activation(silu_e[:], cT[:], ACT.Exp, scale=-1.0).then_inc(silu_exp, 1)

            def mod_rows(l, chunks):
                for c in chunks:
                    act.wait_ge(mod_mm, 6 * l + c + 1)
                    act.activation(MODROW[l][:, c], bank[c % 4][0:B, :], ACT.Copy).then_inc(mod_row, 1)

            def norm_std(ph):
                act.wait_ge(ln_eps, ph + 1)
                act.activation(std[:], var_eps[:], ACT.Sqrt).then_inc(ln_std, 1)

            def norm_hi(ph):
                for j in range(NT):
                    act.wait_ge(ln_full, NT * ph + j + 1)
                    act.activation(hT_hi[:, j % KT, (j // KT) * S:(j // KT + 1) * S], NORM[ph][1][:, j % 2], ACT.Copy).then_inc(ln_hi, 1)

            mod_rows(0, (0, 1))
            norm_std(0)
            norm_hi(0)
            mod_rows(0, (2, 3, 4, 5))

            def rope_high(half, name, b):
                r = 5 * half + ROPE_NO[name]
                act.wait_ge(rope_sum, r + 1)
                hi = kT_hi[:, b] if name == "K" else qT_hi[:, b, ROPE_NO[name] - 1]
                act.activation(hi, rope_a[:, (b + ROPE_NO[name]) % 2], ACT.Copy).then_inc(rope_hi, 1)

            def v_high(half, b):
                act.wait_ge(proj_done, TURNS * half + TURN["Vt"] + 1)
                act.activation(v_hi[:, b].rearrange("p t d -> p (t d)"), bank[6 + (b + TURN["Vt"]) % 2][:], ACT.Copy).then_inc(v_hi_done, 1)

            def high(half, name, b):
                if name in ROPE_NO:
                    rope_high(half, name, b)
                elif name == "Vt":
                    v_high(half, b)

            def exps(slot, qb):
                i = qb % 2
                c = slice(P, 2 * P) if qb == 0 else slice(0, 2 * P)
                act.wait_ge(masked0, slot + 1)
                for h in range(GQ):
                    e = act.activation(probs[:, i, h, c], probs[:, i, h, c], ACT.Exp, bias=nmax[:, i, h:h + 1], scale=1.0,
                                       accum_out=den[:, i, h:h + 1])
                e.then_inc(exp0, 1)

            def kv_head0():
                for name in TURN:
                    high(0, name, 0)
                exps(0, 0)

            def kv_head(n, last):
                for b in range(B):
                    half = 2 * n + b
                    more = not (last and b == 1)
                    for qb in range(TB):
                        slot = 4 * half + qb
                        names = [m for m in SLOT_PROJ[qb] if m != "V"] if more else []
                        for name in names[:-1]:
                            high(half + 1, name, 1 - b)
                        act.wait_ge(trans0, slot + 1)
                        for kb in range(1 if qb == 0 else 0, 2):
                            e = act.activation(pT_hi[:, kb], bank[2 + kb][:], ACT.Copy)
                        e.then_inc(pT_hi_done, 1)
                        for name in names[-1:]:
                            high(half + 1, name, 1 - b)
                        if b == 1 and qb == TB - 1:
                            out_high(slot)
                        if not (last and b == 1 and qb == TB - 1):
                            exps(slot + 1, (qb + 1) % TB)
                        if not (b == 1 and qb == TB - 1):
                            out_high(slot)

            def out_high(slot):
                act.wait_ge(pv0, slot + 1)
                act.activation(oT_hi[:].rearrange("p h t -> p (h t)"), bank[4][:], ACT.Copy).then_inc(oT_hi_done, 1)

            if upto >= 2:
                kv_head0()
                kv_head(0, False)
                with act.Fori(1, HKV - 1) as n:
                    kv_head(n, False)
                kv_head(HKV - 1, True)
            if upto >= 3:
                norm_std(1)
                norm_hi(1)
                for t in range(2):
                    act.wait_ge(f_tr, t + 1)
                    act.activation(fbfT[:, t], bank[t][:], ACT.Copy).then_inc(f_trs, 1)
                for k in range(KT):
                    act.wait_ge(f_tr, 2 + k + 1)
                    act.activation(fwT[:, k], bank[2 + k][:], ACT.Copy).then_inc(f_trs, 1)
                for k in range(KT):
                    act.wait_ge(f_sum, k + 1)
                    act.activation(fw_hi[:, k], fwT[:, k], ACT.Copy).then_inc(f_hi, 1)
                mod_rows(1, range(6))
            if upto >= 4:
                norm_std(2)
                norm_hi(2)
                for b in range(B):
                    act.wait_ge(lat_mm, b + 1)
                    act.activation(lat[:, b * S:(b + 1) * S], bank[b][:], ACT.Copy).then_inc(lat_ready, 1)
                act.wait_ge(zeroed, 6)
                for b in range(B):
                    act.wait_ge(kr_mm, b + 1)
                    act.activation(k1[:, b], bank[2 + b][:], ACT.Copy)
                    act.activation(km[0:ROPE, b, 0], bank[2 + b][0:ROPE], ACT.Copy)
                    act.activation(km[ROPE:P, b, 1], bank[2 + b][ROPE:P], ACT.Copy).then_inc(kr_hi_done, 1)
                n = 0
                for b in range(B):
                    for m in range(KT):
                        for w in range(2):
                            n += 1
                            act.wait_ge(c_mm, n)
                            wait(act, c_stored[(n - 1) % 2], 48 * ((n - 1) // 2))
                            act.activation(c_hi[:, (n - 1) % 2], bank[4 + (n - 1) % 2][:], ACT.Copy).then_inc(c_hi_done, 1)
                for t in range(NT):
                    act.wait_ge(vc_mm, t + 1)
                    act.activation(vc[:, t], bank[6 + t % 2][:], ACT.Copy).then_inc(vc_ready, 1)

                act.sem_inc(exp1, 4)

                def q_high(z, k, dst, done):
                    if exists(z, UNITS):
                        act.wait_ge(qr_mm, z + 1)
                        act.activation(dst[0:ROPE, k % 4, 0], bank[6][0:ROPE], ACT.Copy)
                        act.activation(dst[ROPE:P, k % 4, 1], bank[6][ROPE:P], ACT.Copy).then_inc(done, 1)

                def period(u, k, pair):
                    q_high(u + 2, k + 2, q2, q2_hi)
                    for s in range(8):
                        if s == 2:
                            q_high(u + 2, k + 2, q1, q1_hi)
                            if exists(u - 1, UNITS):
                                act.wait_ge(pv1, 2 * u + 1)
                                wait(act, o_stored[(k + 1) % 2], 64 * pair(-1))
                                act.activation(ost[:, (k + 1) % 2], bank[7][:], ACT.Copy).then_inc(o_copied, 1)
                        if exists(u, UNITS):
                            act.wait_ge(scores1, 8 * u + s + 1)
                            wait(act, pv1, 2 * u + s // 4)
                            act.activation(pT[:, s], bank[s % 4][:], ACT.Exp, scale=float((HD1 + ROPE) ** -0.5)).then_inc(exp1, 1)

                for u in range(-3, 6):
                    period(u, u % 4, lambda n, u=u: (u + n) // 2)
                with act.Fori(1, UNITS // 4 - 2) as g:
                    for k in range(2, 6):
                        period(4 * g + k, k, lambda n, k=k: 2 * g + (k + n) // 2)
                for u in range(UNITS - 6, UNITS + 1):
                    period(u, u % 4, lambda n, u=u: (u + n) // 2)
            if upto >= 5:
                for k in range(KT):
                    act.wait_ge(wo1_loaded, 16)
                    act.activation(wo1_hi[:, k], wo1[:, k], ACT.Copy).then_inc(wo1_hi_done, 1)
                n = 0
                for b in range(B):
                    for m in range(KT):
                        n += 1
                        act.wait_ge(o_step, 4 * n)
                        act.activation(oo_hi[:, m, b * S:(b + 1) * S], osum[:, (n - 1) % 2], ACT.Copy).then_inc(oo_hi_done, 1)
            if upto >= 6:
                norm_std(3)
                norm_hi(3)
                for i, dst in enumerate([*(bwT_hi[:, k] for k in range(KT)), laT_hi[:].rearrange("p k n -> p (k n)"),
                                         rwT_hi[:, :, 0:NR], lbT_hi[:]]):
                    act.wait_ge(g_tr, i + 1)
                    src = bank[i][:] if i != 5 else bank[i][:].rearrange("p (k n) -> p k n", k=KT)[:, :, 0:NR]
                    if i == 5:
                        act.wait_ge(g_const, 1)
                    act.activation(dst, src, ACT.Copy).then_inc(g_hi, 1)
                for b in range(B):
                    act.wait_ge(r_mm, b + 1)
                    act.activation(lgT[0:NR, b * S:(b + 1) * S], bank[b][0:NR], ACT.Copy).then_inc(r_copied, 1)
                act.wait_ge(r_step, 3)
                act.activation(prob[:], lg[:], ACT.Exp).then_inc(r_exp, 1)
                for b in range(B):
                    act.wait_ge(r_ktr, b + 1)
                    act.activation(keptT[0:NR, b * S:(b + 1) * S], bank[2 + b][0:NR], ACT.Copy).then_inc(r_ktc, 1)
                for b in range(B):
                    act.wait_ge(r_wmm, b + 1)
                    act.activation(wexp[:, b * S:(b + 1) * S], bank[4 + b][:], ACT.Copy, scale=SCALING).then_inc(r_wexp, 1)
                for b in range(B):
                    act.wait_ge(r_hfull, b + 1)
                    act.activation(lh_hi[:, b * S:(b + 1) * S], lh[:, b * S:(b + 1) * S], ACT.Copy).then_inc(r_hhi, 1)

        @block.vector
        def _(dve):
            dve.wait_ge(silu_exp, 1)
            dve.tensor_scalar(silu_d[:], silu_e[:], 1.0, None, ALU.add).then_inc(silu_step, 1)
            dve.wait_ge(silu_step, 1)
            dve.reciprocal(silu_e[:], silu_d[:]).then_inc(silu_step, 1)
            dve.wait_ge(silu_step, 2)
            dve.tensor_tensor(silu[:], cT[:], silu_e[:], ALU.mult).then_inc(silu_step, 1)

            def mod_cols(l, half):
                i = 2 * l + half
                dve.wait_ge(col_mm, i + 1)
                src = bank[4][:, 0:16].rearrange("p (v k b) -> p v k b", v=2, k=KT)
                dve.tensor_copy(modc[:, l, 2 * half], src[:, 0])
                dve.tensor_scalar(modc[:, l, 2 * half + 1], src[:, 1], 1.0, None, ALU.add).then_inc(col_ready, 1)

            def mod_gate(l, w):
                i = 2 * l + w
                row = MODROW[l][:, 3 * w + 2]
                dve.wait_ge(mod_row, 6 * l + 3 * w + 3)
                dve.tensor_scalar(GSGN[l][:], row, 0.0, 2.0, ALU.is_ge, ALU.mult).then_inc(gate_step, 1)
                dve.wait_ge(gate_step, 3 * i + 1)
                dve.tensor_scalar(GSGN[l][:], GSGN[l][:], -1.0, None, ALU.add).then_inc(gate_step, 1)
                dve.wait_ge(gate_step, 3 * i + 2)
                dve.tensor_tensor(GABS[l][:, w], GSGN[l][:], row, ALU.mult).then_inc(gate_step, 1)
                dve.wait_ge(gate_step, 3 * i + 3)
                dve.scalar_tensor_tensor(GABS[l][:, w], GABS[l][:, w], 0.25, GSGN[l][:], ALU.max, ALU.mult).then_inc(gate_row, 1)
                dve.wait_ge(gate_row, i + 1)

            def norm(ph):
                xn, full, l, v = NORM[ph]
                ready, count = X_READY[ph]
                for t in range(NT):
                    dve.wait_ge(ready, count if ph == 0 else count - NT + t + 1)
                    dve.bn_stats(stats[:, t], x[:, t]).then_inc(ln_stats, 1)
                for t in range(NT):
                    dve.wait_ge(ln_stats, NT * ph + t + 1)
                    dve.bn_aggr(mean_var[:, t], stats[:, t]).then_inc(ln_aggr, 1)
                dve.wait_ge(ln_aggr, NT * (ph + 1))
                dve.tensor_scalar(var_eps[:], mean_var[:, :, 1], EPS, None, ALU.add).then_inc(ln_eps, 1)
                dve.wait_ge(ln_std, ph + 1)
                dve.reciprocal(rstd[:], std[:]).then_inc(ln_rstd, 1)
                dve.wait_ge(ln_rstd, ph + 1)
                for t in range(NT):
                    dve.tensor_scalar(xn[:, t], x[:, t], mean_var[:, t, 0:1], rstd[:, t:t + 1], ALU.subtract, ALU.mult).then_inc(ln_norm, 1)

                def low(j):
                    dve.wait_ge(ln_hi, NT * ph + j + 1)
                    at = slice((j // KT) * S, (j // KT + 1) * S)
                    dve.tensor_tensor(hT_lo[:, j % KT, at], full[:, j % 2], hT_hi[:, j % KT, at].bitcast(F32), ALU.subtract).then_inc(ln_lo, 1)

                dve.wait_ge(col_ready, 2 * l + v // 2 + 1)
                for j in range(NT):
                    b, k = j // KT, j % KT
                    dve.wait_ge(ln_trans, NT * ph + TB * (b + 1))
                    wait(dve, ln_lo, NT * ph + j - 1 if j >= 2 else 0)
                    dve.tensor_scalar(full[:, j % 2], bank[j][:], modc[:, l, v + 1, k, b:b + 1], modc[:, l, v, k, b:b + 1],
                                      ALU.mult, ALU.add).then_inc(ln_full, 1)
                    if j >= 1:
                        low(j - 1)
                low(NT - 1)

            def split_weights(n, tiles):
                for m in tiles:
                    src = st_kv[:, m] if m < 2 else st_q[:, :, (m - 2) * HD:(m - 1) * HD]
                    if m < 2:
                        dve.wait_ge(kv_loaded, 32 * n + 32)
                    else:
                        dve.wait_ge(q_loaded, 16 * n + 16)
                    if not isinstance(n, int) or n > 0:
                        name = [k for k, v in W_TILE.items() if v == m][0]
                        dve.wait_ge(proj_done, TURNS * (2 * n - 1) + TURN[name] + 1)
                    dve.tensor_copy(w_hi[:, m], src).then_inc(w_hi_done, 1)

            def split_wo(n):
                dve.wait_ge(wo_loaded, 16 * n + 16)
                wait(dve, wo_mm, 8 * n)
                dve.tensor_copy(wo_hi[:], st_wo[:]).then_inc(wo_hi_done, 1)

            def evacuate(half, name, b):
                e = TURNS * half + TURN[name]
                ps = bank[6 + (b + TURN[name]) % 2]
                if name == "Vt":
                    dve.wait_ge(v_hi_done, half + 1)
                    dve.tensor_tensor(v_lo[:, b].rearrange("p t d -> p (t d)"), ps[:], v_hi[:, b].rearrange("p t d -> p (t d)").bitcast(F32),
                                      ALU.subtract).then_inc(proj_free, 1)
                    return
                dve.wait_ge(proj_done, e + 1)
                if name == "V":
                    dve.tensor_copy(vT[:], ps[:]).then_inc(proj_free, 1)
                    return
                i = (b + ROPE_NO[name]) % 2
                wait(dve, rope_split, 5 * half + ROPE_NO[name] - 1)
                dve.tensor_tensor(rope_a[:, i], ps[:], rope_cos[:], ALU.mult)
                dve.tensor_tensor(rope_b[0:64, i], ps[64:P], rope_sin[64:P], ALU.mult)
                dve.tensor_tensor(rope_b[64:P, i], ps[0:64], rope_sin[0:64], ALU.mult).then_inc(proj_free, 1)

            def mask(slot, qb):
                i = qb % 2
                c = slice(P, 2 * P) if qb == 0 else slice(0, 2 * P)
                dve.wait_ge(scores0, slot + 1)
                dve.sem_inc(spare, 1)
                for h in range(GQ):
                    ps = bank[h // 2][:, (h % 2) * 2 * P:(h % 2 + 1) * 2 * P]
                    e = dve.tensor_tensor_reduce(probs[:, i, h, c], ps[:, c], window[:, c], float(HD) ** -0.5, -3e38, ALU.add, ALU.max,
                                                 rmax[:, i, h:h + 1])
                e.then_inc(rowmax0, 1)
                dve.wait_ge(rowmax0, slot + 1)
                dve.tensor_scalar(nmax[:, i], rmax[:, i], -1.0, None, ALU.mult).then_inc(masked0, 1)

            def normalise(slot, qb):
                i = qb % 2
                c = slice(P, 2 * P) if qb == 0 else slice(0, 2 * P)
                dve.wait_ge(exp0, slot + 1)
                dve.reciprocal(rden[:, i], den[:, i]).then_inc(rden0, 1)
                dve.wait_ge(rden0, slot + 1)
                for h in range(GQ):
                    e = dve.tensor_scalar(probs[:, i, h, c], probs[:, i, h, c], rden[:, i, h:h + 1], None, ALU.mult)
                e.then_inc(probs0, 1)

            def weights_low(slot, qb):
                dve.wait_ge(pT_hi_done, slot + 1)
                for kb in range(1 if qb == 0 else 0, 2):
                    e = dve.tensor_tensor(pT_lo[:, kb], bank[2 + kb][:], pT_hi[:, kb].bitcast(F32), ALU.subtract)
                e.then_inc(pT_split, 1)

            def out_low(slot):
                dve.wait_ge(oT_hi_done, slot + 1)
                dve.tensor_tensor(oT_lo[:].rearrange("p h t -> p (h t)"), bank[4][:], oT_hi[:].rearrange("p h t -> p (h t)").bitcast(F32),
                                  ALU.subtract).then_inc(oT_split, 1)

            def gate_attention(slot, b):
                dve.wait_ge(wo_mm, slot + 1)
                wait(dve, attn0_added, slot)
                dve.tensor_tensor(gated[:], bank[5][:], gate[:, 0, b], ALU.mult).then_inc(wo_gated, 1)

            def kv_head(n, last):
                for b in range(B):
                    half = 2 * n + b
                    more = not (last and b == 1)
                    for qb in range(TB):
                        slot = 4 * half + qb
                        end = b == 1 and qb == TB - 1
                        if b == 0 and qb == 0:
                            split_wo(n)
                        for name in SLOT_PROJ[qb] if more else []:
                            evacuate(half + 1, name, 1 - b)
                        weights_low(slot, qb)
                        if end:
                            gate_attention(slot - 1, b)
                            out_low(slot)
                        if not (last and end):
                            mask(slot + 1, (qb + 1) % TB)
                        if not end and not (b == 0 and qb == 0):
                            gate_attention(slot - 1, b if qb else 0)
                        if not (last and end):
                            normalise(slot + 1, (qb + 1) % TB)
                        if not end:
                            out_low(slot)
                        else:
                            gate_attention(slot, b)
                        if b == 0 and qb in (1, 2, 3) and not last:
                            split_weights(n + 1, ((0, 1), (2, 3), (4, 5))[qb - 1])

            mod_cols(0, 0)
            split_weights(0, range(6))
            norm(0)
            mod_gate(0, 0)
            mod_cols(0, 1)
            mod_gate(0, 1)
            if upto >= 2:
                dve.wait_ge(consts_loaded, 64)
                for name in TURN:
                    evacuate(0, name, 0)
                mask(0, 0)
                normalise(0, 0)
                dve.wait_ge(gate_loaded, 32)
                kv_head(0, False)
                with dve.Fori(1, HKV - 1) as n:
                    kv_head(n, False)
                kv_head(HKV - 1, True)

            if upto >= 3:
                norm(1)
                dve.wait_ge(f_loaded, 16 * 10)
                dve.tensor_tensor(fcw[:], fco[:, 0:1], fco[:, 1:2], ALU.mult).then_inc(f_cw, 1)
                dve.wait_ge(f_er_mm, 1)
                dve.tensor_copy(fer[:], bank[7][:, 0:2]).then_inc(f_er, 1)
                dve.wait_ge(f_er, 1)
                for t in range(2):
                    dve.tensor_scalar(fa_s[:, t], fa[:, t], fer[:, t:t + 1], None, ALU.mult).then_inc(f_as, 1)
                for k in range(KT):
                    dve.wait_ge(f_mg, k + 1)
                    dve.wait_ge(f_trs, 2 + k + 1)
                    dve.tensor_tensor(fwT[:, k], bank[6 + k % 2][:], fwT[:, k], ALU.add).then_inc(f_sum, 1)
                for k in range(KT):
                    dve.wait_ge(f_hi, k + 1)
                    dve.tensor_tensor(fw_lo[:, k], fwT[:, k], fw_hi[:, k].bitcast(F32), ALU.subtract).then_inc(f_split, 1)
                for t in range(NT):
                    dve.wait_ge(f_mm, t + 1)
                    dve.tensor_tensor(fu[:, t % 2], bank[t % 4][:], fbias[:], ALU.add).then_inc(f_bias, 1)
                    dve.wait_ge(f_bias, t + 1)
                    wait(dve, f_added, t - 1)
                    dve.tensor_tensor(fg[:, t % 2], fu[:, t % 2], gate[:, 1, t // TB], ALU.mult).then_inc(f_gated, 1)
                mod_gate(1, 0)
                mod_gate(1, 1)
                mod_cols(1, 0)
                mod_cols(1, 1)

            if upto >= 4:
                norm(2)
                dve.wait_ge(pre_loaded, 16 * 7)
                for src, hi, lo in ((dn, dn_hi, dn_lo), (kr, kr_hi, kr_lo)):
                    dve.tensor_copy(hi[:], src[:]).then_inc(pre_hi, 1)
                dve.wait_ge(pre_hi, 2)
                for src, hi, lo in ((dn, dn_hi, dn_lo), (kr, kr_hi, kr_lo)):
                    dve.tensor_tensor(lo[:], src[:], hi[:].bitcast(F32), ALU.subtract).then_inc(pre_split, 1)

                def split_rope_weights(p, par, use):
                    if exists(p, PAIRS):
                        dve.wait_ge(wr_loaded[par], 16 * use + 16)
                        wait(dve, qr_mm, 2 * p - 2)
                        dve.tensor_copy(wr_hi[:, par], wst[:, par]).then_inc(wr_hi_done, 1)

                split_rope_weights(0, 0, 0)
                dve.wait_ge(zeroed, 7)
                for b in range(B):
                    dve.wait_ge(kr_hi_done, b + 1)
                    dve.tensor_tensor(k2[0:ROPE, b, 0], bank[2 + b][0:ROPE], k1[0:ROPE, b].bitcast(F32), ALU.subtract)
                    dve.tensor_tensor(k2[ROPE:P, b, 1], bank[2 + b][ROPE:P], k1[ROPE:P, b].bitcast(F32), ALU.subtract).then_inc(kr_split, 1)
                n = 0
                for b in range(B):
                    for m in range(KT):
                        for w in range(2):
                            n += 1
                            dve.wait_ge(c_hi_done, n)
                            dve.tensor_tensor(c_lo[:, (n - 1) % 2], bank[4 + (n - 1) % 2][:], c_hi[:, (n - 1) % 2].bitcast(F32),
                                              ALU.subtract).then_inc(c_split, 1)
                dve.wait_ge(vc_ready, NT)

                def q_low(z, k):
                    if exists(z, UNITS):
                        dve.wait_ge(q1_hi, z + 1)
                        dve.tensor_tensor(q1[ROPE:P, k % 4, 0], bank[6][0:ROPE], q1[0:ROPE, k % 4, 0].bitcast(F32), ALU.subtract)
                        dve.tensor_tensor(q1[0:ROPE, k % 4, 1], bank[6][ROPE:P], q1[ROPE:P, k % 4, 1].bitcast(F32), ALU.subtract)\
                           .then_inc(q1_split, 1)

                def maxima(w, k, use):
                    if exists(w, UNITS):
                        wait(dve, m_loaded[k % 2], 32 * use)
                        for i in range(8):
                            dve.wait_ge(max_mm, 8 * w + i + 1)
                            dve.tensor_reduce(mcol[:, k % 2, i % 4, i // 4:i // 4 + 1], bank[4 + i % 2][:], AX.X, ALU.max, negate=True)\
                               .then_inc(max_done, 1)
                        dve.wait_ge(max_done, 8 * w + 8)
                        dve.transpose(mrow[:, k % 2].rearrange("p (r i) -> p i r", i=4), mcol[:, k % 2].bitcast(F32)).then_inc(m_turned, 1)

                def values(v, k, pair):
                    if exists(v, UNITS):
                        wait(dve, pv1, 2 * v - 1)
                        dve.tensor_copy(vp[:, k % 2, :, :, 0:HD1],
                                        vc[:, TB * (k % 2):TB * (k % 2) + TB, bass.ds(pair * 8, 8)]
                                        .rearrange("p t (h d) -> p t h d", h=2)).then_inc(vp_ready, 1)

                def period(u, k, pair, quad):
                    q_low(u + 2, k + 2)
                    if k % 2 == 0:
                        split_rope_weights(pair(4), (k // 2) % 2, quad(4))
                    values(u + 1, k + 1, pair(1))
                    maxima(u + 2, k + 2, pair(2))

                for u in range(-3, 6):
                    period(u, u % 4, lambda n, u=u: (u + n) // 2, lambda n, u=u: (u + n) // 4)
                with dve.Fori(1, UNITS // 4 - 2) as g:
                    for k in range(2, 6):
                        period(4 * g + k, k, lambda n, k=k: 2 * g + (k + n) // 2, lambda n, k=k: g + (k + n) // 4)
                for u in range(UNITS - 6, UNITS):
                    period(u, u % 4, lambda n, u=u: (u + n) // 2, lambda n, u=u: (u + n) // 4)

            if upto >= 5:
                for k in range(KT):
                    dve.wait_ge(wo1_hi_done, k + 1)
                    dve.tensor_tensor(wo1_lo[:, k], wo1[:, k], wo1_hi[:, k].bitcast(F32), ALU.subtract).then_inc(wo1_split, 1)
                for n in range(B * KT):
                    b, m, i = n // KT, n % KT, n % 2
                    dve.wait_ge(num_loaded[i], 64 * (n // 2 + 1))
                    wait(dve, oo_split, n - 1)
                    dve.tensor_tensor(dsum[:, i], dnm[:, i, 0], dnm[:, i, 1], ALU.add).then_inc(o_step, 1)
                    dve.tensor_tensor(osum[:, i], num[:, i, 0], num[:, i, 1], ALU.add).then_inc(o_step, 1)
                    dve.wait_ge(o_step, 4 * n + 2)
                    dve.reciprocal(dnm[:, i, 0], dsum[:, i]).then_inc(o_step, 1)
                    dve.wait_ge(o_step, 4 * n + 3)
                    dve.tensor_tensor(osum[:, i], osum[:, i], dnm[:, i, 0], ALU.mult).then_inc(o_step, 1)
                    dve.wait_ge(oo_hi_done, n + 1)
                    at = slice(b * S, (b + 1) * S)
                    dve.tensor_tensor(oo_lo[:, m, at], osum[:, i], oo_hi[:, m, at].bitcast(F32), ALU.subtract).then_inc(oo_split, 1)
                dve.wait_ge(gate_loaded, 64)
                for t in range(NT):
                    dve.wait_ge(wo1_mm, t + 1)
                    wait(dve, attn1_added, t - 1)
                    dve.tensor_tensor(og[:, t % 2], bank[t % 4][:], gate[:, 0, t // TB], ALU.mult).then_inc(wo1_gated, 1)

            if upto >= 6:
                norm(3)
                dve.memset(rwT_hi[:].bitcast(F32), 0.0)
                dve.memset(rwT_lo[:].bitcast(F32), 0.0).then_inc(g_const, 1)
                dve.wait_ge(g_loaded, 16 * 12)
                dve.tensor_copy(emap[0:NR], emap_i[0:NR]).then_inc(g_const, 1)
                dve.wait_ge(g_const, 2)
                dve.tensor_scalar(ehot[0:NR], ecol[0:NR], emap[0:NR, 0:1], None, ALU.is_equal).then_inc(g_const, 1)
                for i, (hi, lo) in enumerate([*((bwT_hi[:, k], bwT_lo[:, k]) for k in range(KT)),
                                              (laT_hi[:].rearrange("p k n -> p (k n)"), laT_lo[:].rearrange("p k n -> p (k n)")),
                                              (rwT_hi[:, :, 0:NR], rwT_lo[:, :, 0:NR]), (lbT_hi[:], lbT_lo[:])]):
                    dve.wait_ge(g_hi, i + 1)
                    src = bank[i][:] if i != 5 else bank[i][:].rearrange("p (k n) -> p k n", k=KT)[:, :, 0:NR]
                    dve.tensor_tensor(lo, src, hi.bitcast(F32), ALU.subtract).then_inc(g_lo, 1)
                step = [0]

                def chain(ins):
                    step[0] += 1
                    ins.then_inc(r_step, 1)
                    dve.wait_ge(r_step, step[0])

                over = lambda v: v.unsqueeze(2).broadcast_to([P, NT, NR])
                dve.wait_ge(r_tr, 1)
                chain(dve.tensor_tensor(lg[:], bank[2][:, 0:NT * 16].rearrange("p (t n) -> p t n", n=16)[:, :, 0:NR],
                                        rbias[:].unsqueeze(1).broadcast_to([P, NT, NR]), ALU.add))
                chain(dve.tensor_reduce(lmax[:], lg[:], AX.X, ALU.max))
                chain(dve.tensor_tensor(lg[:], lg[:], over(lmax[:]), ALU.subtract))
                dve.wait_ge(r_exp, 1)
                chain(dve.tensor_reduce(lsum[:], prob[:], AX.X, ALU.add))
                chain(dve.reciprocal(lrec[:], lsum[:]))
                chain(dve.tensor_tensor(prob[:], prob[:], over(lrec[:]), ALU.mult))
                for t in range(NT):
                    p_n = prob[:, t].unsqueeze(2).broadcast_to([P, NR, NR])
                    p_m = prob[:, t].unsqueeze(1).broadcast_to([P, NR, NR])
                    dve.tensor_tensor(cmpg[:, t], p_m, p_n, ALU.is_gt)
                    e = dve.tensor_tensor(cmpe[:, t], p_m, p_n, ALU.is_equal)
                chain(e)
                for t in range(NT):
                    e = dve.tensor_tensor(cmpe[:, t], cmpe[:, t], before[:], ALU.mult)
                chain(e)
                chain(dve.tensor_tensor(cmpg[:].rearrange("p t n m -> p (t n m)"), cmpg[:].rearrange("p t n m -> p (t n m)"),
                                        cmpe[:].rearrange("p t n m -> p (t n m)"), ALU.add))
                chain(dve.tensor_reduce(rank[:].rearrange("p t n -> p (t n)"), cmpg[:].rearrange("p t n m -> p (t n) m"), AX.X, ALU.add))
                dve.memset(kept[:], 0.0)
                chain(dve.tensor_scalar(rank[:], rank[:], float(E1), None, ALU.is_lt))
                dve.tensor_tensor(kept[:, :, 0:NR], rank[:], prob[:], ALU.mult).then_inc(r_kept, 1)
                for b in range(B):
                    dve.wait_ge(r_wexp, b + 1)
                    dve.wait_ge(r_hmm, b + 1)
                    dve.tensor_tensor(lh[:, b * S:(b + 1) * S], bank[6 + b][:], wexp[:, b * S:(b + 1) * S], ALU.mult).then_inc(r_hfull, 1)
                for b in range(B):
                    dve.wait_ge(r_hhi, b + 1)
                    dve.tensor_tensor(lh_lo[:, b * S:(b + 1) * S], lh[:, b * S:(b + 1) * S], lh_hi[:, b * S:(b + 1) * S].bitcast(F32),
                                      ALU.subtract).then_inc(r_hlo, 1)
                for t in range(NT):
                    dve.wait_ge(g_mm, t + 1)
                    dve.tensor_tensor(gu[:, t % 2], bank[t % 4][:], bbias[:], ALU.add).then_inc(g_bias, 1)
                    dve.wait_ge(g_bias, t + 1)
                    wait(dve, g_added, t - 1)
                    dve.tensor_tensor(gg[:, t % 2], gu[:, t % 2], gate[:, 1, t // TB], ALU.mult).then_inc(g_gated, 1)

        @block.tensor
        def _(pe):
            def mm3(ps, pairs, inc=None):
                n = len(pairs)
                for i, (lh_, ll, rh, rl) in enumerate(pairs):
                    pe.matmul(ps, lh_, rh, start=(i == 0), stop=False)
                    pe.matmul(ps, lh_, rl, start=False, stop=False)
                    e = pe.matmul(ps, ll, rh, start=False, stop=(i == n - 1))
                if inc is not None:
                    e.then_inc(inc, 1)

            def mod(l, chunks):
                for c in chunks:
                    i = 6 * l + c
                    pe.wait_ge(wm_loaded[i % 3], 16 * (i // 3 + 1))
                    wait(pe, mod_row, i - 3)
                    for k in range(KT):
                        e = pe.matmul(bank[c % 4][0:B, :], silu[:, l, :, k], WM[l][:, i % 3, k], start=(k == 0), stop=(k == KT - 1))
                    e.then_inc(mod_mm, 1)

            def mod_cols(l, half):
                i = 2 * l + half
                pe.wait_ge(mod_row, 6 * l + 3 * half + 2)
                wait(pe, col_ready, i)
                for v in range(2):
                    for k in range(KT):
                        at = 8 * v + 2 * k
                        e = pe.transpose(bank[4][:, at:at + 2], MODROW[l][:, 3 * half + v, k * P:(k + 1) * P], ident[0:B, 0:B])
                e.then_inc(col_mm, 1)

            def norm(ph):
                xn = NORM[ph][0]
                for t in range(NT):
                    b = t // TB
                    pe.wait_ge(ln_norm, NT * ph + t + 1)
                    for k in range(KT):
                        e = pe.transpose(bank[KT * b + k][:, (t % TB) * P:(t % TB + 1) * P], xn[:, t, k * P:(k + 1) * P], ident[:])
                    e.then_inc(ln_trans, 1)

            pe.wait_ge(consts_loaded, 64)
            pe.wait_ge(silu_step, 3)
            mod(0, (0, 1))
            mod_cols(0, 0)
            pe.wait_ge(col_ready, 1)
            norm(0)
            pe.wait_ge(ln_lo, NT)
            mod(0, (2, 3, 4, 5))
            mod_cols(0, 1)

            def project(half, name, b, n):
                e = TURNS * half + TURN[name]
                ps = bank[6 + (b + TURN[name]) % 2]
                wait(pe, proj_free, e - 1)
                if name == "Vt":
                    pe.wait_ge(proj_free, TURNS * half + TURN["V"] + 1)
                    for t in range(TB):
                        ins = pe.transpose(ps[:, t * P:(t + 1) * P], vT[:, t * P:(t + 1) * P], ident[:])
                    ins.then_inc(proj_done, 1)
                    return
                m = W_TILE[name]
                pe.wait_ge(w_split, 6 * n + m + 1)
                at = slice(b * S, (b + 1) * S)
                mm3(ps[:], [(w_hi[:, m, k], w_lo[:, m, k], hT_hi[:, k, at], hT_lo[:, k, at]) for k in range(KT)], proj_done)

            def scores(slot, half, b, qb):
                if qb == 0:
                    pe.wait_ge(rope_split, 5 * half + 5)
                wait(pe, masked0, slot)
                c = slice(P, 2 * P) if qb == 0 else slice(0, 2 * P)
                keys = slice(0, P) if qb == 0 else slice((qb - 1) * P, (qb + 1) * P)
                for h in range(GQ):
                    q = slice(qb * P, (qb + 1) * P)
                    ps = bank[h // 2][:, (h % 2) * 2 * P:(h % 2 + 1) * 2 * P]
                    mm3(ps[:, c], [(qT_hi[:, b, h, q], qT_lo[:, b, h, q], kT_hi[:, b, keys], kT_lo[:, b, keys])],
                        scores0 if h == GQ - 1 else None)

            def transposes(slot, qb):
                pe.wait_ge(probs0, slot + 1)
                wait(pe, pT_split, slot)
                for kb in range(1 if qb == 0 else 0, 2):
                    for h in range(GQ):
                        e = pe.transpose(bank[2 + kb][:, h * P:(h + 1) * P], probs[:, qb % 2, h, kb * P:(kb + 1) * P], ident[:])
                e.then_inc(trans0, 1)

            def sum_values(slot, half, b, qb):
                pe.wait_ge(pT_split, slot + 1)
                if qb == 0:
                    pe.wait_ge(proj_free, TURNS * half + TURN["Vt"] + 1)
                wait(pe, oT_split, slot)
                mm3(bank[4][:], [(v_hi[:, b, qb - 1 + kb], v_lo[:, b, qb - 1 + kb], pT_hi[:, kb], pT_lo[:, kb])
                                 for kb in range(1 if qb == 0 else 0, 2)], pv0)

            def project_out(slot, n):
                pe.wait_ge(oT_split, slot + 1)
                pe.wait_ge(wo_split, n + 1)
                wait(pe, wo_gated, slot)
                mm3(bank[5][:], [(oT_hi[:, h], oT_lo[:, h], wo_hi[:, h], wo_lo[:, h]) for h in range(GQ)], wo_mm)

            def kv_head(n, last):
                for b in range(B):
                    half = 2 * n + b
                    more = not (last and b == 1)
                    for qb in range(TB):
                        slot = 4 * half + qb
                        end = b == 1 and qb == TB - 1
                        nb, nqb = (1 - b, 0) if qb == TB - 1 else (b, qb + 1)
                        for name in SLOT_PROJ[qb] if more else []:
                            project(half + 1, name, 1 - b, n + b)
                        transposes(slot, qb)
                        if end:
                            project_out(slot - 1, n)
                            sum_values(slot, half, b, qb)
                        if not (last and end):
                            scores(slot + 1, half + (1 if qb == TB - 1 else 0), nb, nqb)
                        if not end:
                            if not (b == 0 and qb == 0):
                                project_out(slot - 1, n)
                            sum_values(slot, half, b, qb)
                        else:
                            project_out(slot, n)

            if upto >= 2:
                pe.wait_ge(col_ready, 2)
                for name in TURN:
                    project(0, name, 0, 0)
                pe.wait_ge(mod_row, 6)
                scores(0, 0, 0, 0)
                kv_head(0, False)
                with pe.Fori(1, HKV - 1) as n:
                    kv_head(n, False)
                kv_head(HKV - 1, True)

            if upto >= 3:
                norm(1)
                pe.wait_ge(ln_lo, 2 * NT)
                pe.wait_ge(f_loaded, 16 * 10)
                for t in range(2):
                    for k in range(KT):
                        e = pe.transpose(bank[t][:, k * P:(k + 1) * P], fbf[:, k, t * P:(t + 1) * P], ident[:])
                    e.then_inc(f_tr, 1)
                for k in range(KT):
                    for o in range(KT):
                        e = pe.transpose(bank[2 + k][:, o * P:(o + 1) * P], fw[:, o, k * P:(k + 1) * P], ident[:])
                    e.then_inc(f_tr, 1)
                pe.wait_ge(f_cw, 1)
                for t in range(2):
                    e = pe.matmul(bank[7][:, t:t + 1], expand[:, t * P:(t + 1) * P], fcw[:], start=True, stop=True)
                e.then_inc(f_er_mm, 1)
                pe.wait_ge(f_as, 2)
                pe.wait_ge(f_trs, 2)
                for k in range(KT):
                    wait(pe, f_sum, k - 1)
                    for t in range(2):
                        e = pe.matmul(bank[6 + k % 2][:], fa_s[:, t, k * P:(k + 1) * P], fbfT[:, t], start=(t == 0), stop=(t == 1))
                    e.then_inc(f_mg, 1)
                pe.wait_ge(f_split, KT)
                for t in range(NT):
                    wait(pe, f_bias, t - 3)
                    at = slice(t * P, (t + 1) * P)
                    mm3(bank[t % 4][:], [(hT_hi[:, k, at], hT_lo[:, k, at], fw_hi[:, k], fw_lo[:, k]) for k in range(KT)], f_mm)
                pe.wait_ge(f_bias, NT)
                mod(1, range(6))
                mod_cols(1, 0)
                mod_cols(1, 1)
                pe.wait_ge(col_ready, 4)

            if upto >= 4:
                norm(2)
                pe.wait_ge(ln_lo, 3 * NT)
                pe.wait_ge(pre_split, 2)
                for b in range(B):
                    at = slice(b * S, (b + 1) * S)
                    mm3(bank[b][:], [(dn_hi[:, k], dn_lo[:, k], hT_hi[:, k, at], hT_lo[:, k, at]) for k in range(KT)], lat_mm)
                for b in range(B):
                    at = slice(b * S, (b + 1) * S)
                    mm3(bank[2 + b][:], [(kr_hi[:, k], kr_lo[:, k], hT_hi[:, k, at], hT_lo[:, k, at]) for k in range(KT)], kr_mm)
                n = 0
                for b in range(B):
                    pe.wait_ge(lat_ready, b + 1)
                    for m in range(KT):
                        for w in range(2):
                            n += 1
                            r = slice(LAT * w, LAT * w + LAT)
                            wait(pe, c_split, n - 2)
                            pe.matmul(bank[4 + (n - 1) % 2][:], up[r, m * P:(m + 1) * P], lat[r, b * S:(b + 1) * S],
                                      start=True, stop=True).then_inc(c_mm, 1)
                for t in range(NT):
                    wait(pe, vc_ready, t - 1)
                    pe.matmul(bank[6 + t % 2][:], lat[LAT:P, t * P:(t + 1) * P], vup[LAT:P], start=True, stop=True).then_inc(vc_mm, 1)
                pe.wait_ge(vc_ready, NT)
                pe.wait_ge(c_split, 2 * KT * B)
                pe.wait_ge(kr_split, B)

                def rope_queries(z, k, pair, ks, first, last):
                    if exists(z, UNITS):
                        par, b = pair % 2 if isinstance(pair, int) else None, k % 2
                        par = (k % 4) // 2
                        if first:
                            wait(pe, q1_split, z)
                            pe.wait_ge(wr_split, pair + 1)
                        at = slice(b * S, (b + 1) * S)
                        for kk in ks:
                            pe.matmul(bank[6][:], wr_hi[:, par, kk], hT_hi[:, kk, at], start=(kk == 0), stop=False)
                            pe.matmul(bank[6][:], wr_hi[:, par, kk], hT_lo[:, kk, at], start=False, stop=False)
                            e = pe.matmul(bank[6][:], wr_lo[:, par, kk], hT_hi[:, kk, at], start=False, stop=(kk == KT - 1))
                        if last:
                            e.then_inc(qr_mm, 1)

                def max_scores(w, k, i, use):
                    if exists(w, UNITS):
                        h, b = i // 4, k % 2
                        if i == 0:
                            pe.wait_ge(q2_hi, w + 1)
                            pe.wait_ge(mc_loaded[b], 64 * use + 64)
                        wait(pe, max_done, 8 * w + i - 1)
                        pe.matmul(bank[4 + i % 2][:], q2[:, k % 4, h, i % 4:S:4], km[:, b, h], start=True, stop=True).then_inc(max_mm, 1)

                def scores1_slot(u, k, s, use):
                    if exists(u, UNITS):
                        h, kb = SLOTS[s]
                        if s == 0:
                            pe.wait_ge(q1_split, u + 1)
                            pe.wait_ge(m_loaded[k % 2], 32 * use + 32)
                            pe.wait_ge(k2c_loaded[k % 2], 32 * use + 32)
                        pe.wait_ge(exp1, 8 * u + s + 1)
                        t = slice(kb * P, (kb + 1) * P)
                        pe.matmul(bank[s % 4][:], k1[:, k % 2, t], q1[:, k % 4, h], start=True, stop=False)
                        pe.matmul(bank[s % 4][:], k2[:, k % 2, h, t], q2[:, k % 4, h], start=False, stop=True).then_inc(scores1, 1)

                def sum_slots(u, k, c):
                    if exists(u, UNITS):
                        pe.wait_ge(exp1, 8 * u + 4 * c + 8)
                        if c == 0:
                            pe.wait_ge(vp_ready, u + 1)
                            wait(pe, o_copied, u)
                        for s in range(4 * c, 4 * c + 4):
                            h, kb = SLOTS[s]
                            j = 2 * h + kb % 2
                            e = pe.matmul(bank[7][32 * j:32 * j + 32, :], vp[:, k % 2, kb, h], pT[:, s], start=(c == 0), stop=(c == 1))
                        e.then_inc(pv1, 1)

                pe.wait_ge(ones_set, 64)
                pe.sem_inc(pv1, 1)

                def period(u, k, pair):
                    scores1_slot(u, k, 0, pair(0))
                    scores1_slot(u, k, 1, pair(0))
                    sum_slots(u - 1, k - 1, 1)
                    scores1_slot(u, k, 2, pair(0))
                    max_scores(u + 2, k + 2, 0, pair(2))
                    scores1_slot(u, k, 3, pair(0))
                    max_scores(u + 2, k + 2, 1, pair(2))
                    scores1_slot(u, k, 4, pair(0))
                    rope_queries(u + 3, k + 3, pair(3), [0], True, False)
                    max_scores(u + 2, k + 2, 2, pair(2))
                    scores1_slot(u, k, 5, pair(0))
                    rope_queries(u + 3, k + 3, pair(3), [1], False, False)
                    max_scores(u + 2, k + 2, 3, pair(2))
                    sum_slots(u, k, 0)
                    max_scores(u + 2, k + 2, 4, pair(2))
                    scores1_slot(u, k, 6, pair(0))
                    rope_queries(u + 3, k + 3, pair(3), [2], False, False)
                    max_scores(u + 2, k + 2, 5, pair(2))
                    scores1_slot(u, k, 7, pair(0))
                    max_scores(u + 2, k + 2, 6, pair(2))
                    rope_queries(u + 3, k + 3, pair(3), [3], False, True)
                    max_scores(u + 2, k + 2, 7, pair(2))

                for u in range(-3, 6):
                    period(u, u % 4, lambda n, u=u: (u + n) // 2)
                with pe.Fori(1, UNITS // 4 - 2) as g:
                    for k in range(2, 6):
                        period(4 * g + k, k, lambda n, k=k: 2 * g + (k + n) // 2)
                for u in range(UNITS - 6, UNITS + 1):
                    period(u, u % 4, lambda n, u=u: (u + n) // 2)

            if upto >= 5:
                pe.wait_ge(o_copied, UNITS)
                pe.wait_ge(wo1_split, KT)
                pe.wait_ge(oo_split, NT)
                for t in range(NT):
                    wait(pe, wo1_gated, t - 3)
                    at = slice(t * P, (t + 1) * P)
                    mm3(bank[t % 4][:], [(oo_hi[:, k, at], oo_lo[:, k, at], wo1_hi[:, k], wo1_lo[:, k]) for k in range(KT)], wo1_mm)

            if upto >= 6:
                norm(3)
                pe.wait_ge(ln_lo, 4 * NT)
                pe.wait_ge(g_loaded, 16 * 12)
                for k in range(KT):
                    for o in range(KT):
                        e = pe.transpose(bank[k][:, o * P:(o + 1) * P], bw[:, o, k * P:(k + 1) * P], ident[:])
                    e.then_inc(g_tr, 1)
                for k in range(KT):
                    e = pe.transpose(bank[4][:, k * P:(k + 1) * P], la[:, k * P:(k + 1) * P], ident[:])
                e.then_inc(g_tr, 1)
                for k in range(KT):
                    e = pe.transpose(bank[5][:, k * P:k * P + NR], rw[0:NR, k * P:(k + 1) * P], ident[0:NR, 0:NR])
                e.then_inc(g_tr, 1)
                for k in range(KT):
                    e = pe.transpose(bank[6][:, k * P:(k + 1) * P], lb[:, k].rearrange("p e r -> p (e r)"), ident[:])
                e.then_inc(g_tr, 1)
                pe.wait_ge(g_lo, 7)
                for b in range(B):
                    at = slice(b * S, (b + 1) * S)
                    mm3(bank[b][:], [(rwT_hi[:, k], rwT_lo[:, k], hT_hi[:, k, at], hT_lo[:, k, at]) for k in range(KT)], r_mm)
                for b in range(B):
                    at = slice(b * S, (b + 1) * S)
                    mm3(bank[6 + b][:], [(laT_hi[:, k], laT_lo[:, k], hT_hi[:, k, at], hT_lo[:, k, at]) for k in range(KT)], r_hmm)
                pe.wait_ge(r_copied, B)
                for t in range(NT):
                    e = pe.transpose(bank[2][:, 16 * t:16 * t + NR], lgT[0:NR, t * P:(t + 1) * P], ident[0:NR, 0:NR])
                e.then_inc(r_tr, 1)
                pe.wait_ge(r_kept, 1)
                for b in range(B):
                    for t in range(TB):
                        e = pe.transpose(bank[2 + b][0:16, t * P:(t + 1) * P], kept[:, TB * b + t], ident[:])
                    e.then_inc(r_ktr, 1)
                pe.wait_ge(g_const, 3)
                for b in range(B):
                    pe.wait_ge(r_ktc, b + 1)
                    pe.matmul(bank[4 + b][:], ehot[0:NR], keptT[0:NR, b * S:(b + 1) * S], start=True, stop=True).then_inc(r_wmm, 1)
                pe.wait_ge(r_hlo, B)
                for t in range(NT):
                    wait(pe, g_bias, t - 3)
                    at = slice(t * P, (t + 1) * P)
                    mm3(bank[t % 4][:], [*((hT_hi[:, k, at], hT_lo[:, k, at], bwT_hi[:, k], bwT_lo[:, k]) for k in range(KT)),
                                         (lh_hi[:, at], lh_lo[:, at], lbT_hi[:], lbT_lo[:])], g_mm)


def shape_constants():
    import numpy as np

    half = HD // 2
    inv_freq = np.float32(10000.0) ** (-np.arange(half, dtype=np.float32) / np.float32(half))
    ang = (np.arange(S, dtype=np.float32)[:, None] * inv_freq[None, :]).T.astype(np.float32)
    cos, sin = np.cos(ang), np.sin(ang)
    i, j = np.arange(P)[:, None], np.arange(P)[None, :]
    n = np.arange(NR)
    return {
        "identity": np.eye(P, dtype=np.float32),
        "rope_cos": np.concatenate([cos, cos]).astype(np.float32),
        "rope_sin": np.concatenate([sin, -sin]).astype(np.float32),
        "window_mask": np.where(np.concatenate([j > i, j <= i], axis=1), 0.0, MASKED).astype(np.float32),
        "lora_expand": (np.arange(16)[:, None] == np.arange(ER0)[None, :] // 16).astype(np.float32),
        "expert_of_column": np.broadcast_to(np.arange(P) // R1, (16, P)).astype(np.float32),
        "entry_before": (n[None, :] < n[:, None]).astype(np.float32),
    }


_INS = ["L0_attn_x", "L0_attn_wq", "L0_attn_wk", "L0_attn_wv", "L0_attn_wo", "L0_ffn_W", "L0_ffn_bias", "L0_ffn_A", "L0_ffn_Bf",
        "L0_ffn_coeffs", "L0_ffn_scales", "L0_c", "L0_wmod", "L1_attn_Wq_down", "L1_attn_Wq_up", "L1_attn_Wq_rope",
        "L1_attn_Wkv_down", "L1_attn_Wk_up", "L1_attn_Wv_up", "L1_attn_Wk_rope", "L1_attn_Wo", "L1_ffn_base_W", "L1_ffn_base_b",
        "L1_ffn_router_W", "L1_ffn_router_b", "L1_ffn_A", "L1_ffn_B", "L1_ffn_expert_map", "L1_c", "L1_wmod"]


def kernel(**inputs):
    import numpy as np
    import concourse.bacc as bacc
    from concourse.bass_utils import run_bass_kernel_spmd

    nc = bacc.Bacc("TRN2", target_bir_lowering=False, num_devices=1)
    arrays = {name: np.ascontiguousarray(inputs[name]) for name in _INS}
    arrays.update(shape_constants())
    aps = {name: nc.dram_tensor(f"in_{name}", v.shape, mybir.dt.from_np(v.dtype), kind="ExternalInput").ap() for name, v in arrays.items()}
    out = nc.dram_tensor("out_x", (B, S, D), F32, kind="ExternalOutput").ap()
    adaln_two_layers(nc, aps, out)
    r = run_bass_kernel_spmd(nc, [{f"in_{name}": v for name, v in arrays.items()}], core_ids=[0])
    return r.results[0]["out_x"]
```

```python
from contextlib import ExitStack

import concourse.bass as bass
from concourse import mybir

F32 = mybir.dt.float32
F32R = mybir.dt.float32r
I32 = mybir.dt.int32
ALU = mybir.AluOpType
ACT = mybir.ActivationFunctionType
AX = mybir.AxisListType

P = 128
B, S, D = 2, 512, 512
KT = D // P
TB = S // P
NT = B * TB
EPS = 1e-5

HQ, HKV, HD = 32, 8, 128
GQ = HQ // HKV
NPROJ = GQ + 2
TURNS = NPROJ + 1
TURN = {"K": 0, "V": 1, "Q0": 2, "Q1": 3, "Vt": 4, "Q2": 5, "Q3": 6}
MASKED = -1e30
ER0 = 256

H1, HD1, LAT, ROPE = 128, 4, 64, 64
PAIRS = H1 // 2
UNITS = PAIRS * B
CR = 3 * HD1
SLOTS = [(0, 0), (0, 1), (1, 0), (1, 1), (0, 2), (0, 3), (1, 2), (1, 3)]
E1, R1 = 8, 16
F_PAD = 256
W_PAD = 720
NR = 2 * E1 - 1
SCALING = 2.0


def exists(v, n):
    return not isinstance(v, int) or 0 <= v < n


def wait(eng, sem, v):
    if not isinstance(v, int) or v > 0:
        eng.wait_ge(sem, v)


def adaln_two_layers(nc, a, out):
    x_in, out_t = (v.rearrange("b (t p) d -> p (b t) d", p=P) for v in (a["L0_attn_x"], out))
    scratch = lambda name, shape: nc.dram_tensor(name, shape, F32, kind="Internal").ap()
    qc_d = scratch("qc_d", (B, H1, CR, S))
    kc_d = scratch("kc_d", (B, H1, CR, S))
    o_d = scratch("o_d", (B, H1, 2, 8, S))

    ctx = ExitStack()
    with ctx:
        def sbuf_in(stack):
            return lambda name, shape, dt=F32: stack.enter_context(nc.sbuf_tensor(name, shape, dt))

        sb = sbuf_in(ctx)
        sem = lambda name: ctx.enter_context(nc.semaphore(name))
        bank = [ctx.enter_context(nc.psum_tensor(f"bank{i}", [P, 512], F32)) for i in range(8)]

        x = sb("x", [P, NT, D])
        hT_hi = sb("hT_hi", [P, KT, B * S], F32R)
        hT_lo = sb("hT_lo", [P, KT, B * S], F32R)
        ident = sb("ident", [P, P])
        sel = sb("sel", [P, B, P])
        rowsum = sb("rowsum", [P, 32])
        grows0 = sb("grows0", [2 * 32, D])
        cT = sb("cT", [P, 2, B, KT])
        silu_e = sb("silu_e", [P, 2, B, KT])
        silu_d = sb("silu_d", [P, 2, B, KT])
        silu = sb("silu", [P, 2, KT, 32])
        modc = sb("modc", [P, 2, 4, KT, B])
        stats = sb("stats", [P, NT, 6])
        mean_var = sb("mean_var", [P, NT, 2])
        var_eps = sb("var_eps", [P, NT])
        std = sb("std", [P, NT])
        rstd = sb("rstd", [P, NT])

        l0 = ctx.enter_context(ExitStack())
        sb0 = sbuf_in(l0)
        wo_hi = sb0("wo_hi", [P, GQ, D], F32R)
        wo_lo = sb0("wo_lo", [P, GQ, D], F32R)
        rope_cos = sb0("rope_cos", [P, S])
        rope_sin = sb0("rope_sin", [P, S])
        window = sb0("window", [P, 2 * P])
        kT_hi = sb0("kT_hi", [P, B, S], F32R)
        kT_lo = sb0("kT_lo", [P, B, S], F32R)
        v_hi = sb0("v_hi", [P, B, TB, HD], F32R)
        v_lo = sb0("v_lo", [P, B, TB, HD], F32R)
        oT_hi = sb0("oT_hi", [P, GQ, P], F32R)
        oT_lo = sb0("oT_lo", [P, GQ, P], F32R)
        gate_a0 = sb0("gate_a0", [P, B, D])
        vT = sb0("vT", [P, S])
        gated = sb0("gated", [P, D])
        st_kv = sb0("st_kv", [P, 2, KT, HD])
        st_q = sb0("st_q", [P, KT, GQ * HD])
        st_wo = sb0("st_wo", [P, GQ, D])
        w_hi = sb0("w_hi", [P, NPROJ, KT, HD], F32R)
        w_lo = sb0("w_lo", [P, NPROJ, KT, HD], F32R)
        rmax = sb0("rmax", [P, 2, GQ])
        nmax = sb0("nmax", [P, 2, GQ])
        den = sb0("den", [P, 2, GQ])
        rden = sb0("rden", [P, 2, GQ])
        with ExitStack() as pro:
            sbp = sbuf_in(pro)
            xn0 = sbp("xn0", [P, NT, D])
            full0 = sbp("full0", [P, 4, S])
            wm0 = sbp("wm0", [P, 3, KT, D])
            modrow0 = sbp("modrow0", [P, 4, D])
        rope_a = sb0("rope_a", [P, 2, S])
        rope_b = sb0("rope_b", [P, 2, S])
        q0_hi = sb0("q0_hi", [P, GQ, S], F32R)
        q0_lo = sb0("q0_lo", [P, GQ, S], F32R)
        q1_hi_ = sb0("q1_hi_", [P, GQ, S], F32R)
        q1_lo_ = sb0("q1_lo_", [P, GQ, S], F32R)
        probs = sb0("probs", [P, 2, GQ, 2 * P])
        pT_hi = sb0("pT_hi", [P, 2, GQ * P], F32R)
        pT_lo = sb0("pT_lo", [P, 2, GQ * P], F32R)
        qT_hi, qT_lo = (q0_hi, q1_hi_), (q0_lo, q1_lo_)
        l0.close()

        gate = sb("gate", [P, 3, B, D])

        pre = ctx.enter_context(ExitStack())
        sbq = sbuf_in(pre)
        dn = sbq("dn", [P, KT, P])
        kr = sbq("kr", [P, KT, P])
        dn_hi = sbq("dn_hi", [P, KT, P], F32R)
        dn_lo = sbq("dn_lo", [P, KT, P], F32R)
        kr_hi = sbq("kr_hi", [P, KT, P], F32R)
        kr_lo = sbq("kr_lo", [P, KT, P], F32R)
        up = sbq("up", [P, D])
        vup = sbq("vup", [P, D])
        lat = sbq("lat", [P, B * S])
        with ExitStack() as rows1:
            modrow1 = sbuf_in(rows1)("modrow1", [P, 4, D])
        c_hi = sbq("c_hi", [P, 4, S], F32R)
        c_lo = sbq("c_lo", [P, 4, S], F32R)

        f0 = ctx.enter_context(ExitStack())
        sbf = sbuf_in(f0)
        sbf("f_pad", [P, F_PAD])
        fw = sbf("fw", [P, KT, D])
        fbf = sbf("fbf", [P, KT, ER0])
        fa = sbf("fa", [P, 2, D])
        fco = sbf("fco", [16, 2])
        fcw = sbf("fcw", [16, 1])
        fer = sbf("fer", [P, 2])
        expand = sbf("expand", [16, ER0])
        sbf("w_pad", [P, W_PAD])
        wm1 = sbf("wm1", [P, 3, KT, D])
        xn1 = sbf("xn1", [P, NT, D])
        full1 = sbf("full1", [P, 4, S])
        fbias = sbf("fbias", [P, D])
        fa_s = sbf("fa_s", [P, 2, D])
        fbfT = sbf("fbfT", [P, 2, D])
        grows1 = sbf("grows1", [2 * 32, D])
        gsign1 = sbf("gsign1", [2 * 32, D])
        fw_hi = sbf("fw_hi", [P, KT, D], F32R)
        fw_lo = sbf("fw_lo", [P, KT, D], F32R)
        fu = xn1[:, NT - 2:NT]
        fg = sbf("fg", [P, 2, D])
        f0.close()

        l1 = ctx.enter_context(ExitStack())
        sb1 = sbuf_in(l1)
        sb1("l_pad", [P, F_PAD])
        k2 = sb1("k2", [P, B, 2, S], F32R)
        km = sb1("km", [P, B, 2, S], F32R)
        q2 = sb1("q2", [P, 4, 2, S], F32R)
        vp = sb1("vp", [P, 2, TB, 2, 32])
        mcol = sb1("mcol", [P, 2, 4, 32], F32R)
        wst = sb1("wst", [P, 2, KT, P])
        mrow = sb1("mrow", [P, 2, 4 * 32])
        k1 = sb1("k1", [P, B, S], F32R)
        vc = sb1("vc", [P, NT, H1 * HD1])
        q1 = sb1("q1", [P, 4, 2, S], F32R)
        pT = sb1("pT", [P, 8, S])
        wr_hi = sb1("wr_hi", [P, 2, KT, P], F32R)
        wr_lo = sb1("wr_lo", [P, 2, KT, P], F32R)
        ost = sb1("ost", [P, 2, S])
        l1.close()
        pre.close()

        f1 = ctx.enter_context(ExitStack())
        sbg = sbuf_in(f1)
        oo_hi = sbg("oo_hi", [P, KT - 1, B * S], F32R)
        oo_lo = sbg("oo_lo", [P, KT - 1, B * S], F32R)
        num = sbg("num", [P, 2, S])
        dnm = sbg("dnm", [P, 2, S])
        sbg("o_pad", [P, 1024])
        oo3_hi = sbg("oo3_hi", [P, B * S], F32R)
        oo3_lo = sbg("oo3_lo", [P, B * S], F32R)
        num3 = sbg("num3", [P, B, 2, S])
        dnm3 = sbg("dnm3", [P, B, 2, S])
        wo1 = sbg("wo1", [P, KT, D])
        wo1_hi = sbg("wo1_hi", [P, KT, D], F32R)
        wo1_lo = sbg("wo1_lo", [P, KT, D], F32R)
        og = sbg("og", [P, 2, D])
        f1.close()
        g1 = ctx.enter_context(ExitStack())
        sbh = sbuf_in(g1)
        xn2 = sbh("xn2", [P, NT, D])
        full2 = sbh("full2", [P, 4, S])
        lg = sbh("lg", [P, NT, NR])
        lmax = sbh("lmax", [P, NT])
        lsum = sbh("lsum", [P, NT])
        lrec = sbh("lrec", [P, NT])
        prob = sbh("prob", [P, NT, NR])
        cmpg = sbh("cmpg", [P, NT, NR, NR])
        cmpe = sbh("cmpe", [P, NT, NR, NR])
        rank = sbh("rank", [P, NT, NR])
        kept = sbh("kept", [P, NT, 16])
        keptT = sbh("keptT", [16, B * S])
        wexp = sbh("wexp", [P, B * S])
        lh = sbh("lh", [P, B * S])
        lh_hi = sbh("lh_hi", [P, B * S], F32R)
        lh_lo = sbh("lh_lo", [P, B * S], F32R)
        gu = sbh("gu", [P, 2, D])
        gg = sbh("gg", [P, 2, D])
        sbh("g_pad", [P, 5120])
        bw = sbh("bw", [P, KT, D])
        bwT_hi = sbh("bwT_hi", [P, KT, D], F32R)
        bwT_lo = sbh("bwT_lo", [P, KT, D], F32R)
        la = sbh("la", [P, D])
        laT_hi = sbh("laT_hi", [P, KT, P], F32R)
        laT_lo = sbh("laT_lo", [P, KT, P], F32R)
        rw = sbh("rw", [16, D])
        rwT_hi = sbh("rwT_hi", [P, KT, P], F32R)
        rwT_lo = sbh("rwT_lo", [P, KT, P], F32R)
        lb = sbh("lb", [P, KT, E1, R1])
        lbT_hi = sbh("lbT_hi", [P, D], F32R)
        lbT_lo = sbh("lbT_lo", [P, D], F32R)
        bbias = sbh("bbias", [P, D])
        rbias = sbh("rbias", [P, NR])
        emap_i = sbh("emap_i", [16, 1], I32)
        emap = sbh("emap", [16, 1])
        ecol = sbh("ecol", [16, P])
        ehot = sbh("ehot", [16, P])
        before = sbh("before", [P, NR, NR])
        g1.close()

        NORM = [(xn0, full0, 0, 0), (xn1, full1, 0, 2), (xn1, full1, 1, 0), (xn2, full2, 1, 2)]
        WM, MODROW, ROW_SLOT = (wm0, wm1), (modrow0, modrow1), (0, 1, 2, 0, 1, 3)
        GROWS, GSIGN = (grows0, grows1), (gated, gsign1)
        GATE_CHUNKS = (2, 5)

        x_loaded, ident_loaded, cond_loaded, rope_loaded = (sem(n) for n in ("x_loaded", "ident_loaded", "cond_loaded", "rope_loaded"))
        silu_zeroed, silu_exp, silu_step = sem("silu_zeroed"), sem("silu_exp"), sem("silu_step")
        wm_loaded = [sem(f"wm_loaded{i}") for i in range(3)]
        mod_mm, mod_row, mod_used, col_ready = (sem(n) for n in ("mod_mm", "mod_row", "mod_used", "col_ready"))
        gate_step, gate_rows, gate_bc, gate_ready = (sem(n) for n in ("gate_step", "gate_rows", "gate_bc", "gate_ready"))
        ln_stats, ln_aggr, ln_eps, ln_std, ln_rstd, ln_norm, ln_trans, ln_full, ln_hi, ln_lo, ln_lo_odd = (
            sem(f"ln_{n}") for n in ("stats", "aggr", "eps", "std", "rstd", "norm", "trans", "full", "hi", "lo", "lo_odd"))
        kv_loaded, q_loaded, wo_loaded = sem("kv_loaded"), sem("q_loaded"), sem("wo_loaded")
        w_hi_done, w_split, wo_hi_done, wo_split = sem("w_hi_done"), sem("w_split"), sem("wo_hi_done"), sem("wo_split")
        proj_done, proj_free = sem("proj_done"), sem("proj_free")
        rope_sum, rope_hi, rope_split, v_hi_done = sem("rope_sum"), sem("rope_hi"), sem("rope_split"), sem("v_hi_done")
        scores0, rowmax0, masked0, exp0, rden0, probs0 = (sem(n) for n in ("scores0", "rowmax0", "masked0", "exp0", "rden0", "probs0"))
        trans0, pT_hi_done, pT_split, pv0 = sem("trans0"), sem("pT_hi_done"), sem("pT_split"), sem("pv0")
        oT_hi_done, oT_split, wo_mm, wo_gated, attn0_added = (sem(n) for n in ("oT_hi_done", "oT_split", "wo_mm", "wo_gated", "attn0_added"))
        f_loaded, f_cw, f_er_mm, f_er, f_as, fbias_loaded = (sem(n) for n in ("f_loaded", "f_cw", "f_er_mm", "f_er", "f_as", "fbias_loaded"))
        f_tr, f_trs, f_mg, f_hi, f_split = (sem(n) for n in ("f_tr", "f_trs", "f_mg", "f_hi", "f_split"))
        f_mm, f_bias, f_gated, f_added = (sem(n) for n in ("f_mm", "f_bias", "f_gated", "f_added"))
        pre_loaded, pre_hi, pre_split, lat_mm, lat_ready = (sem(n) for n in ("pre_loaded", "pre_hi", "pre_split", "lat_mm", "lat_ready"))
        kr_mm, kr_hi_done, kr_split, zeroed = sem("kr_mm"), sem("kr_hi_done"), sem("kr_split"), sem("zeroed")
        c_mm, c_hi_done, c_split, vc_mm, vc_ready = (sem(n) for n in ("c_mm", "c_hi_done", "c_split", "vc_mm", "vc_ready"))
        c_stored = [sem(f"c_stored{i}") for i in range(4)]
        wr_loaded = [sem(f"wr_loaded{i}") for i in range(2)]
        wr_hi_done, wr_split = sem("wr_hi_done"), sem("wr_split")
        qr_mm, q2_hi, q1_hi, q1_split = sem("qr_mm"), sem("q2_hi"), sem("q1_hi"), sem("q1_split")
        mc_loaded, k2c_loaded, m_loaded = ([sem(f"{n}{i}") for i in range(2)] for n in ("mc_loaded", "k2c_loaded", "m_loaded"))
        ones_set = sem("ones_set")
        max_mm, max_done, m_turned = sem("max_mm"), sem("max_done"), sem("m_turned")
        scores1, exp1, pv1, vp_ready, o_copied = (sem(n) for n in ("scores1", "exp1", "pv1", "vp_ready", "o_copied"))
        o_stored = [sem(f"o_stored{i}") for i in range(2)]
        num_loaded, num3_loaded = sem("num_loaded"), [sem(f"num3_loaded{b}") for b in range(B)]
        o_step, oo_hi_done, oo_split = sem("o_step"), sem("oo_hi_done"), sem("oo_split")
        wo1_loaded, wo1_hi_done, wo1_split, wo1_mm, wo1_gated, attn1_added = (
            sem(n) for n in ("wo1_loaded", "wo1_hi_done", "wo1_split", "wo1_mm", "wo1_gated", "attn1_added"))
        g_loaded, g_tr, g_hi, g_lo, g_const = (sem(n) for n in ("g_loaded", "g_tr", "g_hi", "g_lo", "g_const"))
        r_mm, r_step, r_exp, r_kept, r_ktr, r_ktc = (
            sem(n) for n in ("r_mm", "r_step", "r_exp", "r_kept", "r_ktr", "r_ktc"))
        r_wmm, r_wexp, r_hmm, r_hfull, r_hhi, r_hlo = (sem(n) for n in ("r_wmm", "r_wexp", "r_hmm", "r_hfull", "r_hhi", "r_hlo"))
        g_mm, g_bias, g_gated, g_added, stored = (sem(n) for n in ("g_mm", "g_bias", "g_gated", "g_added", "stored"))
        spare = sem("spare")

        def wait_norm(eng, ph, b):
            eng.wait_ge(ln_lo, NT // 2 * ph + TB // 2 * (b + 1))
            eng.wait_ge(ln_lo_odd, NT // 2 * ph + TB // 2 * (b + 1))

        def norm_bank(j):
            return bank[(j + KT) % 8]

        def col_bank(l, half):
            return bank[4 + (half + l) % 2][:, 0:16]

        def gate_sums(l):
            return bank[4][0:2 * 32] if l == 0 else bank[2][0:2 * 32]

        USES = [(0, 1, 2, 3, 4, 5), (0, 1, 3, 4, 2, 5)]
        COLS_USED = [(2, 5), (2, 4)]
        GATE_BANKS = [(4, 5), (0, 1), (2, 3), (0, 1)]

        def g_bank(i):
            ps = bank[i % 4][:]
            return ps if i != 5 else ps.rearrange("p (k n) -> p k n", k=KT)[:, :, 0:NR]

        X_READY = [(x_loaded, 16 * NT), (attn0_added, NT * HKV), (f_added, NT), (attn1_added, NT)]

        wq, wk, wv, wo = a["L0_attn_wq"], a["L0_attn_wk"], a["L0_attn_wv"], a["L0_attn_wo"]
        wq_v, wk_v, wv_v = (w.rearrange("(k p) n -> p k n", p=P) for w in (wq, wk, wv))
        wo_v = wo.rearrange("(h p) n -> p h n", p=P)
        wr_v = a["L1_attn_Wq_rope"].rearrange("(k p) n -> p k n", p=P)
        wmod_v = [a[f"L{l}_wmod"].rearrange("(p k) n -> p k n", k=KT) for l in range(2)]

        W_TILE = {"K": 0, "V": 1, "Q0": 2, "Q1": 3, "Q2": 4, "Q3": 5}
        ROPE_NO = {"K": 0, "Q0": 1, "Q1": 2, "Q2": 3, "Q3": 4}

        block = ctx.enter_context(nc.Block())

        @block.sync
        def _(sp):
            sp.dma_start(cT[:, 0], a["L0_c"].rearrange("b (p k) -> p b k", k=KT)).then_inc(cond_loaded, 16)
            sp.dma_start(cT[:, 1], a["L1_c"].rearrange("b (p k) -> p b k", k=KT)).then_inc(cond_loaded, 16)
            for t in range(NT):
                sp.dma_start(x[:, t], x_in[:, t]).then_inc(x_loaded, 16)

            def load_wmod(l, c):
                i = 6 * l + c
                wait(sp, mod_mm, i - 2)
                sp.dma_start(WM[l][:, i % 3], wmod_v[l][:, :, c * D:(c + 1) * D]).then_inc(wm_loaded[i % 3], 16)

            def hold(semaphore, v):
                if not isinstance(v, int) or v > 0:
                    sp.wait_ge(semaphore, v)
                    sp.sem_inc(spare, 1)

            def load_kv(n):
                if exists(n, HKV):
                    hold(w_split, 6 * n)
                    sp.dma_start(st_kv[:, 0], wk_v[:, :, bass.ts(n, HD)]).then_inc(kv_loaded, 16)
                    sp.dma_start(st_kv[:, 1], wv_v[:, :, bass.ts(n, HD)]).then_inc(kv_loaded, 16)
                    sp.dma_start(st_q[:], wq_v[:, :, bass.ts(n, GQ * HD)]).then_inc(q_loaded, 16)

            def load_wo(n):
                if exists(n, HKV):
                    hold(wo_split, n)
                    sp.dma_start(st_wo[:], wo_v[:, bass.ts(n, GQ)]).then_inc(wo_loaded, 16)

            sp.dma_start(ident[:], a["identity"]).then_inc(ident_loaded, 16)
            sp.dma_start(sel[:], a["batch_rows"].rearrange("p (b m) -> p b m", b=B)).then_inc(ident_loaded, 16)
            sp.dma_start(rowsum[:], a["batch_columns"]).then_inc(ident_loaded, 16)
            load_wmod(0, 0)
            load_wmod(0, 1)
            load_kv(0)
            load_wmod(0, 2)
            sp.dma_start(rope_cos[:], a["rope_cos"]).then_inc(rope_loaded, 16)
            sp.dma_start(rope_sin[:], a["rope_sin"]).then_inc(rope_loaded, 16)
            sp.dma_start(window[:], a["window_mask"]).then_inc(rope_loaded, 16)
            load_wmod(0, 3)
            load_wmod(0, 4)
            load_wo(0)
            load_wmod(0, 5)
            with sp.Fori(1, HKV) as n:
                load_kv(n)
                load_wo(n)

            sp.wait_ge(w_split, 6 * HKV)
            sp.wait_ge(wo_split, HKV)
            sp.dma_start(fw[:], a["L0_ffn_W"].rearrange("(k p) d -> p k d", p=P)).then_inc(f_loaded, 16)
            for k in range(KT):
                sp.dma_start(fbf[:, k].rearrange("p (e r) -> p e r", r=16),
                             a["L0_ffn_Bf"].rearrange("e (k p) r -> k p e r", p=P)[k]).then_inc(f_loaded, 16)
            sp.dma_start(fa[:], a["L0_ffn_A"].rearrange("(t e) r d -> (e r) t d", t=2)).then_inc(f_loaded, 16)
            sp.dma_start(fco[:, 0:1], a["L0_ffn_coeffs"].rearrange("(e o) -> e o", o=1)).then_inc(f_loaded, 16)
            sp.dma_start(fco[:, 1:2], a["L0_ffn_scales"].rearrange("(e o) -> e o", o=1)).then_inc(f_loaded, 16)
            sp.dma_start(expand[:], a["lora_expand"]).then_inc(f_loaded, 16)
            sp.wait_ge(proj_done, TURNS * B * HKV)
            for c in range(3):
                load_wmod(1, c)

            sp.wait_ge(attn0_added, NT * HKV)
            sp.dma_start(fbias[:], a["L0_ffn_bias"].rearrange("(o n) -> o n", o=1).partition_broadcast(P)
                         .rearrange("p o n -> p (o n)")).then_inc(fbias_loaded, 16)
            for c in range(3, 6):
                load_wmod(1, c)
            for w, name in enumerate(("L1_attn_Wq_down", "L1_attn_Wkv_down")):
                sp.dma_start(dn[:, :, w * LAT:(w + 1) * LAT], a[name].rearrange("(k p) n -> p k n", p=P)).then_inc(pre_loaded, 16)
            for w in range(2):
                sp.dma_start(kr[:, :, w * ROPE:(w + 1) * ROPE],
                             a["L1_attn_Wk_rope"].rearrange("(k p) n -> p k n", p=P)).then_inc(pre_loaded, 16)
            sp.dma_start(up[0:LAT], a["L1_attn_Wq_up"]).then_inc(pre_loaded, 16)
            sp.dma_start(up[LAT:P], a["L1_attn_Wk_up"]).then_inc(pre_loaded, 16)
            sp.dma_start(vup[LAT:P], a["L1_attn_Wv_up"]).then_inc(pre_loaded, 16)

            def load_rope_weights(p, par):
                if exists(p, PAIRS):
                    hold(wr_split, p - 1)
                    sp.dma_start(wst[:, par], wr_v[:, :, bass.ts(p, P)]).then_inc(wr_loaded[par], 16)

            sp.wait_ge(mod_mm, 12)
            load_rope_weights(0, 0)
            load_rope_weights(1, 1)

            def store_content(m):
                for b in range(B):
                    for w, (dst, order) in enumerate(((qc_d, (0, 1, 0)), (kc_d, (0, 0, 1)))):
                        i = 2 * b + w
                        sp.wait_ge(c_split, 4 * m + i + 1)
                        for g, half in enumerate(order):
                            src = (c_hi, c_lo)[half][:, i].bitcast(F32)
                            sp.dma_start(dst[b, 32 * m:32 * m + 32, HD1 * g:HD1 * g + HD1], src).then_inc(c_stored[i], 16)

            def rows(h):
                return slice(ROPE, ROPE + CR) if h == 0 else slice(0, CR)

            def maxrow(h):
                return ROPE + CR if h == 0 else CR

            def period(u, k):
                v, vb = u + 1, (k + 1) % 2
                if exists(v, UNITS):
                    hold(scores1, 8 * (v - 1))
                    for h in range(2):
                        sp.dma_start(k2[rows(h), vb, h].bitcast(F32), kc_d[vb, hd(u, k, 1, h)].rearrange("o c s -> (o c) s"))\
                          .then_inc(k2c_loaded[vb], 16)
                v, vb = u + 3, (k + 3) % 2
                if exists(v, UNITS):
                    hold(max_mm, 8 * (v - 1))
                    for h in range(2):
                        sp.dma_start(km[rows(h), vb, h].bitcast(F32), kc_d[vb, hd(u, k, 3, h)].rearrange("o c s -> (o c) s"))\
                          .then_inc(mc_loaded[vb], 16)
                    hold(scores1, 8 * (v - 3))
                    for h in range(2):
                        sp.dma_start(q2[rows(h), (k + 3) % 4, h].bitcast(F32), qc_d[vb, hd(u, k, 3, h)].rearrange("o c s -> (o c) s"))\
                          .then_inc(mc_loaded[vb], 16)
                if k % 2 == 0:
                    load_rope_weights(pairs(u, k, 6), (k // 2 + 3) % 2)
                v = u - 1
                if exists(v, UNITS):
                    vb = (k + 1) % 2
                    hold(o_copied, v + 1)
                    for h in range(2):
                        for par in range(2):
                            j = 2 * h + par
                            sp.dma_start(o_d[vb, hd(u, k, -1, h), par].rearrange("o c s -> (o c) s"), ost[32 * j:32 * j + 8, (k + 1) % 2])\
                              .then_inc(o_stored[(k + 1) % 2], 16)
                v = u + 2
                if exists(v, UNITS):
                    hold(m_turned, v + 1)
                    for h in range(2):
                        r = maxrow(h)
                        sp.dma_start(q2[r:r + 1, (k + 2) % 4, h].bitcast(F32).rearrange("p (q n) -> p q n", q=4),
                                     mrow[h:P:32, k % 2]).then_inc(m_loaded[k % 2], 16)

            def pairs(u, k, ahead):
                if isinstance(u, int):
                    return (u + ahead) // 2
                return 2 * G[0] + (k + ahead) // 2

            def hd(u, k, ahead, h):
                return bass.ds(2 * pairs(u, k, ahead) + h, 1)

            G = [None]
            store_content(0)
            for i in range(4):
                sp.wait_ge(c_stored[i], 48)
            sp.wait_ge(zeroed, 6)
            for b in range(B):
                for h in range(2):
                    sp.dma_start(k2[maxrow(h):maxrow(h) + 1, b, h].bitcast(F32), ost[0:1, 0]).then_inc(ones_set, 16)
            for u in range(-3, 0):
                period(u, u % 4)
                store_content(u + 4)
            for u in range(0, 6):
                period(u, u % 4)
            for i in range(4):
                sp.wait_ge(c_stored[i], 48 * KT)
            with sp.Fori(1, UNITS // 4 - 2) as g:
                G[0] = g
                for k in range(2, 6):
                    period(4 * g + k, k)

            def load_sums(dst_num, dst_den, b, m, loaded):
                for par in range(2):
                    for dst, r in ((dst_num, 0), (dst_den, HD1)):
                        sp.dma_start(dst[:, par], o_d[b, 32 * m:32 * m + 32, par, r:r + HD1]).then_inc(loaded, 16)

            for u in range(UNITS - 6, UNITS + 1):
                period(u, u % 4)
                n = u - (UNITS - 6)
                if n < 6:
                    if n == 0:
                        for i in range(2):
                            sp.wait_ge(o_stored[i], 64 * 48)
                    wait(sp, oo_split, n)
                    load_sums(num, dnm, n % 2, n // 2, num_loaded)

            sp.wait_ge(o_copied, UNITS)
            sp.dma_start(wo1[:], a["L1_attn_Wo"].rearrange("(k p) n -> p k n", p=P)).then_inc(wo1_loaded, 16)
            for i in range(2):
                sp.wait_ge(o_stored[i], 64 * PAIRS)
            for b in range(B):
                load_sums(num3[:, b], dnm3[:, b], b, KT - 1, num3_loaded[b])

            sp.dma_start(bw[:], a["L1_ffn_base_W"].rearrange("(k p) d -> p k d", p=P)).then_inc(g_loaded, 16)
            sp.dma_start(la[:], a["L1_ffn_A"].rearrange("e r d -> (e r) d")).then_inc(g_loaded, 16)
            sp.dma_start(rw[0:NR], a["L1_ffn_router_W"]).then_inc(g_loaded, 16)
            for k in range(KT):
                sp.dma_start(lb[:, k], a["L1_ffn_B"].rearrange("e (k p) r -> k p e r", p=P)[k]).then_inc(g_loaded, 16)
            for dst, name in ((bbias, "L1_ffn_base_b"), (rbias, "L1_ffn_router_b")):
                sp.dma_start(dst[:], a[name].rearrange("(o n) -> o n", o=1).partition_broadcast(P)
                             .rearrange("p o n -> p (o n)")).then_inc(g_loaded, 16)
            sp.dma_start(emap_i[0:NR], a["L1_ffn_expert_map"].rearrange("(e o) -> e o", o=1)).then_inc(g_loaded, 16)
            sp.dma_start(ecol[:], a["expert_of_column"]).then_inc(g_loaded, 16)
            sp.dma_start(before[:].rearrange("p n m -> p (n m)"),
                         a["entry_before"].rearrange("n m -> (n m)").rearrange("(o k) -> o k", o=1).partition_broadcast(P)
                         .rearrange("p o n -> p (o n)")).then_inc(g_loaded, 16)
            for t in range(NT):
                sp.wait_ge(g_added, t + 1)
                sp.dma_start(out_t[:, t], x[:, t]).then_inc(stored, 16)
            sp.wait_ge(stored, 16 * NT)

        @block.gpsimd
        def _(pool):
            def split_weights(n, tiles):
                for m in tiles:
                    pool.wait_ge(w_hi_done, 6 * n + m + 1)
                    src = st_kv[:, m] if m < 2 else st_q[:, :, (m - 2) * HD:(m - 1) * HD]
                    pool.tensor_tensor(w_lo[:, m], src, w_hi[:, m].bitcast(F32), ALU.subtract).then_inc(w_split, 1)

            def split_wo(n):
                pool.wait_ge(wo_hi_done, n + 1)
                pool.tensor_tensor(wo_lo[:], st_wo[:], wo_hi[:].bitcast(F32), ALU.subtract).then_inc(wo_split, 1)

            def rope(half, name, b):
                r = 5 * half + ROPE_NO[name]
                i = (b + ROPE_NO[name]) % 2
                pool.wait_ge(proj_free, TURNS * half + TURN[name] + 1)
                pool.tensor_tensor(rope_a[:, i], rope_a[:, i], rope_b[:, i], ALU.add).then_inc(rope_sum, 1)
                pool.wait_ge(rope_hi, r + 1)
                hi, lo = (kT_hi[:, b], kT_lo[:, b]) if name == "K" else (qT_hi[b][:, ROPE_NO[name] - 1], qT_lo[b][:, ROPE_NO[name] - 1])
                pool.tensor_tensor(lo, rope_a[:, i], hi.bitcast(F32), ALU.subtract).then_inc(rope_split, 1)

            def add_attention(slot, tile):
                pool.wait_ge(wo_gated, slot + 1)
                pool.tensor_tensor(x[:, tile], x[:, tile], gated[:], ALU.add).then_inc(attn0_added, 1)

            def norm(ph, b):
                for j in range(KT * b + 1, KT * b + KT, 2):
                    pool.wait_ge(ln_hi, NT * ph + j + 1)
                    at = slice(b * S, (b + 1) * S)
                    pool.tensor_tensor(hT_lo[:, j % KT, at], NORM[ph][1][:, j % 4], hT_hi[:, j % KT, at].bitcast(F32), ALU.subtract)\
                        .then_inc(ln_lo_odd, 1)

            pool.memset(silu[:], 0.0).then_inc(silu_zeroed, 1)
            split_weights(0, (0, 1))
            norm(0, 0)
            split_weights(0, (2,))
            norm(0, 1)
            split_weights(0, (3, 4, 5))
            wait_norm(pool, 0, 1)
            for name in ROPE_NO:
                rope(0, name, 0)
            rope(1, "K", 1)

            def kv_head(n, last):
                for b in range(B):
                    half = 2 * n + b
                    if not (isinstance(n, int) and n == 0 and b == 0):
                        add_attention(4 * half - 1, TB * (1 - b) + 3)
                    if b == 0:
                        split_wo(n)
                    if not (last and b == 1):
                        rope(half + 1, "Q0", 1 - b)
                        rope(half + 1, "Q1", 1 - b)
                    add_attention(4 * half, TB * b)
                    if b == 0 and not last:
                        split_weights(n + 1, (0, 1))
                    if not (last and b == 1):
                        rope(half + 1, "Q2", 1 - b)
                        rope(half + 1, "Q3", 1 - b)
                    add_attention(4 * half + 1, TB * b + 1)
                    if not last:
                        rope(half + 2, "K", b)
                        if b == 0:
                            split_weights(n + 1, (2, 3, 4, 5))
                    add_attention(4 * half + 2, TB * b + 2)
                if last:
                    add_attention(8 * n + 7, NT - 1)

            kv_head(0, False)
            with pool.Fori(1, HKV - 1) as n:
                kv_head(n, False)
            kv_head(HKV - 1, True)
            for b in range(B):
                norm(1, b)
            for t in range(NT):
                pool.wait_ge(f_gated, t + 1)
                pool.tensor_tensor(x[:, t], x[:, t], fg[:, t % 2], ALU.add).then_inc(f_added, 1)
                if t == 1:
                    for i, (src, hi, lo) in enumerate(((dn, dn_hi, dn_lo), (kr, kr_hi, kr_lo))):
                        pool.wait_ge(pre_hi, i + 1)
                        pool.tensor_tensor(lo[:], src[:], hi[:].bitcast(F32), ALU.subtract).then_inc(pre_split, 1)
            if True:
                for b in range(B):
                    norm(2, b)
                pool.wait_ge(f_split, KT)
                pool.wait_ge(mod_mm, 12)
                pool.memset(k2[:].bitcast(F32), 0.0).then_inc(zeroed, 1)
                pool.memset(km[:].bitcast(F32), 0.0).then_inc(zeroed, 1)
                pool.memset(q2[:].bitcast(F32), 0.0).then_inc(zeroed, 1)
                pool.memset(vp[:], 0.0).then_inc(zeroed, 1)
                pool.memset(mcol[:].bitcast(F32), 0.0).then_inc(zeroed, 1)
                wait_norm(pool, 2, 1)
                pool.memset(ost[0:1, 0], 1.0).then_inc(zeroed, 1)
                pool.wait_ge(zeroed, 6)
                pool.memset(vp[:, :, :, :, HD1:2 * HD1], 1.0).then_inc(zeroed, 1)

                def split_rope_weights(p, par):
                    if exists(p, PAIRS):
                        pool.wait_ge(wr_hi_done, p + 1)
                        pool.tensor_tensor(wr_lo[:, par], wst[:, par], wr_hi[:, par].bitcast(F32), ALU.subtract).then_inc(wr_split, 1)

                split_rope_weights(0, 0)
                split_rope_weights(1, 1)
                with pool.Fori(0, PAIRS // 2 - 1) as g:
                    split_rope_weights(2 * g + 2, 0)
                    split_rope_weights(2 * g + 3, 1)
            for t in range(NT):
                pool.wait_ge(wo1_gated, t + 1)
                pool.tensor_tensor(x[:, t], x[:, t], og[:, t % 2], ALU.add).then_inc(attn1_added, 1)
            for b in range(B):
                norm(3, b)
            if True:
                for t in range(NT):
                    pool.wait_ge(g_gated, t + 1)
                    pool.tensor_tensor(x[:, t], x[:, t], gg[:, t % 2], ALU.add).then_inc(g_added, 1)

        @block.scalar
        def _(act):
            act.wait_ge(cond_loaded, 32)
            act.activation(silu_e[:], cT[:], ACT.Exp, scale=-1.0).then_inc(silu_exp, 1)

            def mod_rows(l, chunks):
                for c in chunks:
                    i = 6 * l + c
                    act.wait_ge(mod_mm, i + 1)
                    if c in (3, 4):
                        act.wait_ge(mod_used, i - 2)
                    act.activation(MODROW[l][:, ROW_SLOT[c]], bank[2 + c % 2][:], ACT.Copy).then_inc(mod_row, 1)

            def gates(l, w, dst):
                act.wait_ge(gate_bc, 2 * l + w + 1)
                for b, ps in enumerate(GATE_BANKS[2 * l + w]):
                    e = act.activation(dst[:, b], bank[ps][:], ACT.Copy)
                e.then_inc(gate_ready, 1)

            def norm_std(ph, b):
                act.wait_ge(ln_eps, B * ph + b + 1)
                act.activation(std[:, TB * b:TB * b + TB], var_eps[:, TB * b:TB * b + TB], ACT.Sqrt).then_inc(ln_std, 1)

            def norm(ph, b):
                _, full, l, v = NORM[ph]
                act.wait_ge(col_ready, 2 * l + v // 2 + 1)
                act.wait_ge(ln_trans, NT * ph + TB * (b + 1))
                for j in range(KT * b, KT * b + KT):
                    k = j % KT
                    if j >= 4:
                        act.wait_ge(ln_lo_odd if j % 2 else ln_lo, NT // 2 * ph + (j - 4) // 2 + 1)
                    act.activation(full[:, j % 4], norm_bank(j)[:], ACT.Identity, bias=modc[:, l, v, k, b:b + 1],
                                   scale=modc[:, l, v + 1, k, b:b + 1]).then_inc(ln_full, 1)

            mod_rows(0, (0, 1))
            for b in range(B):
                norm_std(0, b)
            for b in range(B):
                norm(0, b)

            def rope_high(half, name, b):
                r = 5 * half + ROPE_NO[name]
                act.wait_ge(rope_sum, r + 1)
                hi = kT_hi[:, b] if name == "K" else qT_hi[b][:, ROPE_NO[name] - 1]
                act.activation(hi, rope_a[:, (b + ROPE_NO[name]) % 2], ACT.Copy).then_inc(rope_hi, 1)

            def v_high(half, b):
                act.wait_ge(proj_done, TURNS * half + TURN["Vt"] + 1)
                act.activation(v_hi[:, b].rearrange("p t d -> p (t d)"), bank[6 + (b + TURN["Vt"]) % 2][:], ACT.Copy).then_inc(v_hi_done, 1)

            def exps(slot, qb):
                i = qb % 2
                c = slice(P, 2 * P) if qb == 0 else slice(0, 2 * P)
                act.wait_ge(masked0, slot + 1)
                for h in range(GQ):
                    e = act.activation(probs[:, i, h, c], probs[:, i, h, c], ACT.Exp, bias=nmax[:, i, h:h + 1], scale=1.0,
                                       accum_out=den[:, i, h:h + 1])
                e.then_inc(exp0, 1)

            def weights_high(slot, qb):
                act.wait_ge(trans0, slot + 1)
                for kb in range(1 if qb == 0 else 0, 2):
                    e = act.activation(pT_hi[:, kb], bank[2 + kb][:], ACT.Copy)
                e.then_inc(pT_hi_done, 1)

            def kv_head(n, last):
                for b in range(B):
                    half, slot, nb = 2 * n + b, 8 * n + 4 * b, 1 - b
                    more = not (last and b == 1)
                    weights_high(slot, 0)
                    exps(slot + 1, 1)
                    if isinstance(n, int) and n == 0 and b == 0:
                        gates(0, 0, gate_a0)
                    out_high(slot)
                    if more:
                        rope_high(half + 1, "Q0", nb)
                    weights_high(slot + 1, 1)
                    if more:
                        v_high(half + 1, nb)
                        rope_high(half + 1, "Q1", nb)
                    exps(slot + 2, 2)
                    out_high(slot + 1)
                    weights_high(slot + 2, 2)
                    if more:
                        rope_high(half + 1, "Q2", nb)
                    exps(slot + 3, 3)
                    out_high(slot + 2)
                    if more:
                        rope_high(half + 1, "Q3", nb)
                    weights_high(slot + 3, 3)
                    if not last:
                        rope_high(half + 2, "K", b)
                    out_high(slot + 3)
                    if more:
                        exps(slot + 4, 0)

            def out_high(slot):
                act.wait_ge(pv0, slot + 1)
                act.activation(oT_hi[:].rearrange("p h t -> p (h t)"), bank[4][:], ACT.Copy).then_inc(oT_hi_done, 1)

            rope_high(0, "K", 0)
            rope_high(0, "Q0", 0)
            rope_high(0, "Q1", 0)
            v_high(0, 0)
            rope_high(0, "Q2", 0)
            rope_high(0, "Q3", 0)
            mod_rows(0, (2, 3, 4, 5))
            rope_high(1, "K", 1)
            exps(0, 0)
            kv_head(0, False)
            with act.Fori(1, HKV - 1) as n:
                kv_head(n, False)
            kv_head(HKV - 1, True)

            for t in range(2):
                act.wait_ge(f_tr, t + 1)
                act.activation(fbfT[:, t], bank[6 + t][:], ACT.Copy).then_inc(f_trs, 1)
            for b in range(B):
                norm_std(1, b)
            mod_rows(1, range(6))

            def merged_high(k):
                act.wait_ge(f_mg, k + 1)
                act.activation(fw_hi[:, k], bank[k][:], ACT.Copy).then_inc(f_hi, 1)

            merged_high(0)
            merged_high(1)
            norm(1, 0)
            merged_high(2)
            merged_high(3)
            norm(1, 1)
            gates(0, 1, gate[:, 0])
            act.wait_ge(pre_loaded, 16 * 7)
            for src, hi in ((dn, dn_hi), (kr, kr_hi)):
                act.activation(hi[:], src[:], ACT.Copy).then_inc(pre_hi, 1)
            gates(1, 0, gate[:, 1])
            gates(1, 1, gate[:, 2])

            if True:
                for b in range(B):
                    norm_std(2, b)
                for b in range(B):
                    norm(2, b)
                for b in range(B):
                    act.wait_ge(lat_mm, b + 1)
                    act.activation(lat[:, b * S:(b + 1) * S], bank[4 + b][:], ACT.Copy).then_inc(lat_ready, 1)
                act.wait_ge(zeroed, 6)
                for b in range(B):
                    act.wait_ge(kr_mm, b + 1)
                    act.activation(k1[:, b], bank[6 + b][:], ACT.Copy)
                    act.activation(km[0:ROPE, b, 0], bank[6 + b][0:ROPE], ACT.Copy)
                    act.activation(km[ROPE:P, b, 1], bank[6 + b][ROPE:P], ACT.Copy).then_inc(kr_hi_done, 1)

                def content_high(m):
                    for i in range(4):
                        act.wait_ge(c_mm, 4 * m + i + 1)
                        wait(act, c_stored[i], 48 * m)
                        act.activation(c_hi[:, i], bank[i][:], ACT.Copy).then_inc(c_hi_done, 1)

                content_high(0)
                for t in range(NT):
                    act.wait_ge(vc_mm, t + 1)
                    act.activation(vc[:, t], bank[4 + t % 2][:], ACT.Copy).then_inc(vc_ready, 1)

                act.sem_inc(exp1, 4)

                def q_high(z, k):
                    if exists(z, UNITS):
                        act.wait_ge(qr_mm, z + 1)
                        act.activation(q2[0:ROPE, k % 4, 0], bank[6][0:ROPE], ACT.Copy)
                        act.activation(q2[ROPE:P, k % 4, 1], bank[6][ROPE:P], ACT.Copy).then_inc(q2_hi, 1)

                def q_high_again(z, k):
                    if exists(z, UNITS):
                        act.wait_ge(q2_hi, z + 1)
                        act.activation(q1[0:ROPE, k % 4, 0], q2[0:ROPE, k % 4, 0], ACT.Copy)
                        act.activation(q1[ROPE:P, k % 4, 1], q2[ROPE:P, k % 4, 1], ACT.Copy).then_inc(q1_hi, 1)

                def period(u, k, pair):
                    q_high(u + 2, k + 2)
                    for s in range(8):
                        if s == 6:
                            q_high_again(u + 2, k + 2)
                        if s == 2:
                            if exists(u - 1, UNITS):
                                act.wait_ge(pv1, 2 * u + 1)
                                wait(act, o_stored[(k + 1) % 2], 64 * pair(-1))
                                act.activation(ost[:, (k + 1) % 2], bank[7][:], ACT.Copy).then_inc(o_copied, 1)
                        if exists(u, UNITS):
                            act.wait_ge(scores1, 8 * u + s + 1)
                            wait(act, pv1, 2 * u + s // 4)
                            act.activation(pT[:, s], bank[s % 4][:], ACT.Exp, scale=float((HD1 + ROPE) ** -0.5)).then_inc(exp1, 1)

                for u in range(-3, 6):
                    period(u, u % 4, lambda n, u=u: (u + n) // 2)
                    if u < 0:
                        content_high(u + 4)
                with act.Fori(1, UNITS // 4 - 2) as g:
                    for k in range(2, 6):
                        period(4 * g + k, k, lambda n, k=k: 2 * g + (k + n) // 2)
                def sums_high(n):
                    b, m = n % 2, n // 2
                    at = slice(b * S, (b + 1) * S)
                    act.wait_ge(o_step, 4 * n + 4)
                    src = num[:, 0] if m < KT - 1 else num3[:, b, 0]
                    dst = oo_hi[:, m, at] if m < KT - 1 else oo3_hi[:, at]
                    act.activation(dst, src, ACT.Copy).then_inc(oo_hi_done, 1)

                for u in range(UNITS - 6, UNITS + 1):
                    period(u, u % 4, lambda n, u=u: (u + n) // 2)
                    if u > UNITS - 6:
                        sums_high(u - (UNITS - 5))
            if True:
                act.wait_ge(wo1_loaded, 16)
                for k in range(KT):
                    act.activation(wo1_hi[:, k], wo1[:, k], ACT.Copy).then_inc(wo1_hi_done, 1)
                for b in range(B):
                    sums_high(6 + b)
                for i, dst in enumerate([*(bwT_hi[:, k] for k in range(KT)), laT_hi[:].rearrange("p k n -> p (k n)"),
                                         rwT_hi[:, :, 0:NR], lbT_hi[:]]):
                    act.wait_ge(g_tr, i + 1)
                    act.activation(dst, g_bank(i), ACT.Copy).then_inc(g_hi, 1)
                    if i == KT - 1:
                        for b in range(B):
                            norm_std(3, b)
                for b in range(B):
                    norm(3, b)
                act.wait_ge(r_step, 3)
                act.activation(prob[:], lg[:], ACT.Exp).then_inc(r_exp, 1)
                for b in range(B):
                    act.wait_ge(r_ktr, b + 1)
                    act.activation(keptT[0:NR, b * S:(b + 1) * S], bank[(7, 4)[b]][0:NR], ACT.Copy).then_inc(r_ktc, 1)
                for b in range(B):
                    act.wait_ge(r_wmm, b + 1)
                    act.activation(wexp[:, b * S:(b + 1) * S], bank[(7, 4)[b]][:], ACT.Copy, scale=SCALING).then_inc(r_wexp, 1)
                for b in range(B):
                    act.wait_ge(r_hfull, b + 1)
                    act.activation(lh_hi[:, b * S:(b + 1) * S], lh[:, b * S:(b + 1) * S], ACT.Copy).then_inc(r_hhi, 1)

        @block.vector
        def _(dve):
            dve.wait_ge(silu_exp, 1)
            dve.tensor_scalar(silu_d[:], silu_e[:], 1.0, None, ALU.add).then_inc(silu_step, 1)
            dve.wait_ge(silu_step, 1)
            dve.reciprocal(silu_e[:], silu_d[:]).then_inc(silu_step, 1)
            dve.wait_ge(silu_step, 2)
            dve.wait_ge(silu_zeroed, 1)
            for l in range(2):
                e = dve.tensor_tensor(silu[:, l, :, 0:B].rearrange("p k b -> p b k"), cT[:, l], silu_e[:, l], ALU.mult)
            e.then_inc(silu_step, 1)

            def mod_cols(l, half):
                dve.wait_ge(mod_used, 6 * l + COLS_USED[l][half])
                src = col_bank(l, half).rearrange("p (v k b) -> p v k b", v=2, k=KT)
                dve.tensor_copy(modc[:, l, 2 * half], src[:, 0])
                dve.tensor_scalar(modc[:, l, 2 * half + 1], src[:, 1], 1.0, None, ALU.add).then_inc(col_ready, 1)

            def clamp_gates(l):
                src, sign, g = gate_sums(l), GSIGN[l][0:2 * 32], GROWS[l]
                dve.wait_ge(mod_used, 6 * l + 6)
                dve.tensor_scalar(sign, src, 0.0, 2.0, ALU.is_ge, ALU.mult).then_inc(gate_step, 1)
                dve.wait_ge(gate_step, 3 * l + 1)
                dve.tensor_scalar(sign, sign, -1.0, None, ALU.add).then_inc(gate_step, 1)
                dve.wait_ge(gate_step, 3 * l + 2)
                dve.tensor_tensor(g[:], src, sign, ALU.mult).then_inc(gate_step, 1)
                dve.wait_ge(gate_step, 3 * l + 3)
                dve.scalar_tensor_tensor(g[:], g[:], 0.25, sign, ALU.max, ALU.mult).then_inc(gate_rows, 1)

            def norm_stats(ph, b):
                ready, count = X_READY[ph]
                tiles = range(TB * b, TB * b + TB)
                for t in tiles:
                    dve.wait_ge(ready, count if ph == 0 else count - NT + t + 1)
                    dve.bn_stats(stats[:, t], x[:, t]).then_inc(ln_stats, 1)
                for t in tiles:
                    dve.wait_ge(ln_stats, NT * ph + t + 1)
                    dve.bn_aggr(mean_var[:, t], stats[:, t]).then_inc(ln_aggr, 1)
                dve.wait_ge(ln_aggr, NT * ph + TB * (b + 1))
                at = slice(TB * b, TB * b + TB)
                dve.tensor_scalar(var_eps[:, at], mean_var[:, at, 1], EPS, None, ALU.add).then_inc(ln_eps, 1)

            def norm_rows(ph, b):
                at = slice(TB * b, TB * b + TB)
                dve.wait_ge(ln_std, B * ph + b + 1)
                dve.reciprocal(rstd[:, at], std[:, at]).then_inc(ln_rstd, 1)
                dve.wait_ge(ln_rstd, B * ph + b + 1)
                for t in range(TB * b, TB * b + TB):
                    dve.tensor_scalar(NORM[ph][0][:, t], x[:, t], mean_var[:, t, 0:1], rstd[:, t:t + 1], ALU.subtract, ALU.mult)\
                       .then_inc(ln_norm, 1)

            def norm_split(ph, b):
                at = slice(b * S, (b + 1) * S)
                for j in range(KT * b, KT * b + KT):
                    dve.wait_ge(ln_full, NT * ph + j + 1)
                    dve.tensor_copy(hT_hi[:, j % KT, at], NORM[ph][1][:, j % 4]).then_inc(ln_hi, 1)
                    if j % 2 == 0:
                        dve.wait_ge(ln_hi, NT * ph + j + 1)
                        dve.tensor_tensor(hT_lo[:, j % KT, at], NORM[ph][1][:, j % 4], hT_hi[:, j % KT, at].bitcast(F32),
                                          ALU.subtract).then_inc(ln_lo, 1)

            def split_weights(n, tiles):
                for m in tiles:
                    src = st_kv[:, m] if m < 2 else st_q[:, :, (m - 2) * HD:(m - 1) * HD]
                    if m < 2:
                        dve.wait_ge(kv_loaded, 32 * n + 32)
                    else:
                        dve.wait_ge(q_loaded, 16 * n + 16)
                    if not isinstance(n, int) or n > 0:
                        name = [k for k, v in W_TILE.items() if v == m][0]
                        dve.wait_ge(proj_done, TURNS * (2 * n - 1) + TURN[name] + 1)
                    dve.tensor_copy(w_hi[:, m], src).then_inc(w_hi_done, 1)

            def split_wo(n):
                dve.wait_ge(wo_loaded, 16 * n + 16)
                wait(dve, wo_mm, 8 * n)
                dve.tensor_copy(wo_hi[:], st_wo[:]).then_inc(wo_hi_done, 1)

            def evacuate(half, name, b):
                e = TURNS * half + TURN[name]
                ps = bank[6 + (b + TURN[name]) % 2]
                if name == "Vt":
                    dve.wait_ge(v_hi_done, half + 1)
                    dve.tensor_tensor(v_lo[:, b].rearrange("p t d -> p (t d)"), ps[:], v_hi[:, b].rearrange("p t d -> p (t d)").bitcast(F32),
                                      ALU.subtract).then_inc(proj_free, 1)
                    return
                dve.wait_ge(proj_done, e + 1)
                if name == "V":
                    dve.tensor_copy(vT[:], ps[:]).then_inc(proj_free, 1)
                    return
                i = (b + ROPE_NO[name]) % 2
                wait(dve, rope_split, 5 * half + ROPE_NO[name] - 1)
                dve.tensor_tensor(rope_a[:, i], ps[:], rope_cos[:], ALU.mult)
                dve.tensor_tensor(rope_b[0:64, i], ps[64:P], rope_sin[64:P], ALU.mult)
                dve.tensor_tensor(rope_b[64:P, i], ps[0:64], rope_sin[0:64], ALU.mult).then_inc(proj_free, 1)

            def mask(slot, qb):
                i = qb % 2
                c = slice(P, 2 * P) if qb == 0 else slice(0, 2 * P)
                dve.wait_ge(scores0, slot + 1)
                dve.sem_inc(spare, 1)
                for h in range(GQ):
                    ps = bank[h // 2][:, (h % 2) * 2 * P:(h % 2 + 1) * 2 * P]
                    e = dve.tensor_tensor_reduce(probs[:, i, h, c], ps[:, c], window[:, c], float(HD) ** -0.5, -3e38, ALU.add, ALU.max,
                                                 rmax[:, i, h:h + 1])
                e.then_inc(rowmax0, 1)
                dve.wait_ge(rowmax0, slot + 1)
                dve.tensor_scalar(nmax[:, i], rmax[:, i], -1.0, None, ALU.mult).then_inc(masked0, 1)

            def normalise(slot, qb):
                i = qb % 2
                c = slice(P, 2 * P) if qb == 0 else slice(0, 2 * P)
                dve.wait_ge(exp0, slot + 1)
                dve.reciprocal(rden[:, i], den[:, i]).then_inc(rden0, 1)
                dve.wait_ge(rden0, slot + 1)
                for h in range(GQ):
                    e = dve.tensor_scalar(probs[:, i, h, c], probs[:, i, h, c], rden[:, i, h:h + 1], None, ALU.mult)
                e.then_inc(probs0, 1)

            def weights_low(slot, qb):
                dve.wait_ge(pT_hi_done, slot + 1)
                for kb in range(1 if qb == 0 else 0, 2):
                    e = dve.tensor_tensor(pT_lo[:, kb], bank[2 + kb][:], pT_hi[:, kb].bitcast(F32), ALU.subtract)
                e.then_inc(pT_split, 1)

            def out_low(slot):
                dve.wait_ge(oT_hi_done, slot + 1)
                dve.tensor_tensor(oT_lo[:].rearrange("p h t -> p (h t)"), bank[4][:], oT_hi[:].rearrange("p h t -> p (h t)").bitcast(F32),
                                  ALU.subtract).then_inc(oT_split, 1)

            def gate_attention(slot, b):
                dve.wait_ge(wo_mm, slot + 1)
                if isinstance(slot, int) and slot == 0:
                    dve.wait_ge(gate_ready, 1)
                wait(dve, attn0_added, slot)
                dve.tensor_tensor(gated[:], bank[5][:], gate_a0[:, b], ALU.mult).then_inc(wo_gated, 1)

            def kv_head(n, last):
                for b in range(B):
                    half, slot, nb = 2 * n + b, 8 * n + 4 * b, 1 - b
                    more = not (last and b == 1)
                    if not (isinstance(n, int) and n == 0 and b == 0):
                        gate_attention(slot - 1, nb)
                    if b == 0:
                        split_wo(n)
                    weights_low(slot, 0)
                    mask(slot + 1, 1)
                    if more:
                        evacuate(half + 1, "Q0", nb)
                    normalise(slot + 1, 1)
                    out_low(slot)
                    if b == 0 and not last:
                        split_weights(n + 1, (0, 1))
                    if more:
                        evacuate(half + 1, "Q1", nb)
                    weights_low(slot + 1, 1)
                    mask(slot + 2, 2)
                    if more:
                        evacuate(half + 1, "Vt", nb)
                    gate_attention(slot, b)
                    normalise(slot + 2, 2)
                    out_low(slot + 1)
                    if more:
                        evacuate(half + 1, "Q2", nb)
                    weights_low(slot + 2, 2)
                    mask(slot + 3, 3)
                    if more:
                        evacuate(half + 1, "Q3", nb)
                    gate_attention(slot + 1, b)
                    normalise(slot + 3, 3)
                    out_low(slot + 2)
                    if last and b == 1:
                        norm_stats(1, 0)
                    weights_low(slot + 3, 3)
                    if not last:
                        evacuate(half + 2, "K", b)
                        if b == 0:
                            split_weights(n + 1, (2, 3, 4, 5))
                    gate_attention(slot + 2, b)
                    if more:
                        mask(slot + 4, 0)
                    out_low(slot + 3)
                    if more:
                        if not last:
                            evacuate(half + 2, "V", b)
                        normalise(slot + 4, 0)
                if last:
                    gate_attention(8 * n + 7, 1)

            norm_stats(0, 0)
            norm_stats(0, 1)
            norm_rows(0, 0)
            norm_rows(0, 1)
            mod_cols(0, 0)
            split_weights(0, (0, 1))
            norm_split(0, 0)
            split_weights(0, (2, 3))
            norm_split(0, 1)
            split_weights(0, (4, 5))
            dve.wait_ge(rope_loaded, 48)
            for name in TURN:
                evacuate(0, name, 0)
            evacuate(1, "K", 1)
            mod_cols(0, 1)
            mask(0, 0)
            evacuate(1, "V", 1)
            normalise(0, 0)
            clamp_gates(0)
            kv_head(0, False)
            with dve.Fori(1, HKV - 1) as n:
                kv_head(n, False)
            kv_head(HKV - 1, True)

            dve.wait_ge(f_loaded, 16 * 9)
            dve.tensor_tensor(fcw[:], fco[:, 0:1], fco[:, 1:2], ALU.mult).then_inc(f_cw, 1)
            norm_stats(1, 1)
            norm_rows(1, 0)
            dve.wait_ge(f_er_mm, 1)
            dve.tensor_copy(fer[:], bank[4][:, 0:2]).then_inc(f_er, 1)
            dve.wait_ge(f_er, 1)
            for t in range(2):
                dve.tensor_scalar(fa_s[:, t], fa[:, t], fer[:, t:t + 1], None, ALU.mult).then_inc(f_as, 1)

            def merged_low(k):
                dve.wait_ge(f_hi, k + 1)
                dve.tensor_tensor(fw_lo[:, k], bank[k][:], fw_hi[:, k].bitcast(F32), ALU.subtract).then_inc(f_split, 1)

            norm_rows(1, 1)
            mod_cols(1, 0)
            merged_low(0)
            merged_low(1)
            mod_cols(1, 1)
            norm_split(1, 0)
            merged_low(2)
            merged_low(3)
            norm_split(1, 1)
            dve.wait_ge(fbias_loaded, 16)
            for t in range(NT):
                dve.wait_ge(f_mm, t + 1)
                dve.tensor_tensor(fu[:, t % 2], bank[4 + t % 4][:], fbias[:], ALU.add).then_inc(f_bias, 1)
                if t == 0:
                    dve.wait_ge(gate_ready, 2)
                dve.wait_ge(f_bias, t + 1)
                wait(dve, f_added, t - 1)
                dve.tensor_tensor(fg[:, t % 2], fu[:, t % 2], gate[:, 0, t // TB], ALU.mult).then_inc(f_gated, 1)
                if t == 1:
                    clamp_gates(1)
                if t == 5:
                    norm_stats(2, 0)

            norm_stats(2, 1)
            norm_rows(2, 0)
            norm_rows(2, 1)
            norm_split(2, 0)
            norm_split(2, 1)
            if True:
                def split_rope_weights(p, par, use):
                    if exists(p, PAIRS):
                        dve.wait_ge(wr_loaded[par], 16 * use + 16)
                        wait(dve, qr_mm, 2 * p - 2)
                        dve.tensor_copy(wr_hi[:, par], wst[:, par]).then_inc(wr_hi_done, 1)

                split_rope_weights(0, 0, 0)
                dve.wait_ge(zeroed, 7)
                for b in range(B):
                    dve.wait_ge(kr_hi_done, b + 1)
                    dve.tensor_tensor(k2[0:ROPE, b, 0], bank[6 + b][0:ROPE], k1[0:ROPE, b].bitcast(F32), ALU.subtract)
                    dve.tensor_tensor(k2[ROPE:P, b, 1], bank[6 + b][ROPE:P], k1[ROPE:P, b].bitcast(F32), ALU.subtract).then_inc(kr_split, 1)

                def content_low(m):
                    for i in range(4):
                        dve.wait_ge(c_hi_done, 4 * m + i + 1)
                        dve.tensor_tensor(c_lo[:, i], bank[i][:], c_hi[:, i].bitcast(F32), ALU.subtract).then_inc(c_split, 1)

                content_low(0)
                dve.wait_ge(vc_ready, NT)

                def q_low(z, k):
                    if exists(z, UNITS):
                        dve.wait_ge(q2_hi, z + 1)
                        dve.tensor_tensor(q1[ROPE:P, k % 4, 0], bank[6][0:ROPE], q2[0:ROPE, k % 4, 0].bitcast(F32), ALU.subtract)
                        dve.tensor_tensor(q1[0:ROPE, k % 4, 1], bank[6][ROPE:P], q2[ROPE:P, k % 4, 1].bitcast(F32), ALU.subtract)\
                           .then_inc(q1_split, 1)

                def maxima(w, k, use):
                    if exists(w, UNITS):
                        wait(dve, m_loaded[k % 2], 32 * use)
                        for i in range(8):
                            dve.wait_ge(max_mm, 8 * w + i + 1)
                            dve.tensor_reduce(mcol[:, k % 2, i % 4, i // 4:i // 4 + 1], bank[4 + i % 2][:], AX.X, ALU.max, negate=True)\
                               .then_inc(max_done, 1)
                        dve.wait_ge(max_done, 8 * w + 8)
                        dve.transpose(mrow[:, k % 2].rearrange("p (r i) -> p i r", i=4), mcol[:, k % 2].bitcast(F32)).then_inc(m_turned, 1)

                def values(v, k, pair):
                    if exists(v, UNITS):
                        wait(dve, pv1, 2 * v - 1)
                        dve.tensor_copy(vp[:, k % 2, :, :, 0:HD1],
                                        vc[:, TB * (k % 2):TB * (k % 2) + TB, bass.ds(pair * 8, 8)]
                                        .rearrange("p t (h d) -> p t h d", h=2)).then_inc(vp_ready, 1)

                def period(u, k, pair, quad):
                    q_low(u + 2, k + 2)
                    if k % 2 == 0:
                        split_rope_weights(pair(4), (k // 2) % 2, quad(4))
                    values(u + 1, k + 1, pair(1))
                    maxima(u + 2, k + 2, pair(2))

                for u in range(-3, 6):
                    period(u, u % 4, lambda n, u=u: (u + n) // 2, lambda n, u=u: (u + n) // 4)
                    if u < 0:
                        content_low(u + 4)
                with dve.Fori(1, UNITS // 4 - 2) as g:
                    for k in range(2, 6):
                        period(4 * g + k, k, lambda n, k=k: 2 * g + (k + n) // 2, lambda n, k=k: g + (k + n) // 4)

                def sums(n):
                    b, m = n % 2, n // 2
                    at = slice(b * S, (b + 1) * S)
                    o, d = (num, dnm) if m < KT - 1 else (num3[:, b], dnm3[:, b])
                    lo, hi = (oo_lo[:, m, at], oo_hi[:, m, at]) if m < KT - 1 else (oo3_lo[:, at], oo3_hi[:, at])
                    if m < KT - 1:
                        dve.wait_ge(num_loaded, 64 * (n + 1))
                    else:
                        dve.wait_ge(num3_loaded[b], 64)
                    dve.tensor_tensor(d[:, 0], d[:, 0], d[:, 1], ALU.add).then_inc(o_step, 1)
                    dve.tensor_tensor(o[:, 0], o[:, 0], o[:, 1], ALU.add).then_inc(o_step, 1)
                    dve.wait_ge(o_step, 4 * n + 2)
                    dve.reciprocal(d[:, 1], d[:, 0]).then_inc(o_step, 1)
                    dve.wait_ge(o_step, 4 * n + 3)
                    dve.tensor_tensor(o[:, 0], o[:, 0], d[:, 1], ALU.mult).then_inc(o_step, 1)
                    dve.wait_ge(oo_hi_done, n + 1)
                    dve.tensor_tensor(lo, o[:, 0], hi.bitcast(F32), ALU.subtract).then_inc(oo_split, 1)

                for u in range(UNITS - 6, UNITS):
                    period(u, u % 4, lambda n, u=u: (u + n) // 2, lambda n, u=u: (u + n) // 4)
                    if u > UNITS - 6:
                        sums(u - (UNITS - 5))
                sums(5)

            if True:
                for k in range(KT):
                    dve.wait_ge(wo1_hi_done, k + 1)
                    dve.tensor_tensor(wo1_lo[:, k], wo1[:, k], wo1_hi[:, k].bitcast(F32), ALU.subtract).then_inc(wo1_split, 1)
                sums(6)
                sums(7)
                dve.wait_ge(gate_ready, 4)
                dve.wait_ge(o_copied, UNITS)
                dve.memset(rwT_hi[:].bitcast(F32), 0.0)
                dve.memset(rwT_lo[:].bitcast(F32), 0.0).then_inc(g_const, 1)
                dve.wait_ge(g_loaded, 16 * 12)
                dve.tensor_copy(emap[0:NR], emap_i[0:NR]).then_inc(g_const, 1)
                dve.wait_ge(g_const, 2)
                dve.tensor_scalar(ehot[0:NR], ecol[0:NR], emap[0:NR, 0:1], None, ALU.is_equal).then_inc(g_const, 1)
                for t in range(NT):
                    dve.wait_ge(wo1_mm, t + 1)
                    wait(dve, attn1_added, t - 1)
                    dve.tensor_tensor(og[:, t % 2], bank[t][:], gate[:, 1, t // TB], ALU.mult).then_inc(wo1_gated, 1)
                    if t == 5:
                        norm_stats(3, 0)
                norm_stats(3, 1)
                for i, (hi, lo) in enumerate([*((bwT_hi[:, k], bwT_lo[:, k]) for k in range(KT)),
                                              (laT_hi[:].rearrange("p k n -> p (k n)"), laT_lo[:].rearrange("p k n -> p (k n)")),
                                              (rwT_hi[:, :, 0:NR], rwT_lo[:, :, 0:NR]), (lbT_hi[:], lbT_lo[:])]):
                    dve.wait_ge(g_hi, i + 1)
                    dve.tensor_tensor(lo, g_bank(i), hi.bitcast(F32), ALU.subtract).then_inc(g_lo, 1)
                    if i == KT - 1:
                        norm_rows(3, 0)
                        norm_rows(3, 1)
                norm_split(3, 0)
                norm_split(3, 1)
                step = [0]

                def chain(ins):
                    step[0] += 1
                    ins.then_inc(r_step, 1)
                    dve.wait_ge(r_step, step[0])

                over = lambda v: v.unsqueeze(2).broadcast_to([P, NT, NR])
                dve.wait_ge(r_mm, 1)
                chain(dve.tensor_tensor(lg[:], bank[4][:, 0:NT * 16].rearrange("p (t n) -> p t n", n=16)[:, :, 0:NR],
                                        rbias[:].unsqueeze(1).broadcast_to([P, NT, NR]), ALU.add))
                chain(dve.tensor_reduce(lmax[:], lg[:], AX.X, ALU.max))
                chain(dve.tensor_tensor(lg[:], lg[:], over(lmax[:]), ALU.subtract))
                dve.wait_ge(r_exp, 1)
                chain(dve.tensor_reduce(lsum[:], prob[:], AX.X, ALU.add))
                chain(dve.reciprocal(lrec[:], lsum[:]))
                chain(dve.tensor_tensor(prob[:], prob[:], over(lrec[:]), ALU.mult))
                for t in range(NT):
                    p_n = prob[:, t].unsqueeze(2).broadcast_to([P, NR, NR])
                    p_m = prob[:, t].unsqueeze(1).broadcast_to([P, NR, NR])
                    dve.tensor_tensor(cmpg[:, t], p_m, p_n, ALU.is_gt)
                    e = dve.tensor_tensor(cmpe[:, t], p_m, p_n, ALU.is_equal)
                chain(e)
                for t in range(NT):
                    e = dve.tensor_tensor(cmpe[:, t], cmpe[:, t], before[:], ALU.mult)
                chain(e)
                chain(dve.tensor_tensor(cmpg[:].rearrange("p t n m -> p (t n m)"), cmpg[:].rearrange("p t n m -> p (t n m)"),
                                        cmpe[:].rearrange("p t n m -> p (t n m)"), ALU.add))
                chain(dve.tensor_reduce(rank[:].rearrange("p t n -> p (t n)"), cmpg[:].rearrange("p t n m -> p (t n) m"), AX.X, ALU.add))
                dve.memset(kept[:], 0.0)
                chain(dve.tensor_scalar(rank[:], rank[:], float(E1), None, ALU.is_lt))
                dve.tensor_tensor(kept[:, :, 0:NR], rank[:], prob[:], ALU.mult).then_inc(r_kept, 1)
                for b in range(B):
                    dve.wait_ge(r_wexp, b + 1)
                    dve.wait_ge(r_hmm, b + 1)
                    dve.tensor_tensor(lh[:, b * S:(b + 1) * S], bank[5 + b][:], wexp[:, b * S:(b + 1) * S], ALU.mult).then_inc(r_hfull, 1)
                for b in range(B):
                    dve.wait_ge(r_hhi, b + 1)
                    dve.tensor_tensor(lh_lo[:, b * S:(b + 1) * S], lh[:, b * S:(b + 1) * S], lh_hi[:, b * S:(b + 1) * S].bitcast(F32),
                                      ALU.subtract).then_inc(r_hlo, 1)
                for t in range(NT):
                    dve.wait_ge(g_mm, t + 1)
                    dve.tensor_tensor(gu[:, t % 2], bank[t][:], bbias[:], ALU.add).then_inc(g_bias, 1)
                    dve.wait_ge(g_bias, t + 1)
                    wait(dve, g_added, t - 1)
                    dve.tensor_tensor(gg[:, t % 2], gu[:, t % 2], gate[:, 2, t // TB], ALU.mult).then_inc(g_gated, 1)

        @block.tensor
        def _(pe):
            def mm3(ps, pairs, inc=None):
                n = len(pairs)
                for i, (lh_, ll, rh, rl) in enumerate(pairs):
                    pe.matmul(ps, lh_, rh, start=(i == 0), stop=False)
                    pe.matmul(ps, lh_, rl, start=False, stop=False)
                    e = pe.matmul(ps, ll, rh, start=False, stop=(i == n - 1))
                if inc is not None:
                    e.then_inc(inc, 1)

            def mod(l, c):
                i = 6 * l + c
                pe.wait_ge(wm_loaded[i % 3], 16 * (i // 3 + 1))
                wait(pe, mod_row, i - 1)
                for k in range(KT):
                    e = pe.matmul(bank[2 + c % 2][32 * k:32 * k + 32, :], silu[:, l, k], WM[l][:, i % 3, k], start=True, stop=True)
                e.then_inc(mod_mm, 1)

            def mod_use(l, c):
                pe.wait_ge(mod_row, 6 * l + c + 1)
                rows = MODROW[l][:, ROW_SLOT[c]]
                if c in GATE_CHUNKS:
                    w = GATE_CHUNKS.index(c)
                    e = pe.matmul(gate_sums(l)[32 * w:32 * w + 32], rowsum[:], rows, start=True, stop=True)
                else:
                    for k in range(KT):
                        at = 8 * (c % 3) + 2 * k
                        e = pe.matmul(col_bank(l, c // 3)[:, at:at + 2], rows[:, k * P:(k + 1) * P], rowsum[:, 0:B], start=True, stop=True)
                e.then_inc(mod_used, 1)

            def broadcast_gate(l, w):
                pe.wait_ge(gate_rows, l + 1)
                r = slice(32 * w, 32 * w + 32)
                for b in range(B):
                    e = pe.matmul(bank[GATE_BANKS[2 * l + w][b]][:], sel[r, b], GROWS[l][r], start=True, stop=True)
                e.then_inc(gate_bc, 1)

            def norm(ph, b):
                for t in range(TB * b, TB * b + TB):
                    pe.wait_ge(ln_norm, NT * ph + t + 1)
                    for k in range(KT):
                        e = pe.transpose(norm_bank(KT * b + k)[:, (t % TB) * P:(t % TB + 1) * P], NORM[ph][0][:, t, k * P:(k + 1) * P],
                                         ident[:])
                    e.then_inc(ln_trans, 1)

            pe.wait_ge(ident_loaded, 48)
            pe.wait_ge(silu_step, 3)
            mod(0, 0)
            mod(0, 1)
            mod_use(0, 0)
            mod_use(0, 1)
            pe.wait_ge(col_ready, 1)
            norm(0, 0)
            norm(0, 1)

            def project(half, name, b, n):
                e = TURNS * half + TURN[name]
                ps = bank[6 + (b + TURN[name]) % 2]
                wait(pe, proj_free, e - 1)
                if name == "Vt":
                    pe.wait_ge(proj_free, TURNS * half + TURN["V"] + 1)
                    for t in range(TB):
                        ins = pe.transpose(ps[:, t * P:(t + 1) * P], vT[:, t * P:(t + 1) * P], ident[:])
                    ins.then_inc(proj_done, 1)
                    return
                m = W_TILE[name]
                pe.wait_ge(w_split, 6 * n + m + 1)
                at = slice(b * S, (b + 1) * S)
                mm3(ps[:], [(w_hi[:, m, k], w_lo[:, m, k], hT_hi[:, k, at], hT_lo[:, k, at]) for k in range(KT)], proj_done)

            def scores(slot, half, b, qb):
                if qb == 0:
                    pe.wait_ge(rope_split, 5 * half + 5)
                wait(pe, masked0, slot)
                c = slice(P, 2 * P) if qb == 0 else slice(0, 2 * P)
                keys = slice(0, P) if qb == 0 else slice((qb - 1) * P, (qb + 1) * P)
                for h in range(GQ):
                    q = slice(qb * P, (qb + 1) * P)
                    ps = bank[h // 2][:, (h % 2) * 2 * P:(h % 2 + 1) * 2 * P]
                    mm3(ps[:, c], [(qT_hi[b][:, h, q], qT_lo[b][:, h, q], kT_hi[:, b, keys], kT_lo[:, b, keys])],
                        scores0 if h == GQ - 1 else None)

            def transposes(slot, qb):
                pe.wait_ge(probs0, slot + 1)
                wait(pe, pT_split, slot)
                for kb in range(1 if qb == 0 else 0, 2):
                    for h in range(GQ):
                        e = pe.transpose(bank[2 + kb][:, h * P:(h + 1) * P], probs[:, qb % 2, h, kb * P:(kb + 1) * P], ident[:])
                e.then_inc(trans0, 1)

            def sum_values(slot, half, b, qb):
                pe.wait_ge(pT_split, slot + 1)
                if qb == 0:
                    pe.wait_ge(proj_free, TURNS * half + TURN["Vt"] + 1)
                wait(pe, oT_split, slot)
                mm3(bank[4][:], [(v_hi[:, b, qb - 1 + kb], v_lo[:, b, qb - 1 + kb], pT_hi[:, kb], pT_lo[:, kb])
                                 for kb in range(1 if qb == 0 else 0, 2)], pv0)

            def project_out(slot, n):
                pe.wait_ge(oT_split, slot + 1)
                pe.wait_ge(wo_split, n + 1)
                wait(pe, wo_gated, slot)
                mm3(bank[5][:], [(oT_hi[:, h], oT_lo[:, h], wo_hi[:, h], wo_lo[:, h]) for h in range(GQ)], wo_mm)

            def kv_head(n, last):
                for b in range(B):
                    half, slot, nb = 2 * n + b, 8 * n + 4 * b, 1 - b
                    more = not (last and b == 1)
                    transposes(slot, 0)
                    scores(slot + 1, half, b, 1)
                    if more:
                        project(half + 1, "Q0", nb, n + b)
                    if isinstance(n, int) and n == 0 and b == 0:
                        broadcast_gate(0, 0)
                        pe.wait_ge(gate_ready, 1)
                    sum_values(slot, half, b, 0)
                    if more:
                        project(half + 1, "Q1", nb, n + b)
                    transposes(slot + 1, 1)
                    scores(slot + 2, half, b, 2)
                    if more:
                        project(half + 1, "Vt", nb, n + b)
                    project_out(slot, n)
                    sum_values(slot + 1, half, b, 1)
                    if more:
                        project(half + 1, "Q2", nb, n + b)
                    transposes(slot + 2, 2)
                    scores(slot + 3, half, b, 3)
                    if more:
                        project(half + 1, "Q3", nb, n + b)
                    project_out(slot + 1, n)
                    sum_values(slot + 2, half, b, 2)
                    transposes(slot + 3, 3)
                    if not last:
                        project(half + 2, "K", b, n + 1)
                    project_out(slot + 2, n)
                    if more:
                        scores(slot + 4, half + 1, nb, 0)
                    sum_values(slot + 3, half, b, 3)
                    if not last:
                        project(half + 2, "V", b, n + 1)
                    project_out(slot + 3, n)

            wait_norm(pe, 0, 0)
            for name in TURN:
                project(0, name, 0, 0)
            wait_norm(pe, 0, 1)
            project(1, "K", 1, 0)
            mod(0, 2)
            mod(0, 3)
            mod_use(0, 2)
            mod(0, 4)
            mod_use(0, 3)
            mod(0, 5)
            mod_use(0, 4)
            mod_use(0, 5)
            scores(0, 0, 0, 0)
            project(1, "V", 1, 0)
            pe.wait_ge(col_ready, 2)
            kv_head(0, False)
            with pe.Fori(1, HKV - 1) as n:
                kv_head(n, False)
            kv_head(HKV - 1, True)

            pe.wait_ge(f_loaded, 16 * 9)
            pe.wait_ge(proj_free, TURNS * B * HKV)
            for t in range(2):
                for k in range(KT):
                    e = pe.transpose(bank[6 + t][:, k * P:(k + 1) * P], fbf[:, k, t * P:(t + 1) * P], ident[:])
                e.then_inc(f_tr, 1)
            pe.wait_ge(f_cw, 1)
            for t in range(2):
                e = pe.matmul(bank[4][:, t:t + 1], expand[:, t * P:(t + 1) * P], fcw[:], start=True, stop=True)
            e.then_inc(f_er_mm, 1)

            def merge(k):
                for t in range(2):
                    pe.matmul(bank[k][:], fa_s[:, t, k * P:(k + 1) * P], fbfT[:, t], start=(t == 0), stop=False)
                for o in range(KT):
                    e = pe.matmul(bank[k][:, o * P:(o + 1) * P], fw[:, o, k * P:(k + 1) * P], ident[:], start=False, stop=(o == KT - 1))
                e.then_inc(f_mg, 1)

            mod(1, 0)
            mod(1, 1)
            pe.wait_ge(wo_gated, NT * HKV)
            mod_use(1, 0)
            mod(1, 2)
            mod_use(1, 1)
            mod(1, 3)
            pe.wait_ge(f_as, 2)
            pe.wait_ge(f_trs, 2)
            merge(0)
            merge(1)
            mod(1, 4)
            pe.wait_ge(f_er, 1)
            mod_use(1, 3)
            mod(1, 5)
            mod_use(1, 4)
            pe.wait_ge(col_ready, 4)
            norm(1, 0)
            pe.wait_ge(mod_row, 12)
            merge(2)
            merge(3)
            pe.wait_ge(f_split, KT)
            norm(1, 1)

            def ffn(t):
                wait(pe, f_bias, t - 3)
                at = slice(t * P, (t + 1) * P)
                mm3(bank[4 + t % 4][:], [(hT_hi[:, k, at], hT_lo[:, k, at], fw_hi[:, k], fw_lo[:, k]) for k in range(KT)], f_mm)

            wait_norm(pe, 1, 0)
            ffn(0)
            wait_norm(pe, 1, 1)
            broadcast_gate(0, 1)
            mod_use(1, 2)
            mod_use(1, 5)
            ffn(1)
            ffn(2)
            ffn(3)
            broadcast_gate(1, 0)
            ffn(4)
            ffn(5)
            pe.wait_ge(gate_ready, 2)
            broadcast_gate(1, 1)
            ffn(6)
            ffn(7)

            if True:
                pe.wait_ge(f_bias, NT)
                norm(2, 0)
                pe.wait_ge(gate_ready, 4)
                norm(2, 1)
                pe.wait_ge(pre_split, 2)
                for b in range(B):
                    wait_norm(pe, 2, b)
                    at = slice(b * S, (b + 1) * S)
                    mm3(bank[4 + b][:], [(dn_hi[:, k], dn_lo[:, k], hT_hi[:, k, at], hT_lo[:, k, at]) for k in range(KT)], lat_mm)
                for b in range(B):
                    at = slice(b * S, (b + 1) * S)
                    mm3(bank[6 + b][:], [(kr_hi[:, k], kr_lo[:, k], hT_hi[:, k, at], hT_lo[:, k, at]) for k in range(KT)], kr_mm)

                def content(m):
                    for b in range(B):
                        for w in range(2):
                            i = 2 * b + w
                            rows = slice(LAT * w, LAT * w + LAT)
                            wait(pe, c_split, 4 * (m - 1) + i + 1 if m else 0)
                            pe.matmul(bank[i][:], up[rows, m * P:(m + 1) * P], lat[rows, b * S:(b + 1) * S],
                                      start=True, stop=True).then_inc(c_mm, 1)

                pe.wait_ge(lat_ready, B)
                content(0)
                for t in range(NT):
                    wait(pe, vc_ready, t - 1)
                    pe.matmul(bank[4 + t % 2][:], lat[LAT:P, t * P:(t + 1) * P], vup[LAT:P], start=True, stop=True).then_inc(vc_mm, 1)
                pe.wait_ge(vc_ready, NT)
                pe.wait_ge(kr_split, B)

                def rope_queries(z, k, pair, ks, first, last):
                    if exists(z, UNITS):
                        par, b = pair % 2 if isinstance(pair, int) else None, k % 2
                        par = (k % 4) // 2
                        if first:
                            wait(pe, q1_split, z)
                            pe.wait_ge(wr_split, pair + 1)
                        at = slice(b * S, (b + 1) * S)
                        for kk in ks:
                            pe.matmul(bank[6][:], wr_hi[:, par, kk], hT_hi[:, kk, at], start=(kk == 0), stop=False)
                            pe.matmul(bank[6][:], wr_hi[:, par, kk], hT_lo[:, kk, at], start=False, stop=False)
                            e = pe.matmul(bank[6][:], wr_lo[:, par, kk], hT_hi[:, kk, at], start=False, stop=(kk == KT - 1))
                        if last:
                            e.then_inc(qr_mm, 1)

                def max_scores(w, k, i, use):
                    if exists(w, UNITS):
                        h, b = i // 4, k % 2
                        if i == 0:
                            pe.wait_ge(q2_hi, w + 1)
                            pe.wait_ge(mc_loaded[b], 64 * use + 64)
                        wait(pe, max_done, 8 * w + i - 1)
                        pe.matmul(bank[4 + i % 2][:], q2[:, k % 4, h, i % 4:S:4], km[:, b, h], start=True, stop=True).then_inc(max_mm, 1)

                def scores1_slot(u, k, s, use):
                    if exists(u, UNITS):
                        h, kb = SLOTS[s]
                        if s == 0:
                            pe.wait_ge(q1_hi, u + 1)
                            pe.wait_ge(q1_split, u + 1)
                            pe.wait_ge(m_loaded[k % 2], 32 * use + 32)
                            pe.wait_ge(k2c_loaded[k % 2], 32 * use + 32)
                        pe.wait_ge(exp1, 8 * u + s + 1)
                        t = slice(kb * P, (kb + 1) * P)
                        pe.matmul(bank[s % 4][:], k1[:, k % 2, t], q1[:, k % 4, h], start=True, stop=False)
                        pe.matmul(bank[s % 4][:], k2[:, k % 2, h, t], q2[:, k % 4, h], start=False, stop=True).then_inc(scores1, 1)

                def sum_slots(u, k, c):
                    if exists(u, UNITS):
                        pe.wait_ge(exp1, 8 * u + 4 * c + 8)
                        if c == 0:
                            pe.wait_ge(vp_ready, u + 1)
                            wait(pe, o_copied, u)
                        for s in range(4 * c, 4 * c + 4):
                            h, kb = SLOTS[s]
                            j = 2 * h + kb % 2
                            e = pe.matmul(bank[7][32 * j:32 * j + 32, :], vp[:, k % 2, kb, h], pT[:, s], start=(c == 0), stop=(c == 1))
                        e.then_inc(pv1, 1)

                pe.wait_ge(ones_set, 64)
                pe.sem_inc(pv1, 1)

                def period(u, k, pair):
                    scores1_slot(u, k, 0, pair(0))
                    scores1_slot(u, k, 1, pair(0))
                    sum_slots(u - 1, k - 1, 1)
                    scores1_slot(u, k, 2, pair(0))
                    max_scores(u + 2, k + 2, 0, pair(2))
                    scores1_slot(u, k, 3, pair(0))
                    max_scores(u + 2, k + 2, 1, pair(2))
                    scores1_slot(u, k, 4, pair(0))
                    rope_queries(u + 3, k + 3, pair(3), [0], True, False)
                    max_scores(u + 2, k + 2, 2, pair(2))
                    scores1_slot(u, k, 5, pair(0))
                    rope_queries(u + 3, k + 3, pair(3), [1], False, False)
                    max_scores(u + 2, k + 2, 3, pair(2))
                    sum_slots(u, k, 0)
                    max_scores(u + 2, k + 2, 4, pair(2))
                    scores1_slot(u, k, 6, pair(0))
                    rope_queries(u + 3, k + 3, pair(3), [2], False, False)
                    max_scores(u + 2, k + 2, 5, pair(2))
                    scores1_slot(u, k, 7, pair(0))
                    max_scores(u + 2, k + 2, 6, pair(2))
                    rope_queries(u + 3, k + 3, pair(3), [3], False, True)
                    max_scores(u + 2, k + 2, 7, pair(2))

                for u in range(-3, 6):
                    period(u, u % 4, lambda n, u=u: (u + n) // 2)
                    if u < 0:
                        content(u + 4)
                    if u == -1:
                        pe.wait_ge(c_split, 4 * KT)
                with pe.Fori(1, UNITS // 4 - 2) as g:
                    for k in range(2, 6):
                        period(4 * g + k, k, lambda n, k=k: 2 * g + (k + n) // 2)
                for u in range(UNITS - 6, UNITS + 1):
                    period(u, u % 4, lambda n, u=u: (u + n) // 2)

            pe.wait_ge(o_copied, UNITS)
            pe.wait_ge(wo1_split, KT)
            pe.wait_ge(oo_split, 6)
            for t in range(NT):
                at = slice(t * P, (t + 1) * P)
                for k in range(KT - 1):
                    pe.matmul(bank[t][:], oo_hi[:, k, at], wo1_hi[:, k], start=(k == 0), stop=False)
                    pe.matmul(bank[t][:], oo_hi[:, k, at], wo1_lo[:, k], start=False, stop=False)
                    pe.matmul(bank[t][:], oo_lo[:, k, at], wo1_hi[:, k], start=False, stop=False)
            for t in range(NT):
                at = slice(t * P, (t + 1) * P)
                pe.wait_ge(oo_split, 7 + t // TB)
                pe.matmul(bank[t][:], oo3_hi[:, at], wo1_hi[:, KT - 1], start=False, stop=False)
                pe.matmul(bank[t][:], oo3_hi[:, at], wo1_lo[:, KT - 1], start=False, stop=False)
                pe.matmul(bank[t][:], oo3_lo[:, at], wo1_hi[:, KT - 1], start=False, stop=True).then_inc(wo1_mm, 1)

            pe.wait_ge(g_loaded, 16 * 12)
            for i in range(KT + 3):
                if i < KT:
                    pe.wait_ge(wo1_gated, i + 1)
                    for o in range(KT):
                        e = pe.transpose(bank[i][:, o * P:(o + 1) * P], bw[:, o, i * P:(i + 1) * P], ident[:])
                else:
                    pe.wait_ge(g_lo, i - 3)
                    for k in range(KT):
                        if i == KT:
                            e = pe.transpose(bank[0][:, k * P:(k + 1) * P], la[:, k * P:(k + 1) * P], ident[:])
                        elif i == KT + 1:
                            e = pe.transpose(bank[1][:, k * P:k * P + NR], rw[0:NR, k * P:(k + 1) * P], ident[0:NR, 0:NR])
                        else:
                            e = pe.transpose(bank[2][:, k * P:(k + 1) * P], lb[:, k].rearrange("p e r -> p (e r)"), ident[:])
                e.then_inc(g_tr, 1)
            pe.wait_ge(wo1_gated, NT)
            norm(3, 0)
            pe.wait_ge(g_lo, KT + 3)
            norm(3, 1)

            for b in range(B):
                wait_norm(pe, 3, b)
                for t in range(TB * b, TB * b + TB):
                    at = slice(t * P, (t + 1) * P)
                    mm3(bank[4][:, 16 * t:16 * t + 16], [(hT_hi[:, k, at], hT_lo[:, k, at], rwT_hi[:, k, 0:16], rwT_lo[:, k, 0:16])
                                                         for k in range(KT)], r_mm if t == NT - 1 else None)
            for b in range(B):
                at = slice(b * S, (b + 1) * S)
                mm3(bank[5 + b][:], [(laT_hi[:, k], laT_lo[:, k], hT_hi[:, k, at], hT_lo[:, k, at]) for k in range(KT)], r_hmm)

            def base(t):
                at = slice(t * P, (t + 1) * P)
                for k in range(KT):
                    pe.matmul(bank[t][:], hT_hi[:, k, at], bwT_hi[:, k], start=(k == 0), stop=False)
                    pe.matmul(bank[t][:], hT_hi[:, k, at], bwT_lo[:, k], start=False, stop=False)
                    pe.matmul(bank[t][:], hT_lo[:, k, at], bwT_hi[:, k], start=False, stop=False)

            def lora(t):
                at = slice(t * P, (t + 1) * P)
                pe.matmul(bank[t][:], lh_hi[:, at], lbT_hi[:], start=False, stop=False)
                pe.matmul(bank[t][:], lh_hi[:, at], lbT_lo[:], start=False, stop=False)
                pe.matmul(bank[t][:], lh_lo[:, at], lbT_hi[:], start=False, stop=True).then_inc(g_mm, 1)

            for t in range(TB):
                base(t)
            pe.wait_ge(r_kept, 1)
            for b in range(B):
                for t in range(TB):
                    e = pe.transpose(bank[(7, 4)[b]][0:16, t * P:(t + 1) * P], kept[:, TB * b + t], ident[:])
                e.then_inc(r_ktr, 1)
            pe.wait_ge(g_const, 3)
            for b in range(B):
                pe.wait_ge(r_ktc, b + 1)
                pe.matmul(bank[(7, 4)[b]][:], ehot[0:NR], keptT[0:NR, b * S:(b + 1) * S], start=True, stop=True).then_inc(r_wmm, 1)
            pe.wait_ge(r_hlo, B)
            for t in range(TB):
                lora(t)
            for t in range(TB, NT):
                base(t)
                lora(t)


def shape_constants():
    import numpy as np

    half = HD // 2
    inv_freq = np.float32(10000.0) ** (-np.arange(half, dtype=np.float32) / np.float32(half))
    ang = (np.arange(S, dtype=np.float32)[:, None] * inv_freq[None, :]).T.astype(np.float32)
    cos, sin = np.cos(ang), np.sin(ang)
    i, j = np.arange(P)[:, None], np.arange(P)[None, :]
    n = np.arange(NR)
    return {
        "identity": np.eye(P, dtype=np.float32),
        "rope_cos": np.concatenate([cos, cos]).astype(np.float32),
        "rope_sin": np.concatenate([sin, -sin]).astype(np.float32),
        "window_mask": np.where(np.concatenate([j > i, j <= i], axis=1), 0.0, MASKED).astype(np.float32),
        "lora_expand": (np.arange(16)[:, None] == np.arange(ER0)[None, :] // 16).astype(np.float32),
        "batch_rows": np.broadcast_to((np.arange(P)[:, None] % 32 == np.arange(B)[None, :])[:, :, None], (P, B, P)).reshape(P, B * P)
        .astype(np.float32),
        "batch_columns": ((np.arange(P)[:, None] % 32 == np.arange(32)[None, :]) & (np.arange(32)[None, :] < B)).astype(np.float32),
        "expert_of_column": np.broadcast_to(np.arange(P) // R1, (16, P)).astype(np.float32),
        "entry_before": (n[None, :] < n[:, None]).astype(np.float32),
    }


_INS = ["L0_attn_x", "L0_attn_wq", "L0_attn_wk", "L0_attn_wv", "L0_attn_wo", "L0_ffn_W", "L0_ffn_bias", "L0_ffn_A", "L0_ffn_Bf",
        "L0_ffn_coeffs", "L0_ffn_scales", "L0_c", "L0_wmod", "L1_attn_Wq_down", "L1_attn_Wq_up", "L1_attn_Wq_rope",
        "L1_attn_Wkv_down", "L1_attn_Wk_up", "L1_attn_Wv_up", "L1_attn_Wk_rope", "L1_attn_Wo", "L1_ffn_base_W", "L1_ffn_base_b",
        "L1_ffn_router_W", "L1_ffn_router_b", "L1_ffn_A", "L1_ffn_B", "L1_ffn_expert_map", "L1_c", "L1_wmod"]


def kernel(**inputs):
    import numpy as np
    import concourse.bacc as bacc
    from concourse.bass_utils import run_bass_kernel_spmd

    nc = bacc.Bacc("TRN2", target_bir_lowering=False, num_devices=1)
    arrays = {name: np.ascontiguousarray(inputs[name]) for name in _INS}
    arrays.update(shape_constants())
    aps = {name: nc.dram_tensor(f"in_{name}", v.shape, mybir.dt.from_np(v.dtype), kind="ExternalInput").ap() for name, v in arrays.items()}
    out = nc.dram_tensor("out_x", (B, S, D), F32, kind="ExternalOutput").ap()
    adaln_two_layers(nc, aps, out)
    r = run_bass_kernel_spmd(nc, [{f"in_{name}": v for name, v in arrays.items()}], core_ids=[0])
    return r.results[0]["out_x"]
```

```python
from contextlib import ExitStack

import concourse.bass as bass
from concourse import mybir

F32 = mybir.dt.float32
F32R = mybir.dt.float32r
I32 = mybir.dt.int32
ALU = mybir.AluOpType
ACT = mybir.ActivationFunctionType
AX = mybir.AxisListType

P = 128
B, S, D = 2, 512, 512
KT = D // P
TB = S // P
NT = B * TB
EPS = 1e-5

HQ, HKV, HD = 32, 8, 128
GQ = HQ // HKV
NPROJ = GQ + 2
TURNS = NPROJ + 1
TURN = {"K": 0, "V": 1, "Q0": 2, "Q1": 3, "Vt": 4, "Q2": 5, "Q3": 6}
MASKED = -1e30
ER0 = 256

H1, HD1, LAT, ROPE = 128, 4, 64, 64
PAIRS = H1 // 2
UNITS = PAIRS * B
EARLY = B * (KT - 1)
TAIL = UNITS - 10
CR = 4 * HD1
SLOTS = [(0, 0), (0, 1), (1, 0), (1, 1), (0, 2), (0, 3), (1, 2), (1, 3)]
E1, R1 = 8, 16
F_PAD = 256
G_PAD = 1280
W_PAD = 720
NR = 2 * E1 - 1
SCALING = 2.0


def exists(v, n):
    return not isinstance(v, int) or 0 <= v < n


def wait(eng, sem, v):
    if not isinstance(v, int) or v > 0:
        eng.wait_ge(sem, v)


def adaln_two_layers(nc, a, out):
    x_in, out_t = (v.rearrange("b (t p) d -> p (b t) d", p=P) for v in (a["L0_attn_x"], out))
    scratch = lambda name, shape: nc.dram_tensor(name, shape, F32, kind="Internal").ap()
    qc_d = scratch("qc_d", (B, H1, HD1, 2, S))
    kc_d = scratch("kc_d", (B, H1, 2, HD1, S))
    o_d = scratch("o_d", (B, H1, 2, 8, S))

    ctx = ExitStack()
    with ctx:
        def sbuf_in(stack):
            return lambda name, shape, dt=F32: stack.enter_context(nc.sbuf_tensor(name, shape, dt))

        sb = sbuf_in(ctx)
        sem = lambda name: ctx.enter_context(nc.semaphore(name))
        bank = [ctx.enter_context(nc.psum_tensor(f"bank{i}", [P, 512], F32)) for i in range(8)]

        x = sb("x", [P, NT, D])
        hT_hi = sb("hT_hi", [P, KT, B * S], F32R)
        hT_lo = sb("hT_lo", [P, KT, B * S], F32R)
        ident = sb("ident", [P, P])
        cT = sb("cT", [P, 2, B, KT])
        silu_e = sb("silu_e", [P, 2, B, KT])
        silu_d = sb("silu_d", [P, 2, B, KT])
        rowsum = sb("rowsum", [P, 32])
        with ExitStack() as early:
            sbe = sbuf_in(early)
            silu = sbe("silu", [P, 2, KT, 32])
            sel = sbe("sel", [P, B, P])
            grows0 = sbe("grows0", [2 * 32, D])
        dnm1 = sb("dnm1", [P, 2, S])
        modc = sb("modc", [P, 2, 4, KT, B])
        stats = sb("stats", [P, NT, 6])
        mean_var = sb("mean_var", [P, NT, 2])
        var_eps = sb("var_eps", [P, NT])
        std = sb("std", [P, NT])
        rstd = sb("rstd", [P, NT])

        l0 = ctx.enter_context(ExitStack())
        sb0 = sbuf_in(l0)
        wo_hi = sb0("wo_hi", [P, GQ, D], F32R)
        wo_lo = sb0("wo_lo", [P, GQ, D], F32R)
        rope_cos = sb0("rope_cos", [P, S])
        rope_sin = sb0("rope_sin", [P, S])
        window = sb0("window", [P, 2 * P])
        kT_hi = sb0("kT_hi", [P, B, S], F32R)
        kT_lo = sb0("kT_lo", [P, B, S], F32R)
        v_hi = sb0("v_hi", [P, B, TB, HD], F32R)
        v_lo = sb0("v_lo", [P, B, TB, HD], F32R)
        oT_hi = sb0("oT_hi", [P, GQ, P], F32R)
        oT_lo = sb0("oT_lo", [P, GQ, P], F32R)
        gate_a0 = sb0("gate_a0", [P, B, D])
        vT = sb0("vT", [P, S])
        gated = sb0("gated", [P, D])
        st_kv = sb0("st_kv", [P, 2, KT, HD])
        st_q = sb0("st_q", [P, KT, GQ * HD])
        st_wo = sb0("st_wo", [P, GQ, D])
        w_hi = sb0("w_hi", [P, NPROJ, KT, HD], F32R)
        w_lo = sb0("w_lo", [P, NPROJ, KT, HD], F32R)
        rmax = sb0("rmax", [P, 2, GQ])
        nmax = sb0("nmax", [P, 2, GQ])
        den = sb0("den", [P, 2, GQ])
        rden = sb0("rden", [P, 2, GQ])
        with ExitStack() as pro:
            sbp = sbuf_in(pro)
            xn0 = sbp("xn0", [P, NT, D])
            full0 = sbp("full0", [P, 4, S])
            wm0 = sbp("wm0", [P, 3, KT, D])
            modrow0 = sbp("modrow0", [P, 4, D])
        rope_a = sb0("rope_a", [P, 2, S])
        rope_b = sb0("rope_b", [P, 2, S])
        bq0_hi = sb0("bq0_hi", [P, GQ, S], F32R)
        bq0_lo = sb0("bq0_lo", [P, GQ, S], F32R)
        bq1_hi = sb0("bq1_hi", [P, GQ, S], F32R)
        bq1_lo = sb0("bq1_lo", [P, GQ, S], F32R)
        probs = sb0("probs", [P, 2, GQ, 2 * P])
        pT_hi = sb0("pT_hi", [P, 2, GQ * P], F32R)
        pT_lo = sb0("pT_lo", [P, 2, GQ * P], F32R)
        qT_hi, qT_lo = (bq0_hi, bq1_hi), (bq0_lo, bq1_lo)
        l0.close()

        gate = sb("gate", [P, 3, B, D])

        pre = ctx.enter_context(ExitStack())
        sbq = sbuf_in(pre)
        dn = sbq("dn", [P, KT, P])
        kr = sbq("kr", [P, KT, P])
        dn_hi = sbq("dn_hi", [P, KT, P], F32R)
        dn_lo = sbq("dn_lo", [P, KT, P], F32R)
        kr_hi = sbq("kr_hi", [P, KT, P], F32R)
        kr_lo = sbq("kr_lo", [P, KT, P], F32R)
        up = sbq("up", [P, D])
        vup = sbq("vup", [P, D])
        lat = sbq("lat", [P, B * S])
        with ExitStack() as rows1:
            modrow1 = sbuf_in(rows1)("modrow1", [P, 4, D])
        c_hi = sbq("c_hi", [P, 4, S], F32R)
        c_lo = sbq("c_lo", [P, 4, S], F32R)

        f0 = ctx.enter_context(ExitStack())
        sbf = sbuf_in(f0)
        sbf("f_pad", [P, F_PAD])
        fw = sbf("fw", [P, KT, D])
        fbf = sbf("fbf", [P, KT, ER0])
        fa = sbf("fa", [P, 2, D])
        fco = sbf("fco", [16, 2])
        fcw = sbf("fcw", [16, 1])
        fer = sbf("fer", [P, 2])
        expand = sbf("expand", [16, ER0])
        sbf("w_pad", [P, W_PAD])
        wm1 = sbf("wm1", [P, 3, KT, D])
        xn1 = sbf("xn1", [P, NT, D])
        full1 = sbf("full1", [P, 4, S])
        fbias = sbf("fbias", [P, D])
        fa_s = sbf("fa_s", [P, 2, D])
        fbfT = sbf("fbfT", [P, 2, D])
        grows1 = sbf("grows1", [2 * 32, D])
        gsign1 = sbf("gsign1", [2 * 32, D])
        fw_hi = sbf("fw_hi", [P, KT, D], F32R)
        fw_lo = sbf("fw_lo", [P, KT, D], F32R)
        fu = xn1[:, NT - 2:NT]
        fg = sbf("fg", [P, 2, D])
        f0.close()

        l1 = ctx.enter_context(ExitStack())
        sb1 = sbuf_in(l1)
        sb1("l_pad", [P, F_PAD])
        k2 = sb1("k2", [P, B, 2, S], F32R)
        km = sb1("km", [P, B, 2, S], F32R)
        q2 = sb1("q2", [P, 4, 2, S], F32R)
        vp = sb1("vp", [P, 2, TB, 2, 32])
        mcol = sb1("mcol", [P, 2, 4, 32], F32R)
        wst = sb1("wst", [P, 2, KT, P])
        mrow = sb1("mrow", [P, 2, 4 * 32])
        k1 = sb1("k1", [P, B, S], F32R)
        vc = sb1("vc", [P, NT, H1 * HD1])
        q1 = sb1("q1", [P, 4, 2, S], F32R)
        pT = sb1("pT", [P, 8, S])
        wr_hi = sb1("wr_hi", [P, 2, KT, P], F32R)
        wr_lo = sb1("wr_lo", [P, 2, KT, P], F32R)
        ost = sb1("ost", [P, 2, S])
        l1.close()
        pre.close()

        f1 = ctx.enter_context(ExitStack())
        sbg = sbuf_in(f1)
        oo_hi = sbg("oo_hi", [P, KT - 1, B * S], F32R)
        oo_lo = sbg("oo_lo", [P, KT - 1, B * S], F32R)
        num0 = sbg("num0", [P, 2, S])
        dnm0 = sbg("dnm0", [P, 2, S])
        num1 = sbg("num1", [P, 2, S])
        oo3_hi = sbg("oo3_hi", [P, B * S], F32R)
        oo3_lo = sbg("oo3_lo", [P, B * S], F32R)
        og = sbg("og", [P, 2, D])
        f1.close()
        wo1_hi, wo1_lo = hT_hi[:, :, 0:D], hT_hi[:, :, D:2 * D]
        SUMS = ((num0, dnm0), (num1, dnm1))

        g1 = ctx.enter_context(ExitStack())
        sbh = sbuf_in(g1)
        xn2 = sbh("xn2", [P, NT, D])
        full2 = sbh("full2", [P, 4, S])
        lg = sbh("lg", [P, NT, NR])
        lmax = sbh("lmax", [P, NT])
        lsum = sbh("lsum", [P, NT])
        lrec = sbh("lrec", [P, NT])
        prob = sbh("prob", [P, NT, NR])
        cmpg = sbh("cmpg", [P, NT, NR, NR])
        cmpe = sbh("cmpe", [P, NT, NR, NR])
        rank = sbh("rank", [P, NT, NR])
        kept = sbh("kept", [P, NT, 16])
        lpart = sbh("lpart", [P, B * S])
        keptT = sbh("keptT", [16, B * S])
        wexp = sbh("wexp", [P, B * S])
        lh = sbh("lh", [P, B * S])
        lh_hi = sbh("lh_hi", [P, B * S], F32R)
        lh_lo = sbh("lh_lo", [P, B * S], F32R)
        gu = sbh("gu", [P, 2, D])
        gg = sbh("gg", [P, 2, D])
        sbh("g_pad", [P, G_PAD])
        bw = sbh("bw", [P, KT, D])
        bwT_hi = sbh("bwT_hi", [P, KT, D], F32R)
        bwT_lo = sbh("bwT_lo", [P, KT, D], F32R)
        la = sbh("la", [P, D])
        laT_hi = sbh("laT_hi", [P, KT, P], F32R)
        laT_lo = sbh("laT_lo", [P, KT, P], F32R)
        rw = sbh("rw", [16, D])
        rwT = sbh("rwT", [P, KT, 32])
        lb = sbh("lb", [P, KT, E1, R1])
        lbT_hi = sbh("lbT_hi", [P, D], F32R)
        lbT_lo = sbh("lbT_lo", [P, D], F32R)
        bbias = sbh("bbias", [P, D])
        rbias = sbh("rbias", [P, NR])
        emap_i = sbh("emap_i", [16, 1], I32)
        emap = sbh("emap", [16, 1])
        ecol = sbh("ecol", [16, P])
        ehot = sbh("ehot", [16, P])
        before = sbh("before", [P, NR, NR])
        g1.close()

        NORM = [(xn0, full0, 0, 0), (xn1, full1, 0, 2), (xn1, full1, 1, 0), (xn2, full2, 1, 2)]
        WM, MODROW, ROW_SLOT = (wm0, wm1), (modrow0, modrow1), (0, 1, 2, 0, 1, 3)
        GROWS, GSIGN = (grows0, grows1), (gated, gsign1)
        GATE_CHUNKS = (2, 5)

        x_loaded = [sem(f"x_loaded{b}") for b in range(B)]
        ident_loaded, cond_loaded, rope_loaded = (sem(n) for n in ("ident_loaded", "cond_loaded", "rope_loaded"))
        silu_zeroed, silu_exp, silu_step = sem("silu_zeroed"), sem("silu_exp"), sem("silu_step")
        wm_loaded = [sem(f"wm_loaded{i}") for i in range(3)]
        mod_mm, mod_row, mod_used, col_ready = (sem(n) for n in ("mod_mm", "mod_row", "mod_used", "col_ready"))
        gate_step, gate_rows, gate_bc, gate_ready = (sem(n) for n in ("gate_step", "gate_rows", "gate_bc", "gate_ready"))
        ln_stats, ln_aggr, ln_eps, ln_std, ln_rstd, ln_norm, ln_trans, ln_full, ln_hi, ln_lo, ln_lo_odd = (
            sem(f"ln_{n}") for n in ("stats", "aggr", "eps", "std", "rstd", "norm", "trans", "full", "hi", "lo", "lo_odd"))
        kv_loaded, q_loaded, wo_loaded = sem("kv_loaded"), sem("q_loaded"), sem("wo_loaded")
        w_hi_done, w_split, wo_hi_done, wo_split = sem("w_hi_done"), sem("w_split"), sem("wo_hi_done"), sem("wo_split")
        proj_done, proj_free = sem("proj_done"), sem("proj_free")
        rope_sum, rope_hi, rope_split, v_hi_done = sem("rope_sum"), sem("rope_hi"), sem("rope_split"), sem("v_hi_done")
        scores0, rowmax0, masked0, exp0, rden0, probs0 = (sem(n) for n in ("scores0", "rowmax0", "masked0", "exp0", "rden0", "probs0"))
        trans0, pT_hi_done, pT_split, pv0 = sem("trans0"), sem("pT_hi_done"), sem("pT_split"), sem("pv0")
        oT_hi_done, oT_split, wo_mm, wo_gated, attn0_added = (sem(n) for n in ("oT_hi_done", "oT_split", "wo_mm", "wo_gated", "attn0_added"))
        f_loaded, f_cw, f_er_mm, f_er, f_as, fbias_loaded = (sem(n) for n in ("f_loaded", "f_cw", "f_er_mm", "f_er", "f_as", "fbias_loaded"))
        f_tr, f_trs, f_mg, f_hi, f_split = (sem(n) for n in ("f_tr", "f_trs", "f_mg", "f_hi", "f_split"))
        f_mm, f_bias, f_gated, f_added = (sem(n) for n in ("f_mm", "f_bias", "f_gated", "f_added"))
        pre_loaded, pre_hi, pre_split, lat_mm, lat_ready = (sem(n) for n in ("pre_loaded", "pre_hi", "pre_split", "lat_mm", "lat_ready"))
        kr_mm, kr_hi_done, kr_split, zeroed = sem("kr_mm"), sem("kr_hi_done"), sem("kr_split"), sem("zeroed")
        c_mm, c_hi_done, c_split, vc_mm, vc_ready = (sem(n) for n in ("c_mm", "c_hi_done", "c_split", "vc_mm", "vc_ready"))
        c_stored = [sem(f"c_stored{i}") for i in range(4)]
        wr_loaded = [sem(f"wr_loaded{i}") for i in range(2)]
        wr_hi_done, wr_split = sem("wr_hi_done"), sem("wr_split")
        qr_mm, q2_hi, q1_hi, q1_split = sem("qr_mm"), sem("q2_hi"), sem("q1_hi"), sem("q1_split")
        mc_loaded, k2c_loaded, m_loaded = ([sem(f"{n}{i}") for i in range(2)] for n in ("mc_loaded", "k2c_loaded", "m_loaded"))
        ones_set = sem("ones_set")
        max_mm, max_done, m_turned = sem("max_mm"), sem("max_done"), sem("m_turned")
        scores1, exp1, pv1, vp_ready, o_copied = (sem(n) for n in ("scores1", "exp1", "pv1", "vp_ready", "o_copied"))
        o_stored = [sem(f"o_stored{i}") for i in range(2)]
        sums_loaded = [sem(f"sums_loaded{b}") for b in range(B)]
        o_added, o_rden, o_normed, oo_hi_done, oo_split, o_last, o_last_den = (
            sem(n) for n in ("o_added", "o_rden", "o_normed", "oo_hi_done", "oo_split", "o_last", "o_last_den"))
        wo1_loaded, wo1_hi_done, wo1_split, wo1_mm, wo1_gated, attn1_added = (
            sem(n) for n in ("wo1_loaded", "wo1_hi_done", "wo1_split", "wo1_mm", "wo1_gated", "attn1_added"))
        g_loaded, g_tr, g_hi, g_lo, g_const = (sem(n) for n in ("g_loaded", "g_tr", "g_hi", "g_lo", "g_const"))
        r_part, r_copied, r_mm, r_step, r_exp, r_kept, r_ktr, r_ktc = (
            sem(n) for n in ("r_part", "r_copied", "r_mm", "r_step", "r_exp", "r_kept", "r_ktr", "r_ktc"))
        r_wmm, r_wexp, r_hmm, r_hfull, r_hhi, r_hlo = (sem(n) for n in ("r_wmm", "r_wexp", "r_hmm", "r_hfull", "r_hhi", "r_hlo"))
        g_mm, g_bias, g_gated, g_added, stored = (sem(n) for n in ("g_mm", "g_bias", "g_gated", "g_added", "stored"))
        spare = sem("spare")

        def wait_norm(eng, ph, b):
            eng.wait_ge(ln_lo, NT // 2 * ph + TB // 2 * (b + 1))
            eng.wait_ge(ln_lo_odd, NT // 2 * ph + TB // 2 * (b + 1))

        def norm_bank(ph, j):
            return bank[j if ph == 2 else (j + KT) % 8]

        def col_bank(l, half):
            return bank[0 if l == 0 and half == 0 else 4 + (half + l) % 2][:, 0:16]

        def gate_sums(l):
            return bank[4][0:2 * 32] if l == 0 else bank[2][0:2 * 32]

        USES = [(0, 1, 2, 3, 4, 5), (0, 1, 3, 4, 2, 5)]
        COLS_USED = [(2, 5), (2, 4)]
        GATE_BANKS = [(4, 5), (0, 1), (2, 3), (0, 1)]

        def g_bank(i):
            ps = bank[i % 4][:]
            return ps if i != KT + 2 else ps.rearrange("p (k n) -> p k n", k=KT)[:, :, 0:NR]

        X_ADDED = [(attn0_added, NT * HKV), (f_added, NT), (attn1_added, NT)]

        wq, wk, wv, wo = a["L0_attn_wq"], a["L0_attn_wk"], a["L0_attn_wv"], a["L0_attn_wo"]
        wq_v, wk_v, wv_v = (w.rearrange("(k p) n -> p k n", p=P) for w in (wq, wk, wv))
        wo_v = wo.rearrange("(h p) n -> p h n", p=P)
        wr_v = a["L1_attn_Wq_rope"].rearrange("(k p) n -> p k n", p=P)
        wmod_v = [a[f"L{l}_wmod"].rearrange("(p k) n -> p k n", k=KT) for l in range(2)]

        W_TILE = {"K": 0, "V": 1, "Q0": 2, "Q1": 3, "Q2": 4, "Q3": 5}
        ROPE_NO = {"K": 0, "Q0": 1, "Q1": 2, "Q2": 3, "Q3": 4}

        block = ctx.enter_context(nc.Block())

        @block.sync
        def _(sp):
            sp.dma_start(cT[:, 0], a["L0_c"].rearrange("b (p k) -> p b k", k=KT)).then_inc(cond_loaded, 16)
            sp.dma_start(cT[:, 1], a["L1_c"].rearrange("b (p k) -> p b k", k=KT)).then_inc(cond_loaded, 16)
            for t in range(NT):
                sp.dma_start(x[:, t], x_in[:, t]).then_inc(x_loaded[t // TB], 16)

            def load_wmod(l, c):
                i = 6 * l + c
                wait(sp, mod_mm, i - 2)
                sp.dma_start(WM[l][:, i % 3], wmod_v[l][:, :, c * D:(c + 1) * D]).then_inc(wm_loaded[i % 3], 16)

            def hold(semaphore, v):
                if not isinstance(v, int) or v > 0:
                    sp.wait_ge(semaphore, v)
                    sp.sem_inc(spare, 1)

            def load_kv(n):
                if exists(n, HKV):
                    hold(w_split, 6 * n)
                    sp.dma_start(st_kv[:, 0], wk_v[:, :, bass.ts(n, HD)]).then_inc(kv_loaded, 16)
                    sp.dma_start(st_kv[:, 1], wv_v[:, :, bass.ts(n, HD)]).then_inc(kv_loaded, 16)
                    sp.dma_start(st_q[:], wq_v[:, :, bass.ts(n, GQ * HD)]).then_inc(q_loaded, 16)

            def load_wo(n):
                if exists(n, HKV):
                    hold(wo_split, n)
                    sp.dma_start(st_wo[:], wo_v[:, bass.ts(n, GQ)]).then_inc(wo_loaded, 16)

            sp.dma_start(ident[:], a["identity"]).then_inc(ident_loaded, 16)
            sp.dma_start(sel[:], a["batch_rows"].rearrange("p (b m) -> p b m", b=B)).then_inc(ident_loaded, 16)
            sp.dma_start(rowsum[:], a["four_identities"]).then_inc(ident_loaded, 16)
            load_wmod(0, 0)
            load_wmod(0, 1)
            load_kv(0)
            load_wmod(0, 2)
            sp.dma_start(rope_cos[:], a["rope_cos"]).then_inc(rope_loaded, 16)
            sp.dma_start(rope_sin[:], a["rope_sin"]).then_inc(rope_loaded, 16)
            sp.dma_start(window[:], a["window_mask"]).then_inc(rope_loaded, 16)
            load_wmod(0, 3)
            load_wmod(0, 4)
            load_wo(0)
            load_wmod(0, 5)
            with sp.Fori(1, HKV) as n:
                load_kv(n)
                load_wo(n)

            sp.wait_ge(w_split, 6 * HKV)
            sp.wait_ge(wo_split, HKV)
            sp.dma_start(fw[:], a["L0_ffn_W"].rearrange("(k p) d -> p k d", p=P)).then_inc(f_loaded, 16)
            for k in range(KT):
                sp.dma_start(fbf[:, k].rearrange("p (e r) -> p e r", r=16),
                             a["L0_ffn_Bf"].rearrange("e (k p) r -> k p e r", p=P)[k]).then_inc(f_loaded, 16)
            sp.dma_start(fa[:], a["L0_ffn_A"].rearrange("(t e) r d -> (e r) t d", t=2)).then_inc(f_loaded, 16)
            sp.dma_start(fco[:, 0:1], a["L0_ffn_coeffs"].rearrange("(e o) -> e o", o=1)).then_inc(f_loaded, 16)
            sp.dma_start(fco[:, 1:2], a["L0_ffn_scales"].rearrange("(e o) -> e o", o=1)).then_inc(f_loaded, 16)
            sp.dma_start(expand[:], a["lora_expand"]).then_inc(f_loaded, 16)
            sp.wait_ge(proj_done, TURNS * B * HKV)
            for c in range(3):
                load_wmod(1, c)

            sp.wait_ge(attn0_added, NT * HKV)
            sp.dma_start(fbias[:], a["L0_ffn_bias"].rearrange("(o n) -> o n", o=1).partition_broadcast(P)
                         .rearrange("p o n -> p (o n)")).then_inc(fbias_loaded, 16)
            for c in range(3, 6):
                load_wmod(1, c)
            for w, name in enumerate(("L1_attn_Wq_down", "L1_attn_Wkv_down")):
                sp.dma_start(dn[:, :, w * LAT:(w + 1) * LAT], a[name].rearrange("(k p) n -> p k n", p=P)).then_inc(pre_loaded, 16)
            for w in range(2):
                sp.dma_start(kr[:, :, w * ROPE:(w + 1) * ROPE],
                             a["L1_attn_Wk_rope"].rearrange("(k p) n -> p k n", p=P)).then_inc(pre_loaded, 16)
            sp.dma_start(up[0:LAT], a["L1_attn_Wq_up"]).then_inc(pre_loaded, 16)
            sp.dma_start(up[LAT:P], a["L1_attn_Wk_up"]).then_inc(pre_loaded, 16)
            sp.dma_start(vup[LAT:P], a["L1_attn_Wv_up"]).then_inc(pre_loaded, 16)

            def load_rope_weights(p, par):
                if exists(p, PAIRS):
                    hold(wr_split, p - 1)
                    sp.dma_start(wst[:, par], wr_v[:, :, bass.ts(p, P)]).then_inc(wr_loaded[par], 16)

            sp.wait_ge(mod_mm, 12)
            load_rope_weights(0, 0)
            load_rope_weights(1, 1)

            def store_content(m):
                for b in range(B):
                    for w, halves in enumerate((qc_d[b].rearrange("h c g s -> g h c s"), kc_d[b].rearrange("h g c s -> g h c s"))):
                        i = 2 * b + w
                        sp.wait_ge(c_split, 4 * m + i + 1)
                        for g, src in enumerate((c_hi, c_lo)):
                            sp.dma_start(halves[g, 32 * m:32 * m + 32], src[:, i].bitcast(F32)).then_inc(c_stored[i], 16)

            def rows(h):
                return slice(ROPE, ROPE + CR) if h == 0 else slice(0, CR)

            def key_rows(v):
                return v.rearrange("o g c s -> (g c) o s").broadcast_to([2 * HD1, 2, S])

            def query_rows(v):
                return v.rearrange("o c g s -> o (c g) s").broadcast_to([2, 2 * HD1, S])

            def maxrow(h):
                return ROPE + CR if h == 0 else CR

            def period(u, k):
                v, vb = u + 1, (k + 1) % 2
                if exists(v, UNITS):
                    hold(scores1, 8 * (v - 1))
                    for h in range(2):
                        sp.dma_start(k2[rows(h), vb, h].bitcast(F32), key_rows(kc_d[vb, hd(u, k, 1, h)]))\
                          .then_inc(k2c_loaded[vb], 16)
                v, vb = u + 3, (k + 3) % 2
                if exists(v, UNITS):
                    hold(max_mm, 8 * (v - 1))
                    for h in range(2):
                        sp.dma_start(km[rows(h), vb, h].bitcast(F32), key_rows(kc_d[vb, hd(u, k, 3, h)]))\
                          .then_inc(mc_loaded[vb], 16)
                    hold(scores1, 8 * (v - 3))
                    for h in range(2):
                        sp.dma_start(q2[rows(h), (k + 3) % 4, h].bitcast(F32), query_rows(qc_d[vb, hd(u, k, 3, h)])).then_inc(mc_loaded[vb], 16)
                if k % 2 == 0:
                    load_rope_weights(pairs(u, k, 6), (k // 2 + 3) % 2)
                v = u - 1
                if exists(v, UNITS):
                    vb = (k + 1) % 2
                    hold(o_copied, v + 1)
                    for h in range(2):
                        for par in range(2):
                            j = 2 * h + par
                            sp.dma_start(o_d[vb, hd(u, k, -1, h), par].rearrange("o c s -> (o c) s"), ost[32 * j:32 * j + 8, (k + 1) % 2])\
                              .then_inc(o_stored[(k + 1) % 2], 16)
                v = u + 2
                if exists(v, UNITS):
                    hold(m_turned, v + 1)
                    for h in range(2):
                        r = maxrow(h)
                        sp.dma_start(q2[r:r + 1, (k + 2) % 4, h].bitcast(F32).rearrange("p (q n) -> p q n", q=4),
                                     mrow[h:P:32, k % 2]).then_inc(m_loaded[k % 2], 16)

            def pairs(u, k, ahead):
                if isinstance(u, int):
                    return (u + ahead) // 2
                return 2 * G[0] + (k + ahead) // 2

            def hd(u, k, ahead, h):
                return bass.ds(2 * pairs(u, k, ahead) + h, 1)

            G = [None]
            store_content(0)
            for i in range(4):
                sp.wait_ge(c_stored[i], 32)
            sp.wait_ge(zeroed, 6)
            for b in range(B):
                for h in range(2):
                    sp.dma_start(k2[maxrow(h):maxrow(h) + 1, b, h].bitcast(F32), ost[0:1, 0]).then_inc(ones_set, 16)
            for u in range(-3, 0):
                period(u, u % 4)
                store_content(u + 4)
            for u in range(0, 6):
                period(u, u % 4)
            for i in range(4):
                sp.wait_ge(c_stored[i], 32 * KT)
            with sp.Fori(1, TAIL // 4) as g:
                G[0] = g
                for k in range(2, 6):
                    period(4 * g + k, k)

            def load_sums(n):
                b, m = n % 2, n // 2
                for par in range(2):
                    for dst, r in zip(SUMS[b], (0, HD1)):
                        sp.dma_start(dst[:, par], o_d[b, 32 * m:32 * m + 32, par, r:r + HD1]).then_inc(sums_loaded[b], 16)

            def load_last_sums(b):
                sp.wait_ge(o_stored[b], 64 * PAIRS)
                sp.wait_ge(oo_split, EARLY - 1 + b)
                load_sums(EARLY + b)

            def load_wo1(ks):
                for k in ks:
                    sp.dma_start(wst[:, k % 2].rearrange("p k n -> p (k n)"), a["L1_attn_Wo"].rearrange("(k p) n -> k p n", p=P)[k])\
                      .then_inc(wo1_loaded, 16)

            for i in range(2):
                sp.wait_ge(o_stored[i], 64 * (PAIRS - PAIRS // KT))
            for u in range(TAIL, UNITS + 1):
                n = u - TAIL
                if n < EARLY:
                    wait(sp, oo_split, n - 1)
                    load_sums(n)
                if u == UNITS:
                    load_last_sums(0)
                period(u, u % 4)
                if u == UNITS - 5:
                    sp.wait_ge(wr_split, PAIRS)
                    load_wo1((0, 1))
                if u == UNITS - 3:
                    sp.wait_ge(wo1_split, 2)
                    load_wo1((2, 3))

            load_last_sums(1)

            sp.wait_ge(o_copied, UNITS)
            sp.dma_start(bw[:], a["L1_ffn_base_W"].rearrange("(k p) d -> p k d", p=P)).then_inc(g_loaded, 16)
            sp.dma_start(la[:], a["L1_ffn_A"].rearrange("e r d -> (e r) d")).then_inc(g_loaded, 16)
            sp.dma_start(rw[0:NR], a["L1_ffn_router_W"]).then_inc(g_loaded, 16)
            for k in range(KT):
                sp.dma_start(lb[:, k], a["L1_ffn_B"].rearrange("e (k p) r -> k p e r", p=P)[k]).then_inc(g_loaded, 16)
            for dst, name in ((bbias, "L1_ffn_base_b"), (rbias, "L1_ffn_router_b")):
                sp.dma_start(dst[:], a[name].rearrange("(o n) -> o n", o=1).partition_broadcast(P)
                             .rearrange("p o n -> p (o n)")).then_inc(g_loaded, 16)
            sp.dma_start(emap_i[0:NR], a["L1_ffn_expert_map"].rearrange("(e o) -> e o", o=1)).then_inc(g_loaded, 16)
            sp.dma_start(ecol[:], a["expert_of_column"]).then_inc(g_loaded, 16)
            sp.dma_start(before[:].rearrange("p n m -> p (n m)"),
                         a["entry_before"].rearrange("n m -> (n m)").rearrange("(o k) -> o k", o=1).partition_broadcast(P)
                         .rearrange("p o n -> p (o n)")).then_inc(g_loaded, 16)
            for t in range(NT):
                sp.wait_ge(g_added, t + 1)
                sp.dma_start(out_t[:, t], x[:, t]).then_inc(stored, 16)
            sp.wait_ge(stored, 16 * NT)

        @block.gpsimd
        def _(pool):
            def split_weights(n, tiles):
                for m in tiles:
                    pool.wait_ge(w_hi_done, 6 * n + m + 1)
                    src = st_kv[:, m] if m < 2 else st_q[:, :, (m - 2) * HD:(m - 1) * HD]
                    pool.tensor_tensor(w_lo[:, m], src, w_hi[:, m].bitcast(F32), ALU.subtract).then_inc(w_split, 1)

            def split_wo(n):
                pool.wait_ge(wo_hi_done, n + 1)
                pool.tensor_tensor(wo_lo[:], st_wo[:], wo_hi[:].bitcast(F32), ALU.subtract).then_inc(wo_split, 1)

            def rope(half, name, b):
                r = 5 * half + ROPE_NO[name]
                i = (b + ROPE_NO[name]) % 2
                pool.wait_ge(proj_free, TURNS * half + TURN[name] + 1)
                pool.tensor_tensor(rope_a[:, i], rope_a[:, i], rope_b[:, i], ALU.add).then_inc(rope_sum, 1)
                pool.wait_ge(rope_hi, r + 1)
                hi, lo = (kT_hi[:, b], kT_lo[:, b]) if name == "K" else (qT_hi[b][:, ROPE_NO[name] - 1], qT_lo[b][:, ROPE_NO[name] - 1])
                pool.tensor_tensor(lo, rope_a[:, i], hi.bitcast(F32), ALU.subtract).then_inc(rope_split, 1)

            def add_attention(slot, tile):
                pool.wait_ge(wo_gated, slot + 1)
                pool.tensor_tensor(x[:, tile], x[:, tile], gated[:], ALU.add).then_inc(attn0_added, 1)

            def norm(ph, b):
                for j in range(KT * b + 1, KT * b + KT, 2):
                    pool.wait_ge(ln_hi, NT * ph + j + 1)
                    at = slice(b * S, (b + 1) * S)
                    pool.tensor_tensor(hT_lo[:, j % KT, at], NORM[ph][1][:, j % 4], hT_hi[:, j % KT, at].bitcast(F32), ALU.subtract)\
                        .then_inc(ln_lo_odd, 1)

            pool.memset(silu[:], 0.0).then_inc(silu_zeroed, 1)
            split_weights(0, (0, 1))
            norm(0, 0)
            split_weights(0, (2,))
            norm(0, 1)
            split_weights(0, (3, 4, 5))
            wait_norm(pool, 0, 1)
            for name in ROPE_NO:
                rope(0, name, 0)
            rope(1, "K", 1)

            def kv_head(n, last):
                for b in range(B):
                    half = 2 * n + b
                    if not (isinstance(n, int) and n == 0 and b == 0):
                        add_attention(4 * half - 1, TB * (1 - b) + 3)
                    if b == 0:
                        split_wo(n)
                    if not (last and b == 1):
                        rope(half + 1, "Q0", 1 - b)
                        rope(half + 1, "Q1", 1 - b)
                    add_attention(4 * half, TB * b)
                    if b == 0 and not last:
                        split_weights(n + 1, (0, 1))
                    if not (last and b == 1):
                        rope(half + 1, "Q2", 1 - b)
                        rope(half + 1, "Q3", 1 - b)
                    add_attention(4 * half + 1, TB * b + 1)
                    if not last:
                        rope(half + 2, "K", b)
                        if b == 0:
                            split_weights(n + 1, (2, 3, 4, 5))
                    add_attention(4 * half + 2, TB * b + 2)
                if last:
                    add_attention(8 * n + 7, NT - 1)

            kv_head(0, False)
            with pool.Fori(1, HKV - 1) as n:
                kv_head(n, False)
            kv_head(HKV - 1, True)
            for b in range(B):
                norm(1, b)
            for t in range(NT):
                pool.wait_ge(f_gated, t + 1)
                pool.tensor_tensor(x[:, t], x[:, t], fg[:, t % 2], ALU.add).then_inc(f_added, 1)
                if t == 1:
                    for i, (src, hi, lo) in enumerate(((dn, dn_hi, dn_lo), (kr, kr_hi, kr_lo))):
                        pool.wait_ge(pre_hi, i + 1)
                        pool.tensor_tensor(lo[:], src[:], hi[:].bitcast(F32), ALU.subtract).then_inc(pre_split, 1)
            for b in range(B):
                norm(2, b)
            pool.wait_ge(f_split, KT)
            pool.wait_ge(mod_mm, 12)
            pool.memset(k2[:].bitcast(F32), 0.0).then_inc(zeroed, 1)
            pool.memset(km[:].bitcast(F32), 0.0).then_inc(zeroed, 1)
            pool.memset(q2[:].bitcast(F32), 0.0).then_inc(zeroed, 1)
            pool.memset(vp[:], 0.0).then_inc(zeroed, 1)
            pool.memset(mcol[:].bitcast(F32), 0.0).then_inc(zeroed, 1)
            wait_norm(pool, 2, 1)
            pool.memset(ost[0:1, 0], 1.0).then_inc(zeroed, 1)
            pool.wait_ge(zeroed, 6)
            pool.memset(vp[:, :, :, :, HD1:2 * HD1], 1.0).then_inc(zeroed, 1)

            def split_rope_weights(p, par):
                if exists(p, PAIRS):
                    pool.wait_ge(wr_hi_done, p + 1)
                    pool.tensor_tensor(wr_lo[:, par], wst[:, par], wr_hi[:, par].bitcast(F32), ALU.subtract).then_inc(wr_split, 1)

            split_rope_weights(0, 0)
            split_rope_weights(1, 1)
            with pool.Fori(0, PAIRS // 2 - 2) as g:
                split_rope_weights(2 * g + 2, 0)
                split_rope_weights(2 * g + 3, 1)

            def sums_add(n):
                o, d = SUMS[n % 2]
                pool.wait_ge(sums_loaded[n % 2], 64 * (n // 2 + 1))
                pool.tensor_tensor(d[:, 0], d[:, 0], d[:, 1], ALU.add).then_inc(o_added, 1)
                pool.tensor_tensor(o[:, 0], o[:, 0], o[:, 1], ALU.add).then_inc(o_added, 1)

            def sums_times(n):
                o, d = SUMS[n % 2]
                pool.wait_ge(o_added, 2 * n + 2)
                pool.wait_ge(o_rden, n + 1)
                pool.tensor_tensor(o[:, 0], o[:, 0], d[:, 1], ALU.mult).then_inc(o_normed, 1)

            def sums_low(n):
                b, m = n % 2, n // 2
                at = slice(b * S, (b + 1) * S)
                lo, hi = (oo_lo[:, m, at], oo_hi[:, m, at]) if m < KT - 1 else (oo3_lo[:, at], oo3_hi[:, at])
                pool.wait_ge(oo_hi_done, n + 1)
                pool.tensor_tensor(lo, SUMS[b][0][:, 0], hi.bitcast(F32), ALU.subtract).then_inc(oo_split, 1)

            def wo1_low(ks):
                for k in ks:
                    pool.wait_ge(wo1_hi_done, k + 1)
                    pool.tensor_tensor(wo1_lo[:, k], wst[:, k % 2].rearrange("p k n -> p (k n)"), wo1_hi[:, k].bitcast(F32), ALU.subtract)\
                        .then_inc(wo1_split, 1)

            sums_add(0)
            for n in range(EARLY):
                if n in (1, 3):
                    split_rope_weights(PAIRS - 2 + n // 2, n // 2)
                sums_times(n)
                if n + 1 < EARLY:
                    sums_add(n + 1)
                sums_low(n)
            wo1_low((0, 1))
            wo1_low((2, 3))
            for b in range(B):
                pool.wait_ge(sums_loaded[b], 64 * KT)
                o = SUMS[b][0]
                pool.tensor_tensor(o[:, 0], o[:, 0], o[:, 1], ALU.add).then_inc(o_last, 1)
            for t in range(NT):
                pool.wait_ge(wo1_gated, t + 1)
                pool.tensor_tensor(x[:, t], x[:, t], og[:, t % 2], ALU.add).then_inc(attn1_added, 1)
            for b in range(B):
                norm(3, b)
            for t in range(NT):
                pool.wait_ge(g_gated, t + 1)
                pool.tensor_tensor(x[:, t], x[:, t], gg[:, t % 2], ALU.add).then_inc(g_added, 1)

        @block.scalar
        def _(act):
            act.wait_ge(cond_loaded, 32)
            act.activation(silu_e[:], cT[:], ACT.Exp, scale=-1.0).then_inc(silu_exp, 1)

            def mod_rows(l, chunks):
                for c in chunks:
                    i = 6 * l + c
                    act.wait_ge(mod_mm, i + 1)
                    if c in (3, 4):
                        act.wait_ge(mod_used, i - 2)
                    act.activation(MODROW[l][:, ROW_SLOT[c]], bank[2 + c % 2][:], ACT.Copy).then_inc(mod_row, 1)

            def gates(l, w, dst):
                act.wait_ge(gate_bc, 2 * l + w + 1)
                for b, ps in enumerate(GATE_BANKS[2 * l + w]):
                    e = act.activation(dst[:, b], bank[ps][:], ACT.Copy)
                e.then_inc(gate_ready, 1)

            def norm_std(ph, b):
                act.wait_ge(ln_eps, B * ph + b + 1)
                act.activation(std[:, TB * b:TB * b + TB], var_eps[:, TB * b:TB * b + TB], ACT.Sqrt).then_inc(ln_std, 1)

            def norm(ph, b):
                _, full, l, v = NORM[ph]
                act.wait_ge(col_ready, 2 * l + v // 2 + 1)
                act.wait_ge(ln_trans, NT * ph + TB * (b + 1))
                for j in range(KT * b, KT * b + KT):
                    k = j % KT
                    if j >= 4:
                        act.wait_ge(ln_lo_odd if j % 2 else ln_lo, NT // 2 * ph + (j - 4) // 2 + 1)
                    act.activation(full[:, j % 4], norm_bank(ph, j)[:], ACT.Identity, bias=modc[:, l, v, k, b:b + 1],
                                   scale=modc[:, l, v + 1, k, b:b + 1]).then_inc(ln_full, 1)

            for b in range(B):
                norm_std(0, b)
            mod_rows(0, (0, 1))
            for b in range(B):
                norm(0, b)

            def rope_high(half, name, b):
                r = 5 * half + ROPE_NO[name]
                act.wait_ge(rope_sum, r + 1)
                hi = kT_hi[:, b] if name == "K" else qT_hi[b][:, ROPE_NO[name] - 1]
                act.activation(hi, rope_a[:, (b + ROPE_NO[name]) % 2], ACT.Copy).then_inc(rope_hi, 1)

            def v_high(half, b):
                act.wait_ge(proj_done, TURNS * half + TURN["Vt"] + 1)
                act.activation(v_hi[:, b].rearrange("p t d -> p (t d)"), bank[6 + (b + TURN["Vt"]) % 2][:], ACT.Copy).then_inc(v_hi_done, 1)

            def exps(slot, qb):
                i = qb % 2
                c = slice(P, 2 * P) if qb == 0 else slice(0, 2 * P)
                act.wait_ge(masked0, slot + 1)
                for h in range(GQ):
                    e = act.activation(probs[:, i, h, c], probs[:, i, h, c], ACT.Exp, bias=nmax[:, i, h:h + 1], scale=1.0,
                                       accum_out=den[:, i, h:h + 1])
                e.then_inc(exp0, 1)

            def weights_high(slot, qb):
                act.wait_ge(trans0, slot + 1)
                for kb in range(1 if qb == 0 else 0, 2):
                    e = act.activation(pT_hi[:, kb], bank[2 + kb][:], ACT.Copy)
                e.then_inc(pT_hi_done, 1)

            def kv_head(n, last):
                for b in range(B):
                    half, slot, nb = 2 * n + b, 8 * n + 4 * b, 1 - b
                    more = not (last and b == 1)
                    weights_high(slot, 0)
                    exps(slot + 1, 1)
                    if isinstance(n, int) and n == 0 and b == 0:
                        gates(0, 0, gate_a0)
                    out_high(slot)
                    if more:
                        rope_high(half + 1, "Q0", nb)
                    weights_high(slot + 1, 1)
                    if more:
                        v_high(half + 1, nb)
                        rope_high(half + 1, "Q1", nb)
                    exps(slot + 2, 2)
                    out_high(slot + 1)
                    weights_high(slot + 2, 2)
                    if more:
                        rope_high(half + 1, "Q2", nb)
                    exps(slot + 3, 3)
                    out_high(slot + 2)
                    if more:
                        rope_high(half + 1, "Q3", nb)
                    weights_high(slot + 3, 3)
                    if not last:
                        rope_high(half + 2, "K", b)
                    out_high(slot + 3)
                    if more:
                        exps(slot + 4, 0)

            def out_high(slot):
                act.wait_ge(pv0, slot + 1)
                act.activation(oT_hi[:].rearrange("p h t -> p (h t)"), bank[4][:], ACT.Copy).then_inc(oT_hi_done, 1)

            rope_high(0, "K", 0)
            rope_high(0, "Q0", 0)
            rope_high(0, "Q1", 0)
            v_high(0, 0)
            rope_high(0, "Q2", 0)
            rope_high(0, "Q3", 0)
            mod_rows(0, (2, 3, 4, 5))
            rope_high(1, "K", 1)
            exps(0, 0)
            kv_head(0, False)
            with act.Fori(1, HKV - 1) as n:
                kv_head(n, False)
            kv_head(HKV - 1, True)

            for t in range(2):
                act.wait_ge(f_tr, t + 1)
                act.activation(fbfT[:, t], bank[6 + t][:], ACT.Copy).then_inc(f_trs, 1)
            for b in range(B):
                norm_std(1, b)
            mod_rows(1, range(6))

            def merged_high(k):
                act.wait_ge(f_mg, k + 1)
                act.activation(fw_hi[:, k], bank[k][:], ACT.Copy).then_inc(f_hi, 1)

            merged_high(0)
            merged_high(1)
            norm(1, 0)
            merged_high(2)
            merged_high(3)
            norm(1, 1)
            gates(0, 1, gate[:, 0])
            act.wait_ge(pre_loaded, 16 * 7)
            for src, hi in ((dn, dn_hi), (kr, kr_hi)):
                act.activation(hi[:], src[:], ACT.Copy).then_inc(pre_hi, 1)
            gates(1, 0, gate[:, 1])
            gates(1, 1, gate[:, 2])

            for b in range(B):
                norm_std(2, b)
            for b in range(B):
                norm(2, b)
            for b in range(B):
                act.wait_ge(lat_mm, b + 1)
                act.activation(lat[:, b * S:(b + 1) * S], bank[b][:], ACT.Copy).then_inc(lat_ready, 1)
            act.wait_ge(zeroed, 6)
            for b in range(B):
                act.wait_ge(kr_mm, b + 1)
                act.activation(k1[:, b], bank[6 + b][:], ACT.Copy)
                act.activation(km[0:ROPE, b, 0], bank[6 + b][0:ROPE], ACT.Copy)
                act.activation(km[ROPE:P, b, 1], bank[6 + b][ROPE:P], ACT.Copy).then_inc(kr_hi_done, 1)

            def content_high(m):
                for i in range(4):
                    act.wait_ge(c_mm, 4 * m + i + 1)
                    wait(act, c_stored[i], 32 * m)
                    act.activation(c_hi[:, i], bank[i][:], ACT.Copy).then_inc(c_hi_done, 1)

            content_high(0)
            for t in range(NT):
                act.wait_ge(vc_mm, t + 1)
                act.activation(vc[:, t], bank[4 + t % 2][:], ACT.Copy).then_inc(vc_ready, 1)

            act.sem_inc(exp1, 4)

            def q_high(z, k):
                if exists(z, UNITS):
                    act.wait_ge(qr_mm, z + 1)
                    act.activation(q2[0:ROPE, k % 4, 0], bank[6][0:ROPE], ACT.Copy)
                    act.activation(q2[ROPE:P, k % 4, 1], bank[6][ROPE:P], ACT.Copy).then_inc(q2_hi, 1)

            def q_high_again(z, k):
                if exists(z, UNITS):
                    act.wait_ge(q2_hi, z + 1)
                    act.activation(q1[0:ROPE, k % 4, 0], q2[0:ROPE, k % 4, 0], ACT.Copy)
                    act.activation(q1[ROPE:P, k % 4, 1], q2[ROPE:P, k % 4, 1], ACT.Copy).then_inc(q1_hi, 1)

            def period(u, k, pair):
                q_high(u + 2, k + 2)
                if isinstance(u, int) and 0 < u + 3 < KT:
                    content_high(u + 3)
                for s in range(8):
                    if s == 6:
                        q_high_again(u + 2, k + 2)
                    if s == 2:
                        if exists(u - 1, UNITS):
                            act.wait_ge(pv1, 2 * u + 1)
                            wait(act, o_stored[(k + 1) % 2], 64 * pair(-1))
                            act.activation(ost[:, (k + 1) % 2], bank[7][:], ACT.Copy).then_inc(o_copied, 1)
                    if exists(u, UNITS):
                        act.wait_ge(scores1, 8 * u + s + 1)
                        wait(act, pv1, 2 * u + s // 4)
                        act.activation(pT[:, s], bank[s % 4][:], ACT.Exp, scale=float((HD1 + ROPE) ** -0.5)).then_inc(exp1, 1)

            for u in range(-3, 6):
                period(u, u % 4, lambda n, u=u: (u + n) // 2)
            with act.Fori(1, TAIL // 4) as g:
                for k in range(2, 6):
                    period(4 * g + k, k, lambda n, k=k: 2 * g + (k + n) // 2)
            def sums_high(n):
                b, m = n % 2, n // 2
                at = slice(b * S, (b + 1) * S)
                act.wait_ge(o_normed, n + 1)
                src = SUMS[b][0][:, 0]
                dst = oo_hi[:, m, at] if m < KT - 1 else oo3_hi[:, at]
                act.activation(dst, src, ACT.Copy).then_inc(oo_hi_done, 1)

            def wo1_high(ks):
                act.wait_ge(qr_mm, UNITS)
                act.wait_ge(wo1_loaded, 16 * (ks[-1] + 1))
                for k in ks:
                    act.activation(wo1_hi[:, k], wst[:, k % 2].rearrange("p k n -> p (k n)"), ACT.Copy).then_inc(wo1_hi_done, 1)

            for u in range(TAIL, UNITS + 1):
                period(u, u % 4, lambda n, u=u: (u + n) // 2)
                if 0 <= u - TAIL - 1 < EARLY:
                    sums_high(u - TAIL - 1)
                if u == UNITS - 3:
                    wo1_high((0, 1))
                if u == UNITS - 2:
                    wo1_high((2, 3))
            for b in range(B):
                sums_high(6 + b)
            for i, dst in enumerate([*(bwT_hi[:, k] for k in range(KT)), laT_hi[:].rearrange("p k n -> p (k n)"),
                                     lbT_hi[:]]):
                act.wait_ge(g_tr, i + 1)
                act.activation(dst, g_bank(i), ACT.Copy).then_inc(g_hi, 1)
                if i == 0:
                    norm_std(3, 0)
                if i == KT + 1:
                    norm_std(3, 1)
            for b in range(B):
                norm(3, b)
            for b in range(B):
                act.wait_ge(r_part, b + 1)
                act.activation(lpart[:, b * S:(b + 1) * S], bank[(7, 4)[b]][:], ACT.Copy).then_inc(r_copied, 1)
            act.wait_ge(r_step, 3)
            act.activation(prob[:], lg[:], ACT.Exp).then_inc(r_exp, 1)
            for b in range(B):
                act.wait_ge(r_ktr, b + 1)
                act.activation(keptT[0:NR, b * S:(b + 1) * S], bank[(4, 7)[b]][0:NR], ACT.Copy).then_inc(r_ktc, 1)
            for b in range(B):
                act.wait_ge(r_wmm, b + 1)
                act.activation(wexp[:, b * S:(b + 1) * S], bank[(4, 7)[b]][:], ACT.Copy, scale=SCALING).then_inc(r_wexp, 1)
            for b in range(B):
                act.wait_ge(r_hfull, b + 1)
                act.activation(lh_hi[:, b * S:(b + 1) * S], lh[:, b * S:(b + 1) * S], ACT.Copy).then_inc(r_hhi, 1)

        @block.vector
        def _(dve):
            dve.wait_ge(silu_exp, 1)
            dve.tensor_scalar(silu_d[:], silu_e[:], 1.0, None, ALU.add).then_inc(silu_step, 1)
            dve.wait_ge(silu_step, 1)
            dve.reciprocal(silu_e[:], silu_d[:]).then_inc(silu_step, 1)
            dve.wait_ge(silu_step, 2)
            dve.wait_ge(silu_zeroed, 1)
            for l in range(2):
                e = dve.tensor_tensor(silu[:, l, :, 0:B].rearrange("p k b -> p b k"), cT[:, l], silu_e[:, l], ALU.mult)
            e.then_inc(silu_step, 1)

            def mod_cols(l, half):
                dve.wait_ge(mod_used, 6 * l + COLS_USED[l][half])
                src = col_bank(l, half).rearrange("p (v k b) -> p v k b", v=2, k=KT)
                dve.tensor_copy(modc[:, l, 2 * half], src[:, 0])
                dve.tensor_scalar(modc[:, l, 2 * half + 1], src[:, 1], 1.0, None, ALU.add).then_inc(col_ready, 1)

            def clamp_gates(l):
                src, sign, g = gate_sums(l), GSIGN[l][0:2 * 32], GROWS[l]
                dve.wait_ge(mod_used, 6 * l + 6)
                dve.tensor_scalar(sign, src, 0.0, 2.0, ALU.is_ge, ALU.mult).then_inc(gate_step, 1)
                dve.wait_ge(gate_step, 3 * l + 1)
                dve.tensor_scalar(sign, sign, -1.0, None, ALU.add).then_inc(gate_step, 1)
                dve.wait_ge(gate_step, 3 * l + 2)
                dve.tensor_tensor(g[:], src, sign, ALU.mult).then_inc(gate_step, 1)
                dve.wait_ge(gate_step, 3 * l + 3)
                dve.scalar_tensor_tensor(g[:], g[:], 0.25, sign, ALU.max, ALU.mult).then_inc(gate_rows, 1)

            def norm_stats(ph, b, part=range(TB)):
                tiles = range(TB * b, TB * b + TB)
                for t in (TB * b + i for i in part):
                    if ph == 0:
                        dve.wait_ge(x_loaded[b], 16 * TB)
                    else:
                        added, count = X_ADDED[ph - 1]
                        dve.wait_ge(added, count - NT + t + 1)
                    dve.bn_stats(stats[:, t], x[:, t]).then_inc(ln_stats, 1)
                if TB - 1 not in part:
                    return
                for t in tiles:
                    dve.wait_ge(ln_stats, NT * ph + t + 1)
                    dve.bn_aggr(mean_var[:, t], stats[:, t]).then_inc(ln_aggr, 1)
                dve.wait_ge(ln_aggr, NT * ph + TB * (b + 1))
                at = slice(TB * b, TB * b + TB)
                dve.tensor_scalar(var_eps[:, at], mean_var[:, at, 1], EPS, None, ALU.add).then_inc(ln_eps, 1)

            def norm_rows(ph, b):
                at = slice(TB * b, TB * b + TB)
                dve.wait_ge(ln_std, B * ph + b + 1)
                dve.reciprocal(rstd[:, at], std[:, at]).then_inc(ln_rstd, 1)
                dve.wait_ge(ln_rstd, B * ph + b + 1)
                for t in range(TB * b, TB * b + TB):
                    dve.tensor_scalar(NORM[ph][0][:, t], x[:, t], mean_var[:, t, 0:1], rstd[:, t:t + 1], ALU.subtract, ALU.mult)\
                       .then_inc(ln_norm, 1)

            def norm_split(ph, b):
                at = slice(b * S, (b + 1) * S)
                for j in range(KT * b, KT * b + KT):
                    dve.wait_ge(ln_full, NT * ph + j + 1)
                    dve.tensor_copy(hT_hi[:, j % KT, at], NORM[ph][1][:, j % 4]).then_inc(ln_hi, 1)
                    if j % 2 == 0:
                        dve.wait_ge(ln_hi, NT * ph + j + 1)
                        dve.tensor_tensor(hT_lo[:, j % KT, at], NORM[ph][1][:, j % 4], hT_hi[:, j % KT, at].bitcast(F32),
                                          ALU.subtract).then_inc(ln_lo, 1)

            def split_weights(n, tiles):
                for m in tiles:
                    src = st_kv[:, m] if m < 2 else st_q[:, :, (m - 2) * HD:(m - 1) * HD]
                    if m < 2:
                        dve.wait_ge(kv_loaded, 32 * n + 32)
                    else:
                        dve.wait_ge(q_loaded, 16 * n + 16)
                    if not isinstance(n, int) or n > 0:
                        name = [k for k, v in W_TILE.items() if v == m][0]
                        dve.wait_ge(proj_done, TURNS * (2 * n - 1) + TURN[name] + 1)
                    dve.tensor_copy(w_hi[:, m], src).then_inc(w_hi_done, 1)

            def split_wo(n):
                dve.wait_ge(wo_loaded, 16 * n + 16)
                wait(dve, wo_mm, 8 * n)
                dve.tensor_copy(wo_hi[:], st_wo[:]).then_inc(wo_hi_done, 1)

            def evacuate(half, name, b):
                e = TURNS * half + TURN[name]
                ps = bank[6 + (b + TURN[name]) % 2]
                if name == "Vt":
                    dve.wait_ge(v_hi_done, half + 1)
                    dve.tensor_tensor(v_lo[:, b].rearrange("p t d -> p (t d)"), ps[:], v_hi[:, b].rearrange("p t d -> p (t d)").bitcast(F32),
                                      ALU.subtract).then_inc(proj_free, 1)
                    return
                dve.wait_ge(proj_done, e + 1)
                if name == "V":
                    dve.tensor_copy(vT[:], ps[:]).then_inc(proj_free, 1)
                    return
                i = (b + ROPE_NO[name]) % 2
                wait(dve, rope_split, 5 * half + ROPE_NO[name] - 1)
                dve.tensor_tensor(rope_a[:, i], ps[:], rope_cos[:], ALU.mult)
                dve.tensor_tensor(rope_b[0:64, i], ps[64:P], rope_sin[64:P], ALU.mult)
                dve.tensor_tensor(rope_b[64:P, i], ps[0:64], rope_sin[0:64], ALU.mult).then_inc(proj_free, 1)

            def mask(slot, qb):
                i = qb % 2
                c = slice(P, 2 * P) if qb == 0 else slice(0, 2 * P)
                dve.wait_ge(scores0, slot + 1)
                dve.sem_inc(spare, 1)
                for h in range(GQ):
                    ps = bank[h // 2][:, (h % 2) * 2 * P:(h % 2 + 1) * 2 * P]
                    e = dve.tensor_tensor_reduce(probs[:, i, h, c], ps[:, c], window[:, c], float(HD) ** -0.5, -3e38, ALU.add, ALU.max,
                                                 rmax[:, i, h:h + 1])
                e.then_inc(rowmax0, 1)
                dve.wait_ge(rowmax0, slot + 1)
                dve.tensor_scalar(nmax[:, i], rmax[:, i], -1.0, None, ALU.mult).then_inc(masked0, 1)

            def normalise(slot, qb):
                i = qb % 2
                c = slice(P, 2 * P) if qb == 0 else slice(0, 2 * P)
                dve.wait_ge(exp0, slot + 1)
                dve.reciprocal(rden[:, i], den[:, i]).then_inc(rden0, 1)
                dve.wait_ge(rden0, slot + 1)
                for h in range(GQ):
                    e = dve.tensor_scalar(probs[:, i, h, c], probs[:, i, h, c], rden[:, i, h:h + 1], None, ALU.mult)
                e.then_inc(probs0, 1)

            def weights_low(slot, qb):
                dve.wait_ge(pT_hi_done, slot + 1)
                for kb in range(1 if qb == 0 else 0, 2):
                    e = dve.tensor_tensor(pT_lo[:, kb], bank[2 + kb][:], pT_hi[:, kb].bitcast(F32), ALU.subtract)
                e.then_inc(pT_split, 1)

            def out_low(slot):
                dve.wait_ge(oT_hi_done, slot + 1)
                dve.tensor_tensor(oT_lo[:].rearrange("p h t -> p (h t)"), bank[4][:], oT_hi[:].rearrange("p h t -> p (h t)").bitcast(F32),
                                  ALU.subtract).then_inc(oT_split, 1)

            def gate_attention(slot, b):
                dve.wait_ge(wo_mm, slot + 1)
                if isinstance(slot, int) and slot == 0:
                    dve.wait_ge(gate_ready, 1)
                wait(dve, attn0_added, slot)
                dve.tensor_tensor(gated[:], bank[5][:], gate_a0[:, b], ALU.mult).then_inc(wo_gated, 1)

            def kv_head(n, last):
                for b in range(B):
                    half, slot, nb = 2 * n + b, 8 * n + 4 * b, 1 - b
                    more = not (last and b == 1)
                    if not (isinstance(n, int) and n == 0 and b == 0):
                        gate_attention(slot - 1, nb)
                    if b == 0:
                        split_wo(n)
                    weights_low(slot, 0)
                    mask(slot + 1, 1)
                    if more:
                        evacuate(half + 1, "Q0", nb)
                    normalise(slot + 1, 1)
                    out_low(slot)
                    if b == 0 and not last:
                        split_weights(n + 1, (0, 1))
                    if more:
                        evacuate(half + 1, "Q1", nb)
                    weights_low(slot + 1, 1)
                    mask(slot + 2, 2)
                    if more:
                        evacuate(half + 1, "Vt", nb)
                    gate_attention(slot, b)
                    normalise(slot + 2, 2)
                    out_low(slot + 1)
                    if more:
                        evacuate(half + 1, "Q2", nb)
                    weights_low(slot + 2, 2)
                    mask(slot + 3, 3)
                    if more:
                        evacuate(half + 1, "Q3", nb)
                    normalise(slot + 3, 3)
                    gate_attention(slot + 1, b)
                    out_low(slot + 2)
                    if last and b == 1:
                        norm_stats(1, 0)
                    weights_low(slot + 3, 3)
                    if not last:
                        evacuate(half + 2, "K", b)
                        if b == 0:
                            split_weights(n + 1, (2, 3, 4, 5))
                    gate_attention(slot + 2, b)
                    if more:
                        mask(slot + 4, 0)
                    out_low(slot + 3)
                    if more:
                        if not last:
                            evacuate(half + 2, "V", b)
                        normalise(slot + 4, 0)
                if last:
                    gate_attention(8 * n + 7, 1)

            norm_stats(0, 0)
            norm_stats(0, 1)
            norm_rows(0, 0)
            norm_rows(0, 1)
            mod_cols(0, 0)
            split_weights(0, (0, 1))
            norm_split(0, 0)
            split_weights(0, (2, 3))
            norm_split(0, 1)
            split_weights(0, (4, 5))
            dve.wait_ge(rope_loaded, 48)
            for name in TURN:
                evacuate(0, name, 0)
            evacuate(1, "K", 1)
            mod_cols(0, 1)
            mask(0, 0)
            evacuate(1, "V", 1)
            normalise(0, 0)
            clamp_gates(0)
            kv_head(0, False)
            with dve.Fori(1, HKV - 1) as n:
                kv_head(n, False)
            kv_head(HKV - 1, True)

            dve.wait_ge(f_loaded, 16 * 9)
            dve.tensor_tensor(fcw[:], fco[:, 0:1], fco[:, 1:2], ALU.mult).then_inc(f_cw, 1)
            norm_stats(1, 1)
            norm_rows(1, 0)
            dve.wait_ge(f_er_mm, 1)
            dve.tensor_copy(fer[:], bank[4][:, 0:2]).then_inc(f_er, 1)
            dve.wait_ge(f_er, 1)
            for t in range(2):
                dve.tensor_scalar(fa_s[:, t], fa[:, t], fer[:, t:t + 1], None, ALU.mult).then_inc(f_as, 1)

            def merged_low(k):
                dve.wait_ge(f_hi, k + 1)
                dve.tensor_tensor(fw_lo[:, k], bank[k][:], fw_hi[:, k].bitcast(F32), ALU.subtract).then_inc(f_split, 1)

            norm_rows(1, 1)
            mod_cols(1, 0)
            merged_low(0)
            merged_low(1)
            mod_cols(1, 1)
            norm_split(1, 0)
            merged_low(2)
            merged_low(3)
            norm_split(1, 1)
            dve.wait_ge(fbias_loaded, 16)
            for t in range(NT):
                dve.wait_ge(f_mm, t + 1)
                dve.tensor_tensor(fu[:, t % 2], bank[4 + t % 4][:], fbias[:], ALU.add).then_inc(f_bias, 1)
                if t == 0:
                    dve.wait_ge(gate_ready, 2)
                dve.wait_ge(f_bias, t + 1)
                wait(dve, f_added, t - 1)
                dve.tensor_tensor(fg[:, t % 2], fu[:, t % 2], gate[:, 0, t // TB], ALU.mult).then_inc(f_gated, 1)
                if t == 1:
                    clamp_gates(1)
                if t == 4:
                    norm_stats(2, 0)
                if t == 6:
                    norm_rows(2, 0)

            norm_stats(2, 1)
            norm_rows(2, 1)
            norm_split(2, 0)
            norm_split(2, 1)
            def split_rope_weights(p, par, use):
                if exists(p, PAIRS):
                    dve.wait_ge(wr_loaded[par], 16 * use + 16)
                    wait(dve, qr_mm, 2 * p - 2)
                    dve.tensor_copy(wr_hi[:, par], wst[:, par]).then_inc(wr_hi_done, 1)

            split_rope_weights(0, 0, 0)
            dve.wait_ge(zeroed, 7)
            for b in range(B):
                dve.wait_ge(kr_hi_done, b + 1)
                dve.tensor_tensor(k2[0:ROPE, b, 0], bank[6 + b][0:ROPE], k1[0:ROPE, b].bitcast(F32), ALU.subtract)
                dve.tensor_tensor(k2[ROPE:P, b, 1], bank[6 + b][ROPE:P], k1[ROPE:P, b].bitcast(F32), ALU.subtract).then_inc(kr_split, 1)

            def content_low(m):
                for i in range(4):
                    dve.wait_ge(c_hi_done, 4 * m + i + 1)
                    dve.tensor_tensor(c_lo[:, i], bank[i][:], c_hi[:, i].bitcast(F32), ALU.subtract).then_inc(c_split, 1)

            content_low(0)
            dve.wait_ge(vc_ready, NT)

            def q_low(z, k):
                if exists(z, UNITS):
                    dve.wait_ge(q2_hi, z + 1)
                    dve.tensor_tensor(q1[ROPE:P, k % 4, 0], bank[6][0:ROPE], q2[0:ROPE, k % 4, 0].bitcast(F32), ALU.subtract)
                    dve.tensor_tensor(q1[0:ROPE, k % 4, 1], bank[6][ROPE:P], q2[ROPE:P, k % 4, 1].bitcast(F32), ALU.subtract)\
                       .then_inc(q1_split, 1)

            def sums_reciprocal(n, part):
                if exists(n, EARLY):
                    d = SUMS[n % 2][1]
                    dve.wait_ge(o_added, 2 * n + 1)
                    e = dve.reciprocal(d[:, 1, part], d[:, 0, part])
                    if part.stop == S:
                        e.then_inc(o_rden, 1)

            def maxima(w, k, use, n=-1):
                if exists(w, UNITS):
                    wait(dve, m_loaded[k % 2], 32 * use)
                    for i in range(8):
                        dve.wait_ge(max_mm, 8 * w + i + 1)
                        dve.tensor_reduce(mcol[:, k % 2, i % 4, i // 4:i // 4 + 1], bank[4 + i % 2][:], AX.X, ALU.max, negate=True)\
                           .then_inc(max_done, 1)
                        if i in (1, 3):
                            sums_reciprocal(n - 1, slice((i + 3) * S // 8, (i + 5) * S // 8))
                        if i in (6, 7):
                            sums_reciprocal(n, slice((i - 6) * S // 4, (i - 5) * S // 4))
                    dve.wait_ge(max_done, 8 * w + 8)
                    dve.transpose(mrow[:, k % 2].rearrange("p (r i) -> p i r", i=4), mcol[:, k % 2].bitcast(F32)).then_inc(m_turned, 1)

            def values(v, k, pair):
                if exists(v, UNITS):
                    wait(dve, pv1, 2 * v - 1)
                    dve.tensor_copy(vp[:, k % 2, :, :, 0:HD1],
                                    vc[:, TB * (k % 2):TB * (k % 2) + TB, bass.ds(pair * 8, 8)]
                                    .rearrange("p t (h d) -> p t h d", h=2)).then_inc(vp_ready, 1)

            def period(u, k, pair, quad, n=-1):
                q_low(u + 2, k + 2)
                if isinstance(u, int) and 0 < u + 3 < KT:
                    content_low(u + 3)
                if k % 2 == 0:
                    split_rope_weights(pair(4), (k // 2) % 2, quad(4))
                values(u + 1, k + 1, pair(1))
                maxima(u + 2, k + 2, pair(2), n)

            for u in range(-3, 6):
                period(u, u % 4, lambda n, u=u: (u + n) // 2, lambda n, u=u: (u + n) // 4)
            with dve.Fori(1, TAIL // 4) as g:
                for k in range(2, 6):
                    period(4 * g + k, k, lambda n, k=k: 2 * g + (k + n) // 2, lambda n, k=k: g + (k + n) // 4)

            for u in range(TAIL, UNITS):
                period(u, u % 4, lambda n, u=u: (u + n) // 2, lambda n, u=u: (u + n) // 4, u - TAIL)

            def last_sums(b):
                o, d = SUMS[b]
                dve.wait_ge(sums_loaded[b], 64 * KT)
                dve.tensor_tensor(d[:, 0], d[:, 0], d[:, 1], ALU.add).then_inc(o_last_den, 1)
                dve.wait_ge(o_last_den, b + 1)
                dve.reciprocal(d[:, 1], d[:, 0]).then_inc(o_rden, 1)
                dve.wait_ge(o_rden, EARLY + b + 1)
                dve.wait_ge(o_last, b + 1)
                dve.tensor_tensor(o[:, 0], o[:, 0], d[:, 1], ALU.mult).then_inc(o_normed, 1)

            def last_sums_low(b):
                at = slice(b * S, (b + 1) * S)
                dve.wait_ge(oo_hi_done, EARLY + b + 1)
                dve.tensor_tensor(oo3_lo[:, at], SUMS[b][0][:, 0], oo3_hi[:, at].bitcast(F32), ALU.subtract).then_inc(oo_split, 1)

            last_sums(0)
            last_sums_low(0)
            last_sums(1)
            last_sums_low(1)

            dve.wait_ge(gate_ready, 4)
            dve.wait_ge(o_copied, UNITS)
            dve.memset(rwT[:], 0.0).then_inc(g_const, 1)
            dve.wait_ge(g_loaded, 16 * 12)
            dve.tensor_copy(emap[0:NR], emap_i[0:NR]).then_inc(g_const, 1)
            dve.wait_ge(g_const, 2)
            dve.tensor_scalar(ehot[0:NR], ecol[0:NR], emap[0:NR, 0:1], None, ALU.is_equal).then_inc(g_const, 1)

            def gate_attention1(t):
                dve.wait_ge(wo1_mm, t + 1)
                wait(dve, attn1_added, t - 1)
                dve.tensor_tensor(og[:, t % 2], bank[t][:], gate[:, 1, t // TB], ALU.mult).then_inc(wo1_gated, 1)

            low = [*((bwT_hi[:, k], bwT_lo[:, k]) for k in range(KT)),
                   (laT_hi[:].rearrange("p k n -> p (k n)"), laT_lo[:].rearrange("p k n -> p (k n)")), (lbT_hi[:], lbT_lo[:])]

            def weights_low1(i):
                hi, lo = low[i]
                dve.wait_ge(g_hi, i + 1)
                dve.tensor_tensor(lo, g_bank(i), hi.bitcast(F32), ALU.subtract).then_inc(g_lo, 1)

            for t in range(TB + 1):
                gate_attention1(t)
            norm_stats(3, 0)
            gate_attention1(TB + 1)
            weights_low1(0)
            weights_low1(1)
            gate_attention1(TB + 2)
            weights_low1(2)
            weights_low1(3)
            norm_stats(3, 1, (0, 1))
            gate_attention1(TB + 3)
            norm_rows(3, 0)
            norm_stats(3, 1, (2, 3))
            weights_low1(KT)
            weights_low1(KT + 1)
            norm_rows(3, 1)
            dve.wait_ge(g_tr, KT + 3)
            dve.tensor_copy(rwT[:, :, 0:NR], g_bank(KT + 2)).then_inc(g_lo, 1)
            norm_split(3, 0)
            norm_split(3, 1)

            step = [0]

            def chain(ins):
                step[0] += 1
                ins.then_inc(r_step, 1)
                dve.wait_ge(r_step, step[0])

            over = lambda v: v.unsqueeze(2).broadcast_to([P, NT, NR])
            dve.wait_ge(r_mm, 1)
            chain(dve.tensor_tensor(lg[:], bank[7][:, 0:NT * 16].rearrange("p (t n) -> p t n", n=16)[:, :, 0:NR],
                                    rbias[:].unsqueeze(1).broadcast_to([P, NT, NR]), ALU.add))
            chain(dve.tensor_reduce(lmax[:], lg[:], AX.X, ALU.max))
            chain(dve.tensor_tensor(lg[:], lg[:], over(lmax[:]), ALU.subtract))
            dve.wait_ge(r_exp, 1)
            chain(dve.tensor_reduce(lsum[:], prob[:], AX.X, ALU.add))
            chain(dve.reciprocal(lrec[:], lsum[:]))
            chain(dve.tensor_tensor(prob[:], prob[:], over(lrec[:]), ALU.mult))
            p_n = prob[:].unsqueeze(3).broadcast_to([P, NT, NR, NR])
            p_m = prob[:].unsqueeze(2).broadcast_to([P, NT, NR, NR])
            dve.tensor_tensor(cmpg[:], p_m, p_n, ALU.is_gt)
            chain(dve.tensor_tensor(cmpe[:], p_m, p_n, ALU.is_equal))
            chain(dve.tensor_tensor(cmpe[:], cmpe[:], before[:].unsqueeze(1).broadcast_to([P, NT, NR, NR]), ALU.mult))
            chain(dve.tensor_tensor(cmpg[:].rearrange("p t n m -> p (t n m)"), cmpg[:].rearrange("p t n m -> p (t n m)"),
                                    cmpe[:].rearrange("p t n m -> p (t n m)"), ALU.add))
            chain(dve.tensor_reduce(rank[:].rearrange("p t n -> p (t n)"), cmpg[:].rearrange("p t n m -> p (t n) m"), AX.X, ALU.add))
            dve.memset(kept[:], 0.0)
            chain(dve.tensor_scalar(rank[:], rank[:], float(E1), None, ALU.is_lt))
            dve.tensor_tensor(kept[:, :, 0:NR], rank[:], prob[:], ALU.mult).then_inc(r_kept, 1)
            for b in range(B):
                dve.wait_ge(r_wexp, b + 1)
                dve.wait_ge(r_hmm, b + 1)
                dve.tensor_tensor(lh[:, b * S:(b + 1) * S], bank[5 + b][:], wexp[:, b * S:(b + 1) * S], ALU.mult).then_inc(r_hfull, 1)
            for b in range(B):
                dve.wait_ge(r_hhi, b + 1)
                dve.tensor_tensor(lh_lo[:, b * S:(b + 1) * S], lh[:, b * S:(b + 1) * S], lh_hi[:, b * S:(b + 1) * S].bitcast(F32),
                                  ALU.subtract).then_inc(r_hlo, 1)
            for t in range(NT):
                dve.wait_ge(g_mm, t + 1)
                dve.tensor_tensor(gu[:, t % 2], bank[t][:], bbias[:], ALU.add).then_inc(g_bias, 1)
                dve.wait_ge(g_bias, t + 1)
                wait(dve, g_added, t - 1)
                dve.tensor_tensor(gg[:, t % 2], gu[:, t % 2], gate[:, 2, t // TB], ALU.mult).then_inc(g_gated, 1)

        @block.tensor
        def _(pe):
            def mm3(ps, pairs, inc=None):
                n = len(pairs)
                for i, (lh_, ll, rh, rl) in enumerate(pairs):
                    pe.matmul(ps, lh_, rh, start=(i == 0), stop=False)
                    pe.matmul(ps, lh_, rl, start=False, stop=False)
                    e = pe.matmul(ps, ll, rh, start=False, stop=(i == n - 1))
                if inc is not None:
                    e.then_inc(inc, 1)

            def mod(l, c):
                i = 6 * l + c
                pe.wait_ge(wm_loaded[i % 3], 16 * (i // 3 + 1))
                wait(pe, mod_row, i - 1)
                for k in range(KT):
                    e = pe.matmul(bank[2 + c % 2][32 * k:32 * k + 32, :], silu[:, l, k], WM[l][:, i % 3, k], start=True, stop=True)
                e.then_inc(mod_mm, 1)

            def mod_use(l, c):
                pe.wait_ge(mod_row, 6 * l + c + 1)
                rows = MODROW[l][:, ROW_SLOT[c]]
                if c in GATE_CHUNKS:
                    w = GATE_CHUNKS.index(c)
                    e = pe.matmul(gate_sums(l)[32 * w:32 * w + 32], rowsum[:], rows, start=True, stop=True)
                else:
                    for k in range(KT):
                        at = 8 * (c % 3) + 2 * k
                        e = pe.matmul(col_bank(l, c // 3)[:, at:at + 2], rows[:, k * P:(k + 1) * P], rowsum[:, 0:B], start=True, stop=True)
                e.then_inc(mod_used, 1)

            def broadcast_gate(l, w):
                pe.wait_ge(gate_rows, l + 1)
                r = slice(32 * w, 32 * w + 32)
                for b in range(B):
                    e = pe.matmul(bank[GATE_BANKS[2 * l + w][b]][:], sel[r, b], GROWS[l][r], start=True, stop=True)
                e.then_inc(gate_bc, 1)

            def norm(ph, b):
                for t in range(TB * b, TB * b + TB):
                    pe.wait_ge(ln_norm, NT * ph + t + 1)
                    for k in range(KT):
                        e = pe.transpose(norm_bank(ph, KT * b + k)[:, (t % TB) * P:(t % TB + 1) * P], NORM[ph][0][:, t, k * P:(k + 1) * P],
                                         ident[:])
                    e.then_inc(ln_trans, 1)

            pe.wait_ge(ident_loaded, 48)
            pe.wait_ge(silu_step, 3)
            mod(0, 0)
            norm(0, 0)
            mod(0, 1)
            mod_use(0, 0)
            mod_use(0, 1)
            pe.wait_ge(col_ready, 1)
            norm(0, 1)

            def project(half, name, b, n):
                e = TURNS * half + TURN[name]
                ps = bank[6 + (b + TURN[name]) % 2]
                wait(pe, proj_free, e - 1)
                if name == "Vt":
                    pe.wait_ge(proj_free, TURNS * half + TURN["V"] + 1)
                    for t in range(TB):
                        ins = pe.transpose(ps[:, t * P:(t + 1) * P], vT[:, t * P:(t + 1) * P], ident[:])
                    ins.then_inc(proj_done, 1)
                    return
                m = W_TILE[name]
                pe.wait_ge(w_split, 6 * n + m + 1)
                at = slice(b * S, (b + 1) * S)
                mm3(ps[:], [(w_hi[:, m, k], w_lo[:, m, k], hT_hi[:, k, at], hT_lo[:, k, at]) for k in range(KT)], proj_done)

            def scores(slot, half, b, qb):
                if qb == 0:
                    pe.wait_ge(rope_split, 5 * half + 5)
                wait(pe, masked0, slot)
                c = slice(P, 2 * P) if qb == 0 else slice(0, 2 * P)
                keys = slice(0, P) if qb == 0 else slice((qb - 1) * P, (qb + 1) * P)
                for h in range(GQ):
                    q = slice(qb * P, (qb + 1) * P)
                    ps = bank[h // 2][:, (h % 2) * 2 * P:(h % 2 + 1) * 2 * P]
                    mm3(ps[:, c], [(qT_hi[b][:, h, q], qT_lo[b][:, h, q], kT_hi[:, b, keys], kT_lo[:, b, keys])],
                        scores0 if h == GQ - 1 else None)

            def transposes(slot, qb):
                pe.wait_ge(probs0, slot + 1)
                wait(pe, pT_split, slot)
                for kb in range(1 if qb == 0 else 0, 2):
                    for h in range(GQ):
                        e = pe.transpose(bank[2 + kb][:, h * P:(h + 1) * P], probs[:, qb % 2, h, kb * P:(kb + 1) * P], ident[:])
                e.then_inc(trans0, 1)

            def sum_values(slot, half, b, qb):
                pe.wait_ge(pT_split, slot + 1)
                if qb == 0:
                    pe.wait_ge(proj_free, TURNS * half + TURN["Vt"] + 1)
                wait(pe, oT_split, slot)
                mm3(bank[4][:], [(v_hi[:, b, qb - 1 + kb], v_lo[:, b, qb - 1 + kb], pT_hi[:, kb], pT_lo[:, kb])
                                 for kb in range(1 if qb == 0 else 0, 2)], pv0)

            def project_out(slot, n):
                pe.wait_ge(oT_split, slot + 1)
                pe.wait_ge(wo_split, n + 1)
                wait(pe, wo_gated, slot)
                mm3(bank[5][:], [(oT_hi[:, h], oT_lo[:, h], wo_hi[:, h], wo_lo[:, h]) for h in range(GQ)], wo_mm)

            def kv_head(n, last):
                for b in range(B):
                    half, slot, nb = 2 * n + b, 8 * n + 4 * b, 1 - b
                    more = not (last and b == 1)
                    transposes(slot, 0)
                    scores(slot + 1, half, b, 1)
                    if more:
                        project(half + 1, "Q0", nb, n + b)
                    if isinstance(n, int) and n == 0 and b == 0:
                        broadcast_gate(0, 0)
                        pe.wait_ge(gate_ready, 1)
                    sum_values(slot, half, b, 0)
                    if more:
                        project(half + 1, "Q1", nb, n + b)
                    transposes(slot + 1, 1)
                    scores(slot + 2, half, b, 2)
                    if more:
                        project(half + 1, "Vt", nb, n + b)
                    project_out(slot, n)
                    sum_values(slot + 1, half, b, 1)
                    if more:
                        project(half + 1, "Q2", nb, n + b)
                    transposes(slot + 2, 2)
                    scores(slot + 3, half, b, 3)
                    if more:
                        project(half + 1, "Q3", nb, n + b)
                    project_out(slot + 1, n)
                    sum_values(slot + 2, half, b, 2)
                    transposes(slot + 3, 3)
                    if not last:
                        project(half + 2, "K", b, n + 1)
                    project_out(slot + 2, n)
                    if more:
                        scores(slot + 4, half + 1, nb, 0)
                    sum_values(slot + 3, half, b, 3)
                    if not last:
                        project(half + 2, "V", b, n + 1)
                    project_out(slot + 3, n)

            wait_norm(pe, 0, 0)
            for name in TURN:
                project(0, name, 0, 0)
            wait_norm(pe, 0, 1)
            project(1, "K", 1, 0)
            mod(0, 2)
            mod(0, 3)
            mod_use(0, 2)
            mod(0, 4)
            mod_use(0, 3)
            mod(0, 5)
            mod_use(0, 4)
            mod_use(0, 5)
            scores(0, 0, 0, 0)
            project(1, "V", 1, 0)
            pe.wait_ge(col_ready, 2)
            kv_head(0, False)
            with pe.Fori(1, HKV - 1) as n:
                kv_head(n, False)
            kv_head(HKV - 1, True)

            pe.wait_ge(f_loaded, 16 * 9)
            pe.wait_ge(proj_free, TURNS * B * HKV)
            for t in range(2):
                for k in range(KT):
                    e = pe.transpose(bank[6 + t][:, k * P:(k + 1) * P], fbf[:, k, t * P:(t + 1) * P], ident[:])
                e.then_inc(f_tr, 1)
            pe.wait_ge(f_cw, 1)
            for t in range(2):
                e = pe.matmul(bank[4][:, t:t + 1], expand[:, t * P:(t + 1) * P], fcw[:], start=True, stop=True)
            e.then_inc(f_er_mm, 1)

            def merge(k):
                for t in range(2):
                    pe.matmul(bank[k][:], fa_s[:, t, k * P:(k + 1) * P], fbfT[:, t], start=(t == 0), stop=False)
                for o in range(KT):
                    e = pe.matmul(bank[k][:, o * P:(o + 1) * P], fw[:, o, k * P:(k + 1) * P], ident[:], start=False, stop=(o == KT - 1))
                e.then_inc(f_mg, 1)

            mod(1, 0)
            mod(1, 1)
            pe.wait_ge(wo_gated, NT * HKV)
            mod_use(1, 0)
            mod(1, 2)
            mod_use(1, 1)
            mod(1, 3)
            pe.wait_ge(f_as, 2)
            pe.wait_ge(f_trs, 2)
            merge(0)
            merge(1)
            mod(1, 4)
            pe.wait_ge(f_er, 1)
            mod_use(1, 3)
            mod(1, 5)
            mod_use(1, 4)
            pe.wait_ge(col_ready, 4)
            norm(1, 0)
            pe.wait_ge(mod_row, 12)
            merge(2)
            merge(3)
            pe.wait_ge(f_split, KT)
            norm(1, 1)

            def ffn(t):
                wait(pe, f_bias, t - 3)
                at = slice(t * P, (t + 1) * P)
                mm3(bank[4 + t % 4][:], [(hT_hi[:, k, at], hT_lo[:, k, at], fw_hi[:, k], fw_lo[:, k]) for k in range(KT)], f_mm)

            wait_norm(pe, 1, 0)
            ffn(0)
            ffn(1)
            wait_norm(pe, 1, 1)
            broadcast_gate(0, 1)
            mod_use(1, 2)
            mod_use(1, 5)
            ffn(2)
            ffn(3)
            broadcast_gate(1, 0)
            ffn(4)
            ffn(5)
            pe.wait_ge(gate_ready, 2)
            broadcast_gate(1, 1)
            ffn(6)
            ffn(7)

            pe.wait_ge(f_bias, NT)
            norm(2, 0)
            pe.wait_ge(gate_ready, 4)
            norm(2, 1)
            pe.wait_ge(pre_split, 2)
            for b in range(B):
                wait_norm(pe, 2, b)
                at = slice(b * S, (b + 1) * S)
                mm3(bank[b][:], [(dn_hi[:, k], dn_lo[:, k], hT_hi[:, k, at], hT_lo[:, k, at]) for k in range(KT)], lat_mm)
            for b in range(B):
                at = slice(b * S, (b + 1) * S)
                mm3(bank[6 + b][:], [(kr_hi[:, k], kr_lo[:, k], hT_hi[:, k, at], hT_lo[:, k, at]) for k in range(KT)], kr_mm)

            def content(m):
                for b in range(B):
                    for w in range(2):
                        i = 2 * b + w
                        rows = slice(LAT * w, LAT * w + LAT)
                        wait(pe, c_split, 4 * (m - 1) + i + 1 if m else 0)
                        pe.matmul(bank[i][:], up[rows, m * P:(m + 1) * P], lat[rows, b * S:(b + 1) * S],
                                  start=True, stop=True).then_inc(c_mm, 1)

            pe.wait_ge(lat_ready, B)
            content(0)
            for t in range(NT):
                wait(pe, vc_ready, t - 1)
                pe.matmul(bank[4 + t % 2][:], lat[LAT:P, t * P:(t + 1) * P], vup[LAT:P], start=True, stop=True).then_inc(vc_mm, 1)
            pe.wait_ge(vc_ready, NT)
            pe.wait_ge(kr_split, B)

            def rope_queries(z, k, pair, ks, first, last):
                if exists(z, UNITS):
                    b = k % 2
                    par = (k % 4) // 2
                    if first:
                        wait(pe, q1_split, z)
                        pe.wait_ge(wr_split, pair + 1)
                    at = slice(b * S, (b + 1) * S)
                    for kk in ks:
                        pe.matmul(bank[6][:], wr_hi[:, par, kk], hT_hi[:, kk, at], start=(kk == 0), stop=False)
                        pe.matmul(bank[6][:], wr_hi[:, par, kk], hT_lo[:, kk, at], start=False, stop=False)
                        e = pe.matmul(bank[6][:], wr_lo[:, par, kk], hT_hi[:, kk, at], start=False, stop=(kk == KT - 1))
                    if last:
                        e.then_inc(qr_mm, 1)

            def max_scores(w, k, i, use):
                if exists(w, UNITS):
                    h, b = i // 4, k % 2
                    if i == 0:
                        pe.wait_ge(q2_hi, w + 1)
                        pe.wait_ge(mc_loaded[b], 64 * use + 64)
                    wait(pe, max_done, 8 * w + i - 1)
                    pe.matmul(bank[4 + i % 2][:], q2[:, k % 4, h, i % 4:S:4], km[:, b, h], start=True, stop=True).then_inc(max_mm, 1)

            def scores1_slot(u, k, s, use):
                if exists(u, UNITS):
                    h, kb = SLOTS[s]
                    if s == 0:
                        pe.wait_ge(q1_hi, u + 1)
                        pe.wait_ge(q1_split, u + 1)
                        pe.wait_ge(m_loaded[k % 2], 32 * use + 32)
                        pe.wait_ge(k2c_loaded[k % 2], 32 * use + 32)
                    pe.wait_ge(exp1, 8 * u + s + 1)
                    t = slice(kb * P, (kb + 1) * P)
                    pe.matmul(bank[s % 4][:], k1[:, k % 2, t], q1[:, k % 4, h], start=True, stop=False)
                    pe.matmul(bank[s % 4][:], k2[:, k % 2, h, t], q2[:, k % 4, h], start=False, stop=True).then_inc(scores1, 1)

            def sum_slots(u, k, c):
                if exists(u, UNITS):
                    pe.wait_ge(exp1, 8 * u + 4 * c + 8)
                    if c == 0:
                        pe.wait_ge(vp_ready, u + 1)
                        wait(pe, o_copied, u)
                    for s in range(4 * c, 4 * c + 4):
                        h, kb = SLOTS[s]
                        j = 2 * h + kb % 2
                        e = pe.matmul(bank[7][32 * j:32 * j + 32, :], vp[:, k % 2, kb, h], pT[:, s], start=(c == 0), stop=(c == 1))
                    e.then_inc(pv1, 1)

            pe.sem_inc(pv1, 1)

            def period(u, k, pair):
                scores1_slot(u, k, 0, pair(0))
                scores1_slot(u, k, 1, pair(0))
                sum_slots(u - 1, k - 1, 1)
                scores1_slot(u, k, 2, pair(0))
                max_scores(u + 2, k + 2, 0, pair(2))
                scores1_slot(u, k, 3, pair(0))
                max_scores(u + 2, k + 2, 1, pair(2))
                scores1_slot(u, k, 4, pair(0))
                rope_queries(u + 3, k + 3, pair(3), [0], True, False)
                max_scores(u + 2, k + 2, 2, pair(2))
                scores1_slot(u, k, 5, pair(0))
                rope_queries(u + 3, k + 3, pair(3), [1], False, False)
                max_scores(u + 2, k + 2, 3, pair(2))
                sum_slots(u, k, 0)
                max_scores(u + 2, k + 2, 4, pair(2))
                scores1_slot(u, k, 6, pair(0))
                rope_queries(u + 3, k + 3, pair(3), [2], False, False)
                max_scores(u + 2, k + 2, 5, pair(2))
                scores1_slot(u, k, 7, pair(0))
                max_scores(u + 2, k + 2, 6, pair(2))
                rope_queries(u + 3, k + 3, pair(3), [3], False, True)
                max_scores(u + 2, k + 2, 7, pair(2))

            for u in range(-3, 6):
                period(u, u % 4, lambda n, u=u: (u + n) // 2)
                if u < 0:
                    content(u + 4)
                if u == -1:
                    pe.wait_ge(c_split, 4 * KT)
                    pe.wait_ge(ones_set, 64)
            with pe.Fori(1, TAIL // 4) as g:
                for k in range(2, 6):
                    period(4 * g + k, k, lambda n, k=k: 2 * g + (k + n) // 2)
            for u in range(TAIL, UNITS + 1):
                period(u, u % 4, lambda n, u=u: (u + n) // 2)

            pe.wait_ge(o_copied, UNITS)
            pe.wait_ge(wo1_split, KT)
            pe.wait_ge(oo_split, 6)

            def first_heads(t):
                at = slice(t * P, (t + 1) * P)
                for k in range(KT - 1):
                    pe.matmul(bank[t][:], oo_hi[:, k, at], wo1_hi[:, k], start=(k == 0), stop=False)
                    pe.matmul(bank[t][:], oo_hi[:, k, at], wo1_lo[:, k], start=False, stop=False)
                    pe.matmul(bank[t][:], oo_lo[:, k, at], wo1_hi[:, k], start=False, stop=False)

            def last_heads(t):
                at = slice(t * P, (t + 1) * P)
                pe.wait_ge(oo_split, 7 + t // TB)
                pe.matmul(bank[t][:], oo3_hi[:, at], wo1_hi[:, KT - 1], start=False, stop=False)
                pe.matmul(bank[t][:], oo3_hi[:, at], wo1_lo[:, KT - 1], start=False, stop=False)
                pe.matmul(bank[t][:], oo3_lo[:, at], wo1_hi[:, KT - 1], start=False, stop=True).then_inc(wo1_mm, 1)

            def turn_base(i):
                pe.wait_ge(wo1_gated, i + 1)
                for o in range(KT):
                    e = pe.transpose(bank[i][:, o * P:(o + 1) * P], bw[:, o, i * P:(i + 1) * P], ident[:])
                e.then_inc(g_tr, 1)

            for t in range(TB + 2):
                first_heads(t)
            for t in range(TB + 2):
                last_heads(t)
            pe.wait_ge(g_loaded, 16 * 12)
            turn_base(0)
            turn_base(1)
            first_heads(TB + 2)
            last_heads(TB + 2)
            turn_base(2)
            turn_base(3)
            first_heads(TB + 3)
            last_heads(TB + 3)
            for i in range(KT, KT + 3):
                pe.wait_ge(g_lo, i - 3)
                for k in range(KT):
                    if i == KT:
                        e = pe.transpose(g_bank(i)[:, k * P:(k + 1) * P], la[:, k * P:(k + 1) * P], ident[:])
                    elif i == KT + 1:
                        e = pe.transpose(g_bank(i)[:, k * P:(k + 1) * P], lb[:, k].rearrange("p e r -> p (e r)"), ident[:])
                    else:
                        e = pe.transpose(g_bank(i)[:, k], rw[0:NR, k * P:(k + 1) * P], ident[0:NR, 0:NR])
                e.then_inc(g_tr, 1)
            pe.wait_ge(wo1_gated, NT)
            norm(3, 0)
            pe.wait_ge(g_lo, KT + 3)
            norm(3, 1)

            for b in range(B):
                wait_norm(pe, 3, b)
                at = slice(b * S, (b + 1) * S)
                for i, h in enumerate((hT_hi, hT_lo)):
                    for k in range(KT):
                        e = pe.matmul(bank[(7, 4)[b]][32 * k:32 * k + 32, :], rwT[:, k], h[:, k, at].bitcast(F32), start=(i == 0), stop=(i == 1))
                e.then_inc(r_part, 1)
            for b in range(B):
                pe.wait_ge(r_copied, b + 1)
                for t in range(TB * b, TB * b + TB):
                    e = pe.matmul(bank[7][:, 16 * t:16 * t + 16], lpart[:, t * P:(t + 1) * P], rowsum[:, 0:16], start=True, stop=True)
            e.then_inc(r_mm, 1)

            for b in range(B):
                at = slice(b * S, (b + 1) * S)
                mm3(bank[5 + b][:], [(laT_hi[:, k], laT_lo[:, k], hT_hi[:, k, at], hT_lo[:, k, at]) for k in range(KT)], r_hmm)

            def base(t):
                at = slice(t * P, (t + 1) * P)
                for k in range(KT):
                    pe.matmul(bank[t][:], hT_hi[:, k, at], bwT_hi[:, k], start=(k == 0), stop=False)
                    pe.matmul(bank[t][:], hT_hi[:, k, at], bwT_lo[:, k], start=False, stop=False)
                    pe.matmul(bank[t][:], hT_lo[:, k, at], bwT_hi[:, k], start=False, stop=False)

            def lora(t):
                at = slice(t * P, (t + 1) * P)
                pe.matmul(bank[t][:], lh_hi[:, at], lbT_hi[:], start=False, stop=False)
                pe.matmul(bank[t][:], lh_hi[:, at], lbT_lo[:], start=False, stop=False)
                pe.matmul(bank[t][:], lh_lo[:, at], lbT_hi[:], start=False, stop=True).then_inc(g_mm, 1)

            for t in range(TB - 1):
                base(t)
            pe.wait_ge(r_kept, 1)
            for b in range(B):
                for t in range(TB):
                    e = pe.transpose(bank[(4, 7)[b]][0:16, t * P:(t + 1) * P], kept[:, TB * b + t], ident[:])
                e.then_inc(r_ktr, 1)
            pe.wait_ge(g_const, 3)
            for b in range(B):
                pe.wait_ge(r_ktc, b + 1)
                pe.matmul(bank[(4, 7)[b]][:], ehot[0:NR], keptT[0:NR, b * S:(b + 1) * S], start=True, stop=True).then_inc(r_wmm, 1)
            base(TB - 1)
            pe.wait_ge(r_hlo, B)
            for t in range(TB):
                lora(t)
            for t in range(TB, NT):
                base(t)
                lora(t)


def shape_constants():
    import numpy as np

    half = HD // 2
    inv_freq = np.float32(10000.0) ** (-np.arange(half, dtype=np.float32) / np.float32(half))
    ang = (np.arange(S, dtype=np.float32)[:, None] * inv_freq[None, :]).T.astype(np.float32)
    cos, sin = np.cos(ang), np.sin(ang)
    i, j = np.arange(P)[:, None], np.arange(P)[None, :]
    n = np.arange(NR)
    return {
        "identity": np.eye(P, dtype=np.float32),
        "rope_cos": np.concatenate([cos, cos]).astype(np.float32),
        "rope_sin": np.concatenate([sin, -sin]).astype(np.float32),
        "window_mask": np.where(np.concatenate([j > i, j <= i], axis=1), 0.0, MASKED).astype(np.float32),
        "lora_expand": (np.arange(16)[:, None] == np.arange(ER0)[None, :] // 16).astype(np.float32),
        "batch_rows": np.broadcast_to((np.arange(P)[:, None] % 32 == np.arange(B)[None, :])[:, :, None], (P, B, P)).reshape(P, B * P)
        .astype(np.float32),
        "four_identities": (np.arange(P)[:, None] % 32 == np.arange(32)[None, :]).astype(np.float32),
        "expert_of_column": np.broadcast_to(np.arange(P) // R1, (16, P)).astype(np.float32),
        "entry_before": (n[None, :] < n[:, None]).astype(np.float32),
    }


_INS = ["L0_attn_x", "L0_attn_wq", "L0_attn_wk", "L0_attn_wv", "L0_attn_wo", "L0_ffn_W", "L0_ffn_bias", "L0_ffn_A", "L0_ffn_Bf",
        "L0_ffn_coeffs", "L0_ffn_scales", "L0_c", "L0_wmod", "L1_attn_Wq_down", "L1_attn_Wq_up", "L1_attn_Wq_rope",
        "L1_attn_Wkv_down", "L1_attn_Wk_up", "L1_attn_Wv_up", "L1_attn_Wk_rope", "L1_attn_Wo", "L1_ffn_base_W", "L1_ffn_base_b",
        "L1_ffn_router_W", "L1_ffn_router_b", "L1_ffn_A", "L1_ffn_B", "L1_ffn_expert_map", "L1_c", "L1_wmod"]


def kernel(**inputs):
    import numpy as np
    import concourse.bacc as bacc
    from concourse.bass_utils import run_bass_kernel_spmd

    nc = bacc.Bacc("TRN2", target_bir_lowering=False, num_devices=1)
    arrays = {name: np.ascontiguousarray(inputs[name]) for name in _INS}
    arrays.update(shape_constants())
    aps = {name: nc.dram_tensor(f"in_{name}", v.shape, mybir.dt.from_np(v.dtype), kind="ExternalInput").ap() for name, v in arrays.items()}
    out = nc.dram_tensor("out_x", (B, S, D), F32, kind="ExternalOutput").ap()
    adaln_two_layers(nc, aps, out)
    r = run_bass_kernel_spmd(nc, [{f"in_{name}": v for name, v in arrays.items()}], core_ids=[0])
    return r.results[0]["out_x"]
```
